# Optimizing a Trainium2 kernel written in Bass

```python
import numpy as np
import jax
import jax.numpy as jnp

def _softmax(x, axis=-1):
    return jax.nn.softmax(x, axis=axis)

def _gelu(x):
    return jax.nn.gelu(x, approximate=True)

def _silu(x):
    return jax.nn.silu(x)

def _sigmoid(x):
    return jax.nn.sigmoid(x)

def _layernorm(x, axis=-1, eps=1e-05):
    m = jnp.mean(x, axis=axis, keepdims=True)
    v = jnp.var(x, axis=axis, keepdims=True)
    return (x - m) / jnp.sqrt(v + eps)

def _scatter_add(tgt, idx, src, axis=0):
    return tgt.at[idx].add(src)

def _segment_sum(src, seg, n):
    return jax.ops.segment_sum(src, seg, n)
kernel_name = 'mk_pixart_seq_d4_seqx_r8_343de7'

def setup_inputs(seed: int=0):
    np.random.seed(seed)
    _w = jnp.asarray

    def _rec_inputs():
        import jax
        import jax.numpy as jnp
        _rk = jax.random.key(seed)
        x = -0.0002928 + 1 * jax.random.normal(jax.random.fold_in(_rk, 1), (4, 512, 128), jnp.float32)
        _lenS = 512 - jax.random.randint(jax.random.fold_in(_rk, 7), (4,), 0, max(1, 512 // 4) + 1, jnp.int32)
        _lenS2 = 77 - jax.random.randint(jax.random.fold_in(_rk, 8), (4,), 0, max(1, 77 // 4) + 1, jnp.int32)
        cond_1024 = 0.0061147 + 1.02565 * jax.random.normal(jax.random.fold_in(_rk, 11), (4, 128), jnp.float32)
        _ctx_1024P = jax.random.normal(jax.random.fold_in(_rk, 12), (4, 16, 128), jnp.float32)
        _ctx_1024c = jax.random.dirichlet(jax.random.fold_in(_rk, 512), 0.3 * jnp.ones((16,), jnp.float32), (4, 77))
        _ctx_1024t = jnp.einsum('bsk,bkd->bsd', _ctx_1024c, _ctx_1024P)
        _ctx_1024t = _ctx_1024t * jax.lax.rsqrt(jnp.mean(jnp.square(_ctx_1024t)) + 1e-12) * 0.953939
        ctx_1024 = -0.00265004 + 0.998804 * (_ctx_1024t + 0.3 * jax.random.normal(jax.random.fold_in(_rk, 612), (4, 77, 128), jnp.float32))
        _validS = jnp.arange(512)[None, :] < _lenS[:, None]
        _validS2 = jnp.arange(77)[None, :] < _lenS2[:, None]
        _causal = jnp.tril(jnp.ones((512, 512), dtype=bool))
        mask_BxS2_ik0 = jnp.where(jnp.broadcast_to(_validS2[:, :], (4, 77)), 0, 1).astype(jnp.int32)
        mask_BxS2_bf1 = jnp.ones((4, 77), dtype=bool)
        mask_SxS_bk0 = jnp.logical_not(jnp.broadcast_to(_validS[0:1, :], (512, 512)))
        return (x, cond_1024, ctx_1024, mask_BxS2_ik0, mask_BxS2_bf1, mask_SxS_bk0)
    x, cond_1024, ctx_1024, mask_BxS2_ik0, mask_BxS2_bf1, mask_SxS_bk0 = _rec_inputs()

    def _L0_xcond_setup():
        import jax, jax.numpy as jnp
        import numpy as np
        LN_EPS = 1e-06

        def _ln(x):
            mu = jnp.mean(x, axis=-1, keepdims=True)
            var = jnp.var(x, axis=-1, keepdims=True)
            return (x - mu) * jax.lax.rsqrt(var + LN_EPS)
        key = jax.random.key(seed)
        H, NH = (128, 16)
        B, N, S = (4, 128, 77)
        MLP = int(H * 4.0)
        ks = jax.random.split(key, 20)
        s = 1.0 / np.sqrt(H)
        return {'x': jax.random.normal(ks[0], (B, N, H), jnp.float32), 'c': jax.random.normal(ks[1], (B, H), jnp.float32), 'context': jax.random.normal(ks[2], (B, S, H), jnp.float32), 'W_mod': jax.random.normal(ks[3], (H, 6 * H), jnp.float32) * s, 'b_mod': jnp.zeros((6 * H,), jnp.float32), 'W_qkv': jax.random.normal(ks[4], (H, 3 * H), jnp.float32) * s, 'b_qkv': jnp.zeros((3 * H,), jnp.float32), 'W_proj': jax.random.normal(ks[5], (H, H), jnp.float32) * s, 'b_proj': jnp.zeros((H,), jnp.float32), 'W_qc': jax.random.normal(ks[6], (H, H), jnp.float32) * s, 'b_qc': jnp.zeros((H,), jnp.float32), 'W_kvc': jax.random.normal(ks[7], (H, 2 * H), jnp.float32) * s, 'b_kvc': jnp.zeros((2 * H,), jnp.float32), 'W_cproj': jax.random.normal(ks[8], (H, H), jnp.float32) * s, 'b_cproj': jnp.zeros((H,), jnp.float32), 'W_mlp1': jax.random.normal(ks[9], (H, MLP), jnp.float32) * s, 'b_mlp1': jnp.zeros((MLP,), jnp.float32), 'W_mlp2': jax.random.normal(ks[10], (MLP, H), jnp.float32) * (1.0 / np.sqrt(MLP)), 'b_mlp2': jnp.zeros((H,), jnp.float32)}
    _L0_xcond_all = _L0_xcond_setup()
    _L0_xcond_in = {k: v for k, v in _L0_xcond_all.items() if k in ('W_mod', 'b_mod', 'W_qkv', 'b_qkv', 'W_proj', 'b_proj', 'W_qc', 'b_qc', 'W_kvc', 'b_kvc', 'W_cproj', 'b_cproj', 'W_mlp1', 'b_mlp1', 'W_mlp2', 'b_mlp2')}
    del _L0_xcond_all

    def _L1_xcond_setup():
        import jax, jax.numpy as jnp
        import numpy as np
        C = 128
        H = 16
        D = C // H
        WIN = 64
        SHIFT = 32
        TOPK = 16
        HID = 512
        EPS = 1e-06

        def _ln(x):
            x32 = x.astype(jnp.float32)
            m = x32.mean(-1, keepdims=True)
            v = jnp.mean((x32 - m) ** 2, axis=-1, keepdims=True)
            return ((x32 - m) * jax.lax.rsqrt(v + EPS)).astype(x.dtype)

        def _self_attn(h, w_qkv, b_qkv, w_so, b_so):
            B, L, _ = h.shape
            qkv = h @ w_qkv + b_qkv
            qkv = jnp.roll(qkv, -SHIFT, axis=1)
            nw = L // WIN
            qkv = qkv.reshape(B, nw, WIN, 3, H, D)
            q, k, v = (qkv[:, :, :, 0], qkv[:, :, :, 1], qkv[:, :, :, 2])
            scores = jnp.einsum('bnqhd,bnkhd->bnhqk', q, k) / jnp.sqrt(jnp.float32(D)).astype(h.dtype)
            attn = jax.nn.softmax(scores, axis=-1)
            o = jnp.einsum('bnhqk,bnkhd->bnqhd', attn, v).reshape(B, L, C)
            o = jnp.roll(o, SHIFT, axis=1)
            return o @ w_so + b_so

        def _topk_cross_attn(h, ctx, w_q, b_q, w_kv, b_kv, w_co, b_co):
            B, L, _ = h.shape
            Lc = ctx.shape[1]
            q = (h @ w_q + b_q).reshape(B, L, H, D)
            kv = (ctx @ w_kv + b_kv).reshape(B, Lc, 2, H, D)
            k, v = (kv[:, :, 0], kv[:, :, 1])
            scores = jnp.einsum('bqhd,bkhd->bhqk', q, k) / jnp.sqrt(jnp.float32(D)).astype(h.dtype)
            top_s, top_i = jax.lax.top_k(scores, TOPK)
            attn = jax.nn.softmax(top_s, axis=-1)
            v_bh = jnp.transpose(v, (0, 2, 1, 3))
            vg = jnp.take_along_axis(v_bh[:, :, None, :, :], top_i[..., None], axis=3)
            o = jnp.einsum('bhqk,bhqkd->bqhd', attn, vg).reshape(B, L, C)
            return o @ w_co + b_co

        def _swiglu(h, w_m1, b_m1, w_m2, b_m2):
            u = h @ w_m1 + b_m1
            a, b = (u[..., :HID], u[..., HID:])
            return jax.nn.silu(a) * b @ w_m2 + b_m2
        key = jax.random.key(seed)
        ks = jax.random.split(key, 24)
        s = 0.02
        inp = {'x': jax.random.normal(ks[0], (2, 512, C), jnp.float32), 'mod': jax.random.normal(ks[1], (2, C), jnp.float32), 'context': jax.random.normal(ks[2], (2, 128, C), jnp.float32), 'w_ada': jax.random.normal(ks[3], (C, 9 * C), jnp.float32) * s, 'b_ada': jnp.zeros((9 * C,), jnp.float32), 'w_qkv': jax.random.normal(ks[4], (C, 3 * C), jnp.float32) * s, 'b_qkv': jnp.zeros((3 * C,), jnp.float32), 'w_so': jax.random.normal(ks[5], (C, C), jnp.float32) * s, 'b_so': jnp.zeros((C,), jnp.float32), 'w_q': jax.random.normal(ks[6], (C, C), jnp.float32) * s, 'b_q': jnp.zeros((C,), jnp.float32), 'w_kv': jax.random.normal(ks[7], (C, 2 * C), jnp.float32) * s, 'b_kv': jnp.zeros((2 * C,), jnp.float32), 'w_co': jax.random.normal(ks[8], (C, C), jnp.float32) * s, 'b_co': jnp.zeros((C,), jnp.float32), 'w_m1': jax.random.normal(ks[9], (C, 2 * HID), jnp.float32) * s, 'b_m1': jnp.zeros((2 * HID,), jnp.float32), 'w_m2': jax.random.normal(ks[10], (HID, C), jnp.float32) * s, 'b_m2': jnp.zeros((C,), jnp.float32)}
        return inp
    _L1_xcond_all = _L1_xcond_setup()
    _L1_xcond_in = {k: v for k, v in _L1_xcond_all.items() if k in ('w_ada', 'b_ada', 'w_qkv', 'b_qkv', 'w_so', 'b_so', 'w_q', 'b_q', 'w_kv', 'b_kv', 'w_co', 'b_co', 'w_m1', 'b_m1', 'w_m2', 'b_m2')}
    del _L1_xcond_all

    def _L2_xcond_setup():
        import jax, jax.numpy as jnp
        import numpy as np
        D = 128
        H = 16
        HD = D // H
        FF = 4 * D
        B, NQ, NK = (8, 128, 64)
        EPS = 1e-05

        def layernorm(x, g, b):
            m = jnp.mean(x, axis=-1, keepdims=True)
            v = jnp.mean(jnp.square(x - m), axis=-1, keepdims=True)
            return (x - m) * jax.lax.rsqrt(v + EPS) * g + b

        def mha(x, ctx, wq, bq, wk, bk, wv, bv, wo, bo, mask=None):
            Bq, Nq, _ = x.shape
            Nk = ctx.shape[1]
            q = (x @ wq + bq).reshape(Bq, Nq, H, HD)
            k = (ctx @ wk + bk).reshape(Bq, Nk, H, HD)
            v = (ctx @ wv + bv).reshape(Bq, Nk, H, HD)
            scores = jnp.einsum('bqhd,bkhd->bhqk', q, k) / np.sqrt(HD)
            if mask is not None:
                scores = jnp.where(mask[:, None, None, :].astype(bool), scores, -jnp.inf)
            attn = jax.nn.softmax(scores.astype(jnp.float32), axis=-1).astype(scores.dtype)
            out = jnp.einsum('bhqk,bkhd->bqhd', attn, v).reshape(Bq, Nq, D)
            return out @ wo + bo
        key = jax.random.key(seed)
        ks = jax.random.split(key, 40)
        rn = lambda k, shape, s=0.02: jax.random.normal(k, shape, jnp.float32) * s
        inp = {'x': jax.random.normal(ks[0], (B, NQ, D), jnp.float32), 't_emb': jax.random.normal(ks[1], (B, D), jnp.float32), 'context_emb': jax.random.normal(ks[2], (B, NK, D), jnp.float32), 'mask': jax.random.randint(ks[3], (B, NK), 0, 2, jnp.int32), 'ln1_g': jnp.ones((D,), jnp.float32), 'ln1_b': jnp.zeros((D,), jnp.float32), 'ln3_g': jnp.ones((D,), jnp.float32), 'ln3_b': jnp.zeros((D,), jnp.float32), 'ln2_g': jnp.ones((D,), jnp.float32), 'ln2_b': jnp.zeros((D,), jnp.float32), 'sa_wq': rn(ks[4], (D, D)), 'sa_bq': jnp.zeros((D,), jnp.float32), 'sa_wk': rn(ks[5], (D, D)), 'sa_bk': jnp.zeros((D,), jnp.float32), 'sa_wv': rn(ks[6], (D, D)), 'sa_bv': jnp.zeros((D,), jnp.float32), 'sa_wo': rn(ks[7], (D, D)), 'sa_bo': jnp.zeros((D,), jnp.float32), 'ca_wq': rn(ks[8], (D, D)), 'ca_bq': jnp.zeros((D,), jnp.float32), 'ca_wk': rn(ks[9], (D, D)), 'ca_bk': jnp.zeros((D,), jnp.float32), 'ca_wv': rn(ks[10], (D, D)), 'ca_bv': jnp.zeros((D,), jnp.float32), 'ca_wo': rn(ks[11], (D, D)), 'ca_bo': jnp.zeros((D,), jnp.float32), 'tp_w': rn(ks[12], (D, 3 * D)), 'tp_b': jnp.zeros((3 * D,), jnp.float32), 'w1': rn(ks[13], (D, FF)), 'b1': jnp.zeros((FF,), jnp.float32), 'w2': rn(ks[14], (FF, D)), 'b2': jnp.zeros((D,), jnp.float32)}
        return inp
    _L2_xcond_all = _L2_xcond_setup()
    _L2_xcond_in = {k: v for k, v in _L2_xcond_all.items() if k in ('ln1_g', 'ln1_b', 'ln3_g', 'ln3_b', 'ln2_g', 'ln2_b', 'sa_wq', 'sa_bq', 'sa_wk', 'sa_bk', 'sa_wv', 'sa_bv', 'sa_wo', 'sa_bo', 'ca_wq', 'ca_bq', 'ca_wk', 'ca_bk', 'ca_wv', 'ca_bv', 'ca_wo', 'ca_bo', 'tp_w', 'tp_b', 'w1', 'b1', 'w2', 'b2')}
    del _L2_xcond_all

    def _L3_xcond_setup():
        import jax, jax.numpy as jnp
        import numpy as np
        B, N, D, H, LC = (2, 128, 128, 16, 77)
        HD = D // H
        BLOCK = 16
        ROPE_BASE = 10000.0
        EPS = 1e-05

        def _block_diff_mask(n, block_size):
            idx = np.arange(2 * n)
            q = idx[:, None]
            kv = idx[None, :]
            fq = q >= n
            fkv = kv >= n
            bq = np.where(fq, (q - n) // block_size, q // block_size)
            bkv = np.where(fkv, (kv - n) // block_size, kv // block_size)
            block_diagonal = (bq == bkv) & (fq == fkv)
            offset_block_causal = (bq > bkv) & fkv & ~fq
            block_causal = (bq >= bkv) & fq & fkv
            return jnp.asarray(block_diagonal | offset_block_causal | block_causal)

        def _rope_tables(n):
            inv_freq = 1.0 / ROPE_BASE ** (np.arange(0, HD, 2, dtype=np.float32) / HD)
            freqs = np.outer(np.arange(n, dtype=np.float32), inv_freq)
            emb = np.concatenate([freqs, freqs], axis=-1)
            cos = jnp.asarray(np.cos(emb), jnp.float32)[None, :, None, :]
            sin = jnp.asarray(np.sin(emb), jnp.float32)[None, :, None, :]
            return (cos, sin)

        def _ln(x, w):
            xf = x.astype(jnp.float32)
            mu = jnp.mean(xf, axis=-1, keepdims=True)
            var = jnp.mean(jnp.square(xf - mu), axis=-1, keepdims=True)
            y = (xf - mu) * jax.lax.rsqrt(var + EPS)
            return y * w[None, None, :]

        def _apply_rope(t, cos, sin):
            t1, t2 = jnp.split(t, 2, axis=-1)
            rot = jnp.concatenate([-t2, t1], axis=-1)
            return t * cos + rot * sin

        def _attn(q, k, v, mask):
            scale = 1.0 / np.sqrt(HD)
            s = jnp.einsum('bqhd,bkhd->bhqk', q, k) * scale
            s = jnp.where(mask, s, jnp.finfo(s.dtype).min)
            a = jax.nn.softmax(s, axis=-1)
            return jnp.einsum('bhqk,bkhd->bqhd', a, v)
        key = jax.random.key(seed)
        ks = jax.random.split(key, 16)
        w = lambda k, shp: jax.random.normal(k, shp, jnp.float32) * 0.02
        inp = {'x': jax.random.normal(ks[0], (B, 2 * N, D), jnp.float32), 'cond_global': jax.random.normal(ks[1], (B, D), jnp.float32), 'cond_tokens': jax.random.normal(ks[2], (B, LC, D), jnp.float32), 'adaLN_W': w(ks[3], (D, 9 * D)), 'adaLN_b': w(ks[4], (9 * D,)), 'norm1_w': jnp.ones((D,), jnp.float32), 'qkv_W': w(ks[5], (D, 3 * D)), 'attn_out_W': w(ks[6], (D, D)), 'normc_w': jnp.ones((D,), jnp.float32), 'cq_W': w(ks[7], (D, D)), 'ck_W': w(ks[8], (D, D)), 'cv_W': w(ks[9], (D, D)), 'co_W': w(ks[10], (D, D)), 'norm2_w': jnp.ones((D,), jnp.float32), 'mlp_W1': w(ks[11], (D, 4 * D)), 'mlp_b1': w(ks[12], (4 * D,)), 'mlp_W2': w(ks[13], (4 * D, D)), 'mlp_b2': w(ks[14], (D,)), 'cond_kv_mask': jnp.ones((B, LC), bool), 'attn_mask': _block_diff_mask(N, BLOCK)}
        return inp
    _L3_xcond_all = _L3_xcond_setup()
    _L3_xcond_in = {k: v for k, v in _L3_xcond_all.items() if k in ('adaLN_W', 'adaLN_b', 'norm1_w', 'qkv_W', 'attn_out_W', 'normc_w', 'cq_W', 'ck_W', 'cv_W', 'co_W', 'norm2_w', 'mlp_W1', 'mlp_b1', 'mlp_W2', 'mlp_b2')}
    del _L3_xcond_all
    return {'x': x, 'cond_1024': cond_1024, 'ctx_1024': ctx_1024, 'mask_BxS2_ik0': mask_BxS2_ik0, 'mask_BxS2_bf1': mask_BxS2_bf1, 'mask_SxS_bk0': mask_SxS_bk0, 'L0_xcond_W_mod': _L0_xcond_in['W_mod'], 'L0_xcond_b_mod': _L0_xcond_in['b_mod'], 'L0_xcond_W_qkv': _L0_xcond_in['W_qkv'], 'L0_xcond_b_qkv': _L0_xcond_in['b_qkv'], 'L0_xcond_W_proj': _L0_xcond_in['W_proj'], 'L0_xcond_b_proj': _L0_xcond_in['b_proj'], 'L0_xcond_W_qc': _L0_xcond_in['W_qc'], 'L0_xcond_b_qc': _L0_xcond_in['b_qc'], 'L0_xcond_W_kvc': _L0_xcond_in['W_kvc'], 'L0_xcond_b_kvc': _L0_xcond_in['b_kvc'], 'L0_xcond_W_cproj': _L0_xcond_in['W_cproj'], 'L0_xcond_b_cproj': _L0_xcond_in['b_cproj'], 'L0_xcond_W_mlp1': _L0_xcond_in['W_mlp1'], 'L0_xcond_b_mlp1': _L0_xcond_in['b_mlp1'], 'L0_xcond_W_mlp2': _L0_xcond_in['W_mlp2'], 'L0_xcond_b_mlp2': _L0_xcond_in['b_mlp2'], 'L1_xcond_w_ada': _L1_xcond_in['w_ada'], 'L1_xcond_b_ada': _L1_xcond_in['b_ada'], 'L1_xcond_w_qkv': _L1_xcond_in['w_qkv'], 'L1_xcond_b_qkv': _L1_xcond_in['b_qkv'], 'L1_xcond_w_so': _L1_xcond_in['w_so'], 'L1_xcond_b_so': _L1_xcond_in['b_so'], 'L1_xcond_w_q': _L1_xcond_in['w_q'], 'L1_xcond_b_q': _L1_xcond_in['b_q'], 'L1_xcond_w_kv': _L1_xcond_in['w_kv'], 'L1_xcond_b_kv': _L1_xcond_in['b_kv'], 'L1_xcond_w_co': _L1_xcond_in['w_co'], 'L1_xcond_b_co': _L1_xcond_in['b_co'], 'L1_xcond_w_m1': _L1_xcond_in['w_m1'], 'L1_xcond_b_m1': _L1_xcond_in['b_m1'], 'L1_xcond_w_m2': _L1_xcond_in['w_m2'], 'L1_xcond_b_m2': _L1_xcond_in['b_m2'], 'L2_xcond_ln1_g': _L2_xcond_in['ln1_g'], 'L2_xcond_ln1_b': _L2_xcond_in['ln1_b'], 'L2_xcond_ln3_g': _L2_xcond_in['ln3_g'], 'L2_xcond_ln3_b': _L2_xcond_in['ln3_b'], 'L2_xcond_ln2_g': _L2_xcond_in['ln2_g'], 'L2_xcond_ln2_b': _L2_xcond_in['ln2_b'], 'L2_xcond_sa_wq': _L2_xcond_in['sa_wq'], 'L2_xcond_sa_bq': _L2_xcond_in['sa_bq'], 'L2_xcond_sa_wk': _L2_xcond_in['sa_wk'], 'L2_xcond_sa_bk': _L2_xcond_in['sa_bk'], 'L2_xcond_sa_wv': _L2_xcond_in['sa_wv'], 'L2_xcond_sa_bv': _L2_xcond_in['sa_bv'], 'L2_xcond_sa_wo': _L2_xcond_in['sa_wo'], 'L2_xcond_sa_bo': _L2_xcond_in['sa_bo'], 'L2_xcond_ca_wq': _L2_xcond_in['ca_wq'], 'L2_xcond_ca_bq': _L2_xcond_in['ca_bq'], 'L2_xcond_ca_wk': _L2_xcond_in['ca_wk'], 'L2_xcond_ca_bk': _L2_xcond_in['ca_bk'], 'L2_xcond_ca_wv': _L2_xcond_in['ca_wv'], 'L2_xcond_ca_bv': _L2_xcond_in['ca_bv'], 'L2_xcond_ca_wo': _L2_xcond_in['ca_wo'], 'L2_xcond_ca_bo': _L2_xcond_in['ca_bo'], 'L2_xcond_tp_w': _L2_xcond_in['tp_w'], 'L2_xcond_tp_b': _L2_xcond_in['tp_b'], 'L2_xcond_w1': _L2_xcond_in['w1'], 'L2_xcond_b1': _L2_xcond_in['b1'], 'L2_xcond_w2': _L2_xcond_in['w2'], 'L2_xcond_b2': _L2_xcond_in['b2'], 'L3_xcond_adaLN_W': _L3_xcond_in['adaLN_W'], 'L3_xcond_adaLN_b': _L3_xcond_in['adaLN_b'], 'L3_xcond_norm1_w': _L3_xcond_in['norm1_w'], 'L3_xcond_qkv_W': _L3_xcond_in['qkv_W'], 'L3_xcond_attn_out_W': _L3_xcond_in['attn_out_W'], 'L3_xcond_normc_w': _L3_xcond_in['normc_w'], 'L3_xcond_cq_W': _L3_xcond_in['cq_W'], 'L3_xcond_ck_W': _L3_xcond_in['ck_W'], 'L3_xcond_cv_W': _L3_xcond_in['cv_W'], 'L3_xcond_co_W': _L3_xcond_in['co_W'], 'L3_xcond_norm2_w': _L3_xcond_in['norm2_w'], 'L3_xcond_mlp_W1': _L3_xcond_in['mlp_W1'], 'L3_xcond_mlp_b1': _L3_xcond_in['mlp_b1'], 'L3_xcond_mlp_W2': _L3_xcond_in['mlp_W2'], 'L3_xcond_mlp_b2': _L3_xcond_in['mlp_b2']}

def reference(x, cond_1024, ctx_1024, mask_BxS2_ik0, mask_BxS2_bf1, mask_SxS_bk0, L0_xcond_W_mod, L0_xcond_b_mod, L0_xcond_W_qkv, L0_xcond_b_qkv, L0_xcond_W_proj, L0_xcond_b_proj, L0_xcond_W_qc, L0_xcond_b_qc, L0_xcond_W_kvc, L0_xcond_b_kvc, L0_xcond_W_cproj, L0_xcond_b_cproj, L0_xcond_W_mlp1, L0_xcond_b_mlp1, L0_xcond_W_mlp2, L0_xcond_b_mlp2, L1_xcond_w_ada, L1_xcond_b_ada, L1_xcond_w_qkv, L1_xcond_b_qkv, L1_xcond_w_so, L1_xcond_b_so, L1_xcond_w_q, L1_xcond_b_q, L1_xcond_w_kv, L1_xcond_b_kv, L1_xcond_w_co, L1_xcond_b_co, L1_xcond_w_m1, L1_xcond_b_m1, L1_xcond_w_m2, L1_xcond_b_m2, L2_xcond_ln1_g, L2_xcond_ln1_b, L2_xcond_ln3_g, L2_xcond_ln3_b, L2_xcond_ln2_g, L2_xcond_ln2_b, L2_xcond_sa_wq, L2_xcond_sa_bq, L2_xcond_sa_wk, L2_xcond_sa_bk, L2_xcond_sa_wv, L2_xcond_sa_bv, L2_xcond_sa_wo, L2_xcond_sa_bo, L2_xcond_ca_wq, L2_xcond_ca_bq, L2_xcond_ca_wk, L2_xcond_ca_bk, L2_xcond_ca_wv, L2_xcond_ca_bv, L2_xcond_ca_wo, L2_xcond_ca_bo, L2_xcond_tp_w, L2_xcond_tp_b, L2_xcond_w1, L2_xcond_b1, L2_xcond_w2, L2_xcond_b2, L3_xcond_adaLN_W, L3_xcond_adaLN_b, L3_xcond_norm1_w, L3_xcond_qkv_W, L3_xcond_attn_out_W, L3_xcond_normc_w, L3_xcond_cq_W, L3_xcond_ck_W, L3_xcond_cv_W, L3_xcond_co_W, L3_xcond_norm2_w, L3_xcond_mlp_W1, L3_xcond_mlp_b1, L3_xcond_mlp_W2, L3_xcond_mlp_b2):
    import jax
    import jax.numpy as jnp

    def _L0_xcond_ref(x, c, context, W_mod, b_mod, W_qkv, b_qkv, W_proj, b_proj, W_qc, b_qc, W_kvc, b_kvc, W_cproj, b_cproj, W_mlp1, b_mlp1, W_mlp2, b_mlp2):
        import jax, jax.numpy as jnp
        import numpy as np
        LN_EPS = 1e-06

        def _ln(x):
            mu = jnp.mean(x, axis=-1, keepdims=True)
            var = jnp.var(x, axis=-1, keepdims=True)
            return (x - mu) * jax.lax.rsqrt(var + LN_EPS)
        B, N, H = x.shape
        NH = 16
        hd = H // NH
        scale = hd ** (-0.5)
        c_proj = jax.nn.silu(c) @ W_mod + b_mod
        shift_a, scale_a, gate_a, shift_m, scale_m, gate_m = jnp.split(c_proj, 6, axis=-1)

        def modulate(t, shift, sc):
            return t * (1 + sc[:, None]) + shift[:, None]
        x_norm = modulate(_ln(x), shift_a, scale_a)
        qkv = x_norm @ W_qkv + b_qkv
        q, k, v = jnp.split(qkv, 3, axis=-1)
        q = q.reshape(B, N, NH, hd).transpose(0, 2, 1, 3)
        k = k.reshape(B, N, NH, hd).transpose(0, 2, 1, 3)
        v = v.reshape(B, N, NH, hd).transpose(0, 2, 1, 3)
        attn_w = jax.nn.softmax(jnp.einsum('bhqd,bhkd->bhqk', q, k) * scale, axis=-1)
        attn_out = jnp.einsum('bhqk,bhkd->bhqd', attn_w, v)
        attn_out = attn_out.transpose(0, 2, 1, 3).reshape(B, N, H)
        attn_out = attn_out @ W_proj + b_proj
        x = x + gate_a[:, None] * attn_out
        S = context.shape[1]
        q_c = _ln(x) @ W_qc + b_qc
        kv_c = _ln(context) @ W_kvc + b_kvc
        k_c, v_c = jnp.split(kv_c, 2, axis=-1)
        q_c = q_c.reshape(B, N, NH, hd).transpose(0, 2, 1, 3)
        k_c = k_c.reshape(B, S, NH, hd).transpose(0, 2, 1, 3)
        v_c = v_c.reshape(B, S, NH, hd).transpose(0, 2, 1, 3)
        c_attn_w = jax.nn.softmax(jnp.einsum('bhqd,bhsd->bhqs', q_c, k_c) * scale, axis=-1)
        c_attn_out = jnp.einsum('bhqs,bhsd->bhqd', c_attn_w, v_c)
        c_attn_out = c_attn_out.transpose(0, 2, 1, 3).reshape(B, N, H)
        c_attn_out = c_attn_out @ W_cproj + b_cproj
        x = x + c_attn_out
        x_norm2 = modulate(_ln(x), shift_m, scale_m)
        h = jax.nn.gelu(x_norm2 @ W_mlp1 + b_mlp1)
        h = h @ W_mlp2 + b_mlp2
        x = x + gate_m[:, None] * h
        return x

    def _L1_xcond_ref(x, mod, context, w_ada, b_ada, w_qkv, b_qkv, w_so, b_so, w_q, b_q, w_kv, b_kv, w_co, b_co, w_m1, b_m1, w_m2, b_m2):
        import jax, jax.numpy as jnp
        import numpy as np
        C = 128
        H = 16
        D = C // H
        WIN = 64
        SHIFT = 32
        TOPK = 16
        HID = 512
        EPS = 1e-06

        def _ln(x):
            x32 = x.astype(jnp.float32)
            m = x32.mean(-1, keepdims=True)
            v = jnp.mean((x32 - m) ** 2, axis=-1, keepdims=True)
            return ((x32 - m) * jax.lax.rsqrt(v + EPS)).astype(x.dtype)

        def _self_attn(h, w_qkv, b_qkv, w_so, b_so):
            B, L, _ = h.shape
            qkv = h @ w_qkv + b_qkv
            qkv = jnp.roll(qkv, -SHIFT, axis=1)
            nw = L // WIN
            qkv = qkv.reshape(B, nw, WIN, 3, H, D)
            q, k, v = (qkv[:, :, :, 0], qkv[:, :, :, 1], qkv[:, :, :, 2])
            scores = jnp.einsum('bnqhd,bnkhd->bnhqk', q, k) / jnp.sqrt(jnp.float32(D)).astype(h.dtype)
            attn = jax.nn.softmax(scores, axis=-1)
            o = jnp.einsum('bnhqk,bnkhd->bnqhd', attn, v).reshape(B, L, C)
            o = jnp.roll(o, SHIFT, axis=1)
            return o @ w_so + b_so

        def _topk_cross_attn(h, ctx, w_q, b_q, w_kv, b_kv, w_co, b_co):
            B, L, _ = h.shape
            Lc = ctx.shape[1]
            q = (h @ w_q + b_q).reshape(B, L, H, D)
            kv = (ctx @ w_kv + b_kv).reshape(B, Lc, 2, H, D)
            k, v = (kv[:, :, 0], kv[:, :, 1])
            scores = jnp.einsum('bqhd,bkhd->bhqk', q, k) / jnp.sqrt(jnp.float32(D)).astype(h.dtype)
            top_s, top_i = jax.lax.top_k(scores, TOPK)
            attn = jax.nn.softmax(top_s, axis=-1)
            v_bh = jnp.transpose(v, (0, 2, 1, 3))
            vg = jnp.take_along_axis(v_bh[:, :, None, :, :], top_i[..., None], axis=3)
            o = jnp.einsum('bhqk,bhqkd->bqhd', attn, vg).reshape(B, L, C)
            return o @ w_co + b_co

        def _swiglu(h, w_m1, b_m1, w_m2, b_m2):
            u = h @ w_m1 + b_m1
            a, b = (u[..., :HID], u[..., HID:])
            return jax.nn.silu(a) * b @ w_m2 + b_m2
        m = jax.nn.silu(mod) @ w_ada + b_ada
        sh_msa, sc_msa, g_msa, sh_mca, sc_mca, g_mca, sh_mlp, sc_mlp, g_mlp = [m[:, i * C:(i + 1) * C][:, None, :] for i in range(9)]
        h = _ln(x) * (1 + sc_msa) + sh_msa
        h = _self_attn(h, w_qkv, b_qkv, w_so, b_so)
        x = x + h * g_msa
        h = _ln(x) * (1 + sc_mca) + sh_mca
        h = _topk_cross_attn(h, context, w_q, b_q, w_kv, b_kv, w_co, b_co)
        x = x + h * g_mca
        h = _ln(x) * (1 + sc_mlp) + sh_mlp
        h = _swiglu(h, w_m1, b_m1, w_m2, b_m2)
        x = x + h * g_mlp
        return x

    def _L2_xcond_ref(x, t_emb, context_emb, mask, ln1_g, ln1_b, ln3_g, ln3_b, ln2_g, ln2_b, sa_wq, sa_bq, sa_wk, sa_bk, sa_wv, sa_bv, sa_wo, sa_bo, ca_wq, ca_bq, ca_wk, ca_bk, ca_wv, ca_bv, ca_wo, ca_bo, tp_w, tp_b, w1, b1, w2, b2):
        import jax, jax.numpy as jnp
        import numpy as np
        D = 128
        H = 16
        HD = D // H
        FF = 4 * D
        B, NQ, NK = (8, 128, 64)
        EPS = 1e-05

        def layernorm(x, g, b):
            m = jnp.mean(x, axis=-1, keepdims=True)
            v = jnp.mean(jnp.square(x - m), axis=-1, keepdims=True)
            return (x - m) * jax.lax.rsqrt(v + EPS) * g + b

        def mha(x, ctx, wq, bq, wk, bk, wv, bv, wo, bo, mask=None):
            Bq, Nq, _ = x.shape
            Nk = ctx.shape[1]
            q = (x @ wq + bq).reshape(Bq, Nq, H, HD)
            k = (ctx @ wk + bk).reshape(Bq, Nk, H, HD)
            v = (ctx @ wv + bv).reshape(Bq, Nk, H, HD)
            scores = jnp.einsum('bqhd,bkhd->bhqk', q, k) / np.sqrt(HD)
            if mask is not None:
                scores = jnp.where(mask[:, None, None, :].astype(bool), scores, -jnp.inf)
            attn = jax.nn.softmax(scores.astype(jnp.float32), axis=-1).astype(scores.dtype)
            out = jnp.einsum('bhqk,bkhd->bqhd', attn, v).reshape(Bq, Nq, D)
            return out @ wo + bo
        t_biases = jax.nn.silu(t_emb) @ tp_w + tp_b
        t_sa, t_ca, t_mlp = jnp.split(t_biases, 3, axis=-1)
        h = layernorm(x, ln1_g, ln1_b)
        h = mha(h, h, sa_wq, sa_bq, sa_wk, sa_bk, sa_wv, sa_bv, sa_wo, sa_bo)
        x = x + h + t_sa[:, None, :]
        h = layernorm(x, ln3_g, ln3_b)
        h = mha(h, context_emb, ca_wq, ca_bq, ca_wk, ca_bk, ca_wv, ca_bv, ca_wo, ca_bo, mask=mask)
        x = x + h + t_ca[:, None, :]
        h = layernorm(x, ln2_g, ln2_b)
        h = jax.nn.gelu(h @ w1 + b1, approximate=False) @ w2 + b2
        x = x + h + t_mlp[:, None, :]
        return x

    def _L3_xcond_ref(x, cond_global, cond_tokens, adaLN_W, adaLN_b, norm1_w, qkv_W, attn_out_W, normc_w, cq_W, ck_W, cv_W, co_W, norm2_w, mlp_W1, mlp_b1, mlp_W2, mlp_b2, cond_kv_mask, attn_mask):
        import jax, jax.numpy as jnp
        import numpy as np
        B, N, D, H, LC = (2, 128, 128, 16, 77)
        HD = D // H
        BLOCK = 16
        ROPE_BASE = 10000.0
        EPS = 1e-05

        def _block_diff_mask(n, block_size):
            idx = np.arange(2 * n)
            q = idx[:, None]
            kv = idx[None, :]
            fq = q >= n
            fkv = kv >= n
            bq = np.where(fq, (q - n) // block_size, q // block_size)
            bkv = np.where(fkv, (kv - n) // block_size, kv // block_size)
            block_diagonal = (bq == bkv) & (fq == fkv)
            offset_block_causal = (bq > bkv) & fkv & ~fq
            block_causal = (bq >= bkv) & fq & fkv
            return jnp.asarray(block_diagonal | offset_block_causal | block_causal)

        def _rope_tables(n):
            inv_freq = 1.0 / ROPE_BASE ** (np.arange(0, HD, 2, dtype=np.float32) / HD)
            freqs = np.outer(np.arange(n, dtype=np.float32), inv_freq)
            emb = np.concatenate([freqs, freqs], axis=-1)
            cos = jnp.asarray(np.cos(emb), jnp.float32)[None, :, None, :]
            sin = jnp.asarray(np.sin(emb), jnp.float32)[None, :, None, :]
            return (cos, sin)

        def _ln(x, w):
            xf = x.astype(jnp.float32)
            mu = jnp.mean(xf, axis=-1, keepdims=True)
            var = jnp.mean(jnp.square(xf - mu), axis=-1, keepdims=True)
            y = (xf - mu) * jax.lax.rsqrt(var + EPS)
            return y * w[None, None, :]

        def _apply_rope(t, cos, sin):
            t1, t2 = jnp.split(t, 2, axis=-1)
            rot = jnp.concatenate([-t2, t1], axis=-1)
            return t * cos + rot * sin

        def _attn(q, k, v, mask):
            scale = 1.0 / np.sqrt(HD)
            s = jnp.einsum('bqhd,bkhd->bhqk', q, k) * scale
            s = jnp.where(mask, s, jnp.finfo(s.dtype).min)
            a = jax.nn.softmax(s, axis=-1)
            return jnp.einsum('bhqk,bkhd->bqhd', a, v)
        b, s, d = x.shape
        n = s // 2
        mod = (cond_global @ adaLN_W + adaLN_b)[:, None, :]
        sh_msa, sc_msa, g_msa, sh_x, sc_x, g_x, sh_mlp, sc_mlp, g_mlp = jnp.split(mod, 9, axis=-1)
        x_norm = _ln(x, norm1_w) * (1 + sc_msa) + sh_msa
        cos, sin = _rope_tables(n)

        def qkv(h):
            t = (h @ qkv_W).reshape(b, n, 3, H, HD)
            q, k, v = (t[:, :, 0], t[:, :, 1], t[:, :, 2])
            return (_apply_rope(q, cos, sin), _apply_rope(k, cos, sin), v)
        q1, k1, v1 = qkv(x_norm[:, :n])
        q2, k2, v2 = qkv(x_norm[:, n:])
        q = jnp.concatenate([q1, q2], axis=1)
        k = jnp.concatenate([k1, k2], axis=1)
        v = jnp.concatenate([v1, v2], axis=1)
        self_out = _attn(q, k, v, attn_mask[None, None]).reshape(b, s, d) @ attn_out_W
        x = x + g_msa * self_out
        xc = _ln(x, normc_w) * (1 + sc_x) + sh_x
        qc = (xc @ cq_W).reshape(b, s, H, HD)
        kc = (cond_tokens @ ck_W).reshape(b, LC, H, HD)
        vc = (cond_tokens @ cv_W).reshape(b, LC, H, HD)
        cross = _attn(qc, kc, vc, cond_kv_mask[:, None, None, :]).reshape(b, s, d) @ co_W
        x = x + g_x * cross
        xm = _ln(x, norm2_w) * (1 + sc_mlp) + sh_mlp
        h = jax.nn.gelu(xm @ mlp_W1 + mlp_b1, approximate=True)
        mlp_out = h @ mlp_W2 + mlp_b2
        return x + g_mlp * mlp_out
    x = _L0_xcond_ref(x, cond_1024, ctx_1024, L0_xcond_W_mod, L0_xcond_b_mod, L0_xcond_W_qkv, L0_xcond_b_qkv, L0_xcond_W_proj, L0_xcond_b_proj, L0_xcond_W_qc, L0_xcond_b_qc, L0_xcond_W_kvc, L0_xcond_b_kvc, L0_xcond_W_cproj, L0_xcond_b_cproj, L0_xcond_W_mlp1, L0_xcond_b_mlp1, L0_xcond_W_mlp2, L0_xcond_b_mlp2)
    x = _L1_xcond_ref(x, cond_1024, ctx_1024, L1_xcond_w_ada, L1_xcond_b_ada, L1_xcond_w_qkv, L1_xcond_b_qkv, L1_xcond_w_so, L1_xcond_b_so, L1_xcond_w_q, L1_xcond_b_q, L1_xcond_w_kv, L1_xcond_b_kv, L1_xcond_w_co, L1_xcond_b_co, L1_xcond_w_m1, L1_xcond_b_m1, L1_xcond_w_m2, L1_xcond_b_m2)
    x = _L2_xcond_ref(x, cond_1024, ctx_1024, mask_BxS2_ik0, L2_xcond_ln1_g, L2_xcond_ln1_b, L2_xcond_ln3_g, L2_xcond_ln3_b, L2_xcond_ln2_g, L2_xcond_ln2_b, L2_xcond_sa_wq, L2_xcond_sa_bq, L2_xcond_sa_wk, L2_xcond_sa_bk, L2_xcond_sa_wv, L2_xcond_sa_bv, L2_xcond_sa_wo, L2_xcond_sa_bo, L2_xcond_ca_wq, L2_xcond_ca_bq, L2_xcond_ca_wk, L2_xcond_ca_bk, L2_xcond_ca_wv, L2_xcond_ca_bv, L2_xcond_ca_wo, L2_xcond_ca_bo, L2_xcond_tp_w, L2_xcond_tp_b, L2_xcond_w1, L2_xcond_b1, L2_xcond_w2, L2_xcond_b2)
    x = _L3_xcond_ref(x, cond_1024, ctx_1024, L3_xcond_adaLN_W, L3_xcond_adaLN_b, L3_xcond_norm1_w, L3_xcond_qkv_W, L3_xcond_attn_out_W, L3_xcond_normc_w, L3_xcond_cq_W, L3_xcond_ck_W, L3_xcond_cv_W, L3_xcond_co_W, L3_xcond_norm2_w, L3_xcond_mlp_W1, L3_xcond_mlp_b1, L3_xcond_mlp_W2, L3_xcond_mlp_b2, mask_BxS2_bf1, mask_SxS_bk0)
    return x

_drawn_inputs = setup_inputs


def setup_inputs(seed=0):
    import zlib

    import numpy as np

    out = dict(_drawn_inputs(seed))
    spreads = {'L0_xcond_b_mod': (0.0, 0.1),
     'L0_xcond_b_qkv': (0.0, 0.1),
     'L0_xcond_b_proj': (0.0, 0.1),
     'L0_xcond_b_qc': (0.0, 0.48),
     'L0_xcond_b_kvc': (0.0, 0.1),
     'L0_xcond_b_cproj': (0.0, 0.1),
     'L0_xcond_b_mlp1': (0.0, 0.1),
     'L0_xcond_b_mlp2': (0.0, 0.1),
     'L1_xcond_b_ada': (0.0, 0.764),
     'L1_xcond_b_qkv': (0.0, 0.8),
     'L1_xcond_b_so': (0.0, 0.733),
     'L1_xcond_b_q': (0.0, 0.8),
     'L1_xcond_b_kv': (0.0, 0.8),
     'L1_xcond_b_co': (0.0, 0.675),
     'L1_xcond_b_m1': (0.0, 0.8),
     'L1_xcond_b_m2': (0.0, 0.75),
     'L2_xcond_ln1_g': (1.0, 0.6),
     'L2_xcond_ln1_b': (0.0, 2.0),
     'L2_xcond_ln3_g': (1.0, 0.6),
     'L2_xcond_ln3_b': (0.0, 2.0),
     'L2_xcond_ln2_g': (1.0, 0.6),
     'L2_xcond_ln2_b': (0.0, 2.0),
     'L2_xcond_sa_bq': (0.0, 2.0),
     'L2_xcond_sa_bk': (0.0, 2.0),
     'L2_xcond_sa_bv': (0.0, 2.0),
     'L2_xcond_sa_bo': (0.0, 0.8),
     'L2_xcond_ca_bq': (0.0, 2.0),
     'L2_xcond_ca_bk': (0.0, 2.0),
     'L2_xcond_ca_bv': (0.0, 2.0),
     'L2_xcond_ca_bo': (0.0, 0.8),
     'L2_xcond_tp_b': (0.0, 0.528),
     'L2_xcond_b1': (0.0, 2.0),
     'L2_xcond_b2': (0.0, 0.8),
     'L3_xcond_norm1_w': (1.0, 0.6),
     'L3_xcond_normc_w': (1.0, 0.6),
     'L3_xcond_norm2_w': (1.0, 0.6)}
    factors = {'L1_xcond_w_ada': 3.09,
     'L1_xcond_w_qkv': 8.0,
     'L1_xcond_w_so': 8.0,
     'L1_xcond_w_q': 8.0,
     'L1_xcond_w_kv': 8.0,
     'L1_xcond_w_co': 8.0,
     'L1_xcond_w_m1': 8.0,
     'L1_xcond_w_m2': 8.0,
     'L2_xcond_sa_wq': 64.0,
     'L2_xcond_sa_wk': 64.0,
     'L2_xcond_ca_wq': 62.093,
     'L2_xcond_ca_wk': 51.916,
     'L2_xcond_ca_wv': 17.66,
     'L3_xcond_adaLN_W': 4.652,
     'L3_xcond_adaLN_b': 8.0,
     'L3_xcond_qkv_W': 8.0,
     'L3_xcond_attn_out_W': 8.0,
     'L3_xcond_cq_W': 8.0,
     'L3_xcond_ck_W': 8.0,
     'L3_xcond_cv_W': 8.0,
     'L3_xcond_co_W': 8.0,
     'L3_xcond_mlp_W1': 5.994,
     'L3_xcond_mlp_b1': 30.544,
     'L3_xcond_mlp_W2': 5.87,
     'L3_xcond_mlp_b2': 62.636,
     'L2_xcond_sa_wv': 8.0,
     'L2_xcond_sa_wo': 5.073,
     'L2_xcond_ca_wo': 4.457,
     'L2_xcond_tp_w': 3.03,
     'L2_xcond_w1': 7.915,
     'L2_xcond_w2': 4.5}
    for name, (base, spread) in spreads.items():
        noise = np.random.default_rng([zlib.crc32(name.encode()), seed]).standard_normal(out[name].shape)
        drawn = base * np.exp(spread * noise) if base else spread * noise
        out[name] = jnp.asarray(drawn.astype(out[name].dtype))
    for name, factor in factors.items():
        out[name] = (out[name] * factor).astype(out[name].dtype)
    return out
```

```python
from contextlib import ExitStack

import numpy as np
import concourse.bass as bass
from concourse import mybir

F32 = mybir.dt.float32
BF16 = mybir.dt.bfloat16
I32 = mybir.dt.int32
U8 = mybir.dt.uint8
ALU = mybir.AluOpType
ACT = mybir.ActivationFunctionType
AX_X = mybir.AxisListType.X

P = 128
B, N, C = 4, 512, 128
H, HD = 16, 8
LC = 77
HG = 4
G = H // HG
TT = N // P
VW = 32
SCALE = float(HD) ** -0.5
MASKED = -float(2 ** 100)
TAKEN = -3.0e38
SHIFT, WIN, TOPK = 32, 64, 16
LAYERS = 4
FULL = (0, 2, 3)

PAIRS = ((0, 0), (0, 1), (1, 0), (0, 2), (2, 0), (1, 1))
STACK_M = 73
STACK = 76

EPS = (1e-6, 1e-6, 1e-5, 1e-5)
NMOD = (6, 9, 3, 9)
HID = 512
WIDTHS = [
    dict(mod=768, qkv=384, proj=128, qc=128, kvc=256, cproj=128, m1=512, m2=512),
    dict(mod=1152, qkv=384, proj=128, qc=128, kvc=256, cproj=128, m1=1024, m2=512),
    dict(mod=384, qkv=384, proj=128, qc=128, kvc=256, cproj=128, m1=512, m2=512),
    dict(mod=1152, qkv=384, rot=256, proj=128, qc=128, kvc=256, cproj=128, m1=512, m2=512),
]
COLS = [
    dict(mod=6, qkv=3, qc=1, kvc=2, m1=4),
    dict(mod=9, qkv=3, qc=1, kvc=2, m1=8),
    dict(qkv=3, qc=1, kvc=2, m1=4, lng=3, lnb=3),
    dict(mod=9, m1=4, lng=3),
]
ROWS = 6
GATE = [(2, None, 5), (2, 5, 8), (0, 1, 2), (2, 5, 8)]
MODS = [((0, 1), None, (3, 4)), ((0, 1), (3, 4), (6, 7)), (None, None, None), ((0, 1), (3, 4), (6, 7))]


def offsets(widths):
    out, at = [], 0
    for layer in widths:
        here = {}
        for name, w in layer.items():
            here[name] = at
            at += w
        out.append(here)
    return out, at


W_AT, W_ALL = offsets(WIDTHS)
C_AT, C_ALL = offsets(COLS)


class Signal:

    def __init__(self, ctx, nc, name, per, start=0, step=1):
        self.sem = ctx.enter_context(nc.semaphore(name))
        self.name, self.per, self.start, self.step = name, per, start, step

    def value(self, layer, b, k):
        fixed = self.start + B * sum(self.per[:layer]) + k
        if isinstance(b, int):
            return self.step * (fixed + b * self.per[layer])
        return b * (self.step * self.per[layer]) + self.step * fixed


def build(nc, a, out):
    ctx = ExitStack()
    with ctx:
        def sb(name, shape, dt=F32):
            return ctx.enter_context(nc.sbuf_tensor(name, shape, dt))

        def sem(name):
            return ctx.enter_context(nc.semaphore(name))

        x = sb("x", [P, B * N])
        w = sb("w", [P, W_ALL])
        cols = sb("cols", [P, C_ALL])
        rows = sb("rows", [P, LAYERS * ROWS * C])
        ident = sb("ident", [P, P])
        identb = sb("identb", [P, P], BF16)
        headmask = sb("headmask", [P, H])
        winbias = sb("winbias", [P, P], BF16)
        rope = sb("rope", [P, 2, N])
        ones16 = sb("ones16", [P, H])
        onesrow = sb("onesrow", [1, P], BF16)
        neghalf = sb("neghalf", [P, TT])
        condT = sb("condT", [P, B])
        scondT = sb("scondT", [P, B])
        modc = sb("modc", [P, 9 * B])
        affine = sb("affine", [P, LAYERS * 3 * 2 * B])
        ctxT = sb("ctxT", [P, B * LC])
        zctxT = sb("zctxT", [P, B * LC])
        cmaskc = sb("cmaskc", [LC, B], I32)
        cmaskf = sb("cmaskf", [LC, B])
        cmrow = sb("cmrow", [1, 2 * B * LC], BF16)
        smask = sb("smask", [P, 2 * TT * N], BF16)
        condB = sb("condB", [P, P])
        ctxb = sb("ctxb", [P, LC])
        gate = sb("gate", [P, 3 * C])
        wproj = sb("wproj", [P, C])
        wcproj = sb("wcproj", [P, C])
        wm2 = sb("wm2", [P, 4 * C])
        bias3 = sb("bias3", [P, 3 * C])
        kcT = sb("kcT", [P, LC])
        kblk = sb("kblk", [P, H * LC])
        vc = sb("vc", [LC, H * VW])
        stat = sb("stat", [P, TT * 6])
        mv = sb("mv", [P, TT * 2])
        veps = sb("veps", [P, TT])
        rstd = sb("rstd", [P, TT])
        z = sb("z", [P, N])
        hT = sb("hT", [P, N])
        qT = sb("qT", [P, N])
        kT = sb("kT", [P, N])
        split = sb("split", [P, 2 * 3 * N], BF16)
        vs = sb("vs", [P, TT * H * VW])
        qstack = sb("qstack", [P, H * N], BF16)
        kstack = sb("kstack", [P, H * N], BF16)
        mx = sb("mx", [P, TT * H])
        msplit = sb("msplit", [H, 3 * N], BF16)
        mrest = sb("mrest", [H, N])
        pt = sb("pt", [P, 2 * HG * N])
        e = sb("e", [P, 4 * HG * P])
        top = sb("top", [P, 2 * HG * 8])
        top2 = sb("top2", [P, HG * 8])
        mxs = sb("mxs", [P, 4 * HG])
        oe = sb("oe", [P, G * N])
        rden = sb("rden", [P, TT * H])
        on = sb("on", [P, N])
        oT = sb("oT", [P, N])
        gact = sb("gact", [P, 4 * N])

        rest = oe[:, 0:2 * N]
        rtmp = oe[:, 2 * N:4 * N]
        kwin = gact[:, 0:2 * HG * P]
        srow = gact[:, 2 * HG * P:2 * HG * (P + LC)]
        spick = gact[:, 0:2 * HG * LC]
        smask_u = gact[:, :].bitcast(U8)[:, 0:2 * TT * N]
        winb32 = z[:, 0:P]
        ctok = on[0:LC, :]
        cmrow_i = oT[0:1, 0:B * LC].bitcast(I32)
        cmrow_u = hT[0:1, :].bitcast(U8)[:, 0:B * LC]
        cmtmp = qT[0:1, 0:B * LC]

        ps = [ctx.enter_context(nc.psum_tensor(f"ps{i}", [P, 512], F32)) for i in range(8)]
        psA = [ctx.enter_context(nc.psum_tensor(f"pa{i}", [P, 1024], F32)) for i in range(0)]

        qk_dram = nc.dram_tensor("qk_parts", [2, P, 3, N], BF16, kind="Internal").ap()
        m_dram = nc.dram_tensor("m_parts", [H, 3, N], BF16, kind="Internal").ap()

        def signal(name, per, start=0, step=1):
            return Signal(ctx, nc, name, per, start, step)

        per = PER
        dbank_full = signal("dbank_full", per["d"], start=NPRO_D)
        dbank_read = signal("dbank_read", per["d"], start=NPRO_D)
        abank_full = signal("abank_full", per["a"])
        abank_read = signal("abank_read", per["a"], start=1)
        pv_done = signal("pv_done", per["pv"])
        obank_read = signal("obank_read", [8] * 4, start=1)
        batch_set = signal("batch_set", [1] * 4)
        z_ready = signal("z_ready", [12] * 4)
        var_ready = signal("var_ready", [3] * 4)
        rstd_ready = signal("rstd_ready", [3] * 4)
        pool_step = signal("pool_step", per["ps"], start=2)
        gated = signal("gated", [1] * 4)
        kblk_ready = signal("kblk_ready", [1] * 4)
        xbias = signal("xbias", [3] * 4)
        part_rest = signal("part_rest", per["pr"])
        part_back = signal("part_back", per["pb"])
        qk_split = signal("qk_split", [2 if l in FULL else 0 for l in range(4)])
        stack_in = signal("stack_in", [14 if l in FULL else 0 for l in range(4)], step=16)
        m_split = signal("m_split", [1 if l in FULL else 0 for l in range(4)])
        mstack_in = signal("mstack_in", [2 if l in FULL else 0 for l in range(4)], step=16)
        kwin_ready = signal("kwin_ready", [0, 16, 0, 0])
        exp_ready = signal("exp_ready", per["sub"])
        sel_ready = signal("sel_ready", [0, 16, 0, 0])
        vstep = signal("vstep", per["v"], start=NPRO_V)
        ctx_rstd = sem("ctx_rstd")
        loaded = sem("loaded")
        loaded_w = [sem(f"loaded_w{l}") for l in range(LAYERS)]
        silu_done = sem("silu_done")
        stored = sem("stored")

        def wcol(l, name, at=0, n=C):
            o = W_AT[l][name] + at
            return w[:, o:o + n]

        def col(l, name, j=0):
            o = C_AT[l][name] + j
            return cols[:, o:o + 1]

        def rowv(l, j, n=1):
            o = (l * ROWS + j) * C
            return rows[:, o:o + n * C]

        def aff(l, i, which, b):
            o = ((l * 3 + i) * 2 + which) * B
            return affine[:, bass.ds(b + o, 1)]

        def heads(ap, n):
            return ap.rearrange("p (h n) -> p h n", n=n)

        nk_of = {"win": P, "cross": LC, "topk": LC}

        def short_kind(l):
            return "topk" if l == 1 else "cross"

        def wait_apart(eng, sig, value):
            value = eng.to_reg(value)
            eng.wait_ge(loaded, 16 * N_LOADS)
            eng.wait_ge(sig.sem, value)

        block = ctx.enter_context(nc.Block())

        @block.sync
        def _(sp):
            for dst, src in ((x[:, :], a["x"]), (cols[:, :], a["cols"]),
                             (rows[:, :], a["rows"].partition_broadcast(P)), (ident[:, :], a["ident"]),
                             (headmask[:, :], a["headmask"]), (winb32[:, :], a["winbias"]),
                             (condT[:, :], a["condT"]), (ctxT[:, :], a["ctxT"]), (ctok[:, :], a["ctok"]),
                             (cmaskc[:, :], a["cmask_iT"]),
                             (cmrow_i[:, :], a["cmask_i"].rearrange("(o b) k -> o (b k)", o=1)),
                             (cmrow_u[:, :], a["cmask_u"].rearrange("(o b) k -> o (b k)", o=1)),
                             (rope[:, :, :], a["rope"]), (smask_u[:, 0:TT * N], a["smask"]),
                             (smask_u[:, TT * N:2 * TT * N], a["smaskT"])):
                sp.dma_start(dst, src).then_inc(loaded, 16)
            qk_view = qk_dram.rearrange("s (h d) i t -> s i d h t", d=HD)
            for l in FULL:
                with sp.Fori(0, B) as b:
                    k = 0
                    for s, stack in ((0, qstack), (1, kstack)):
                        sp.wait_ge(qk_split.sem, qk_split.value(l, b, s + 1))
                        sp.dma_start(qk_dram[s], split[:, s * 3 * N:(s + 1) * 3 * N].rearrange(
                            "p (i t) -> p i t", i=3)).then_inc(stack_in.sem, 16)
                        k += 1
                        sp.wait_ge(stack_in.sem, stack_in.value(l, b, k))
                        for r, pair in enumerate(PAIRS):
                            sp.dma_start(stack[r * HD:(r + 1) * HD, :].rearrange("d (h t) -> d h t", h=H),
                                         qk_view[s, pair[s]]).then_inc(stack_in.sem, 16)
                            k += 1
                    sp.wait_ge(m_split.sem, m_split.value(l, b, 1))
                    sp.dma_start(m_dram, msplit[:, :].rearrange("h (i t) -> h i t", i=3)).then_inc(mstack_in.sem, 16)
                    sp.wait_ge(mstack_in.sem, mstack_in.value(l, b, 1))
                    sp.dma_start(qstack[STACK_M:STACK, :].rearrange("i (h t) -> i h t", h=H),
                                 m_dram.rearrange("h i t -> i h t")).then_inc(mstack_in.sem, 16)
                    wait_apart(sp, mstack_in, mstack_in.value(l, b, 2))
            for b in range(B):
                sp.wait_ge(dbank_read.sem, dbank_read.value(3, b, per["d"][3]))
                sp.dma_start(out[:, b * N:(b + 1) * N], x[:, b * N:(b + 1) * N]).then_inc(stored, 16)
            sp.wait_ge(stored, 16 * B)

        @block.tensor
        def _(pe):
            n_pro = [0]

            def pro_bank():
                if n_pro[0] >= 2:
                    pe.wait_ge(dbank_read.sem, n_pro[0] - 1)
                n_pro[0] += 1
                return ps[6 + (n_pro[0] - 1) % 2]

            pe.wait_ge(loaded, 16 * N_LOADS)
            for b in range(B):
                bank = pro_bank()
                pe.wait_ge(vstep.sem, CTX_VAR + 1)
                pe.transpose(bank[:, 0:LC], ctok[:, b * C:(b + 1) * C], ident[0:LC, 0:LC]).then_inc(dbank_full.sem, 1)
            pe.wait_ge(silu_done, 1)
            for l in (0, 1, 3):
                pe.wait_ge(loaded_w[l], 16)
                bank = pro_bank()
                rhs = condT if l == 3 else scondT
                for j in range(NMOD[l]):
                    mm = pe.matmul(bank[:, j * B:(j + 1) * B], wcol(l, "mod", j * C), rhs[:, :], start=True, stop=True)
                mm.then_inc(dbank_full.sem, 1)
            pe.wait_ge(loaded_w[2], 16)

            def batch(l, b):
                d, na, pv, o = [0], [0], [0], [0]

                def dbank():
                    pe.wait_ge(dbank_read.sem, dbank_read.value(l, b, max(d[0] - 1, 0)))
                    d[0] += 1
                    return ps[6 + (d[0] - 1) % 2]

                def abank():
                    pe.wait_ge(abank_read.sem, abank_read.value(l, b, max(na[0] - 1, 0)))
                    na[0] += 1
                    return 2 * ((na[0] - 1) % 2)

                def obank():
                    pe.wait_ge(obank_read.sem, obank_read.value(l, b, max(o[0] - 1, 0)))
                    o[0] += 1
                    return ps[4 + (o[0] - 1) % 2]

                def filled(mm):
                    mm.then_inc(dbank_full.sem, 1)

                def read_d():
                    pe.wait_ge(dbank_read.sem, dbank_read.value(l, b, d[0]))

                def norm_T(i):
                    bank = dbank()
                    for t in range(TT):
                        pe.wait_ge(z_ready.sem, z_ready.value(l, b, 4 * i + t + 1))
                        mm = pe.transpose(bank[:, t * P:(t + 1) * P], z[:, t * P:(t + 1) * P], ident[:, :])
                    filled(mm)
                    read_d()

                def out_proj(weight):
                    pe.wait_ge(obank_read.sem, obank_read.value(l, b, o[0]))
                    first_d = d[0]
                    for t in range(TT):
                        bank = dbank()
                        for g in range(G):
                            mm = pe.transpose(bank[:, g * P:(g + 1) * P], oe[:, g * N + t * P:g * N + (t + 1) * P],
                                              ident[:, :])
                        filled(mm)
                    bank = dbank()
                    for t in range(TT):
                        pe.wait_ge(dbank_read.sem, dbank_read.value(l, b, first_d + t + 1))
                        mm = pe.transpose(bank[:, t * P:(t + 1) * P], on[:, t * P:(t + 1) * P], ident[:, :])
                    filled(mm)
                    read_d()
                    bank = dbank()
                    for t in range(TT):
                        mm = pe.matmul(bank[:, t * C:(t + 1) * C], oT[:, t * P:(t + 1) * P], weight,
                                       start=True, stop=True)
                    filled(mm)

                def short_attention(kind, n_sub, values):
                    nk = nk_of[kind]
                    lag = 2
                    first_a = na[0]
                    for i in range(G * TT + lag):
                        if i < G * TT:
                            g, t = divmod(i, TT)
                            q = qT[:, t * P:(t + 1) * P]
                            bank = dbank()
                            if kind == "win":
                                pe.wait_ge(kwin_ready.sem, kwin_ready.value(l, b, i + 1))
                                ks = kwin[:, (i % 2) * HG * P:(i % 2 + 1) * HG * P]
                                pe.matmul(bank[:, :], q, ks, start=True, stop=False)
                                mm = pe.matmul(bank[:, :].rearrange("p (h k) -> p h k", h=HG), identb[:, :],
                                               winbias[:, :].unsqueeze(1).broadcast_to([P, HG, P]),
                                               start=False, stop=True)
                            else:
                                masked = l in (2, 3)
                                mm = pe.matmul(bank[:, 0:HG * LC], q, kblk[:, g * HG * LC:(g + 1) * HG * LC],
                                               start=True, stop=not masked)
                                if masked:
                                    o_m = (l - 2) * B * LC
                                    mrow = cmrow[:, bass.ds(b * LC + o_m, LC)]
                                    mm = pe.matmul(bank[:, 0:HG * LC].rearrange("p (h k) -> p h k", h=HG),
                                                   onesrow[:, :], mrow.unsqueeze(1).broadcast_to([1, HG, LC]),
                                                   start=False, stop=True)
                            filled(mm)
                        j = i - lag
                        if j >= 0:
                            g, t = divmod(j, TT)
                            pair = abank()
                            bank = ps[pair]
                            if kind == "topk":
                                pe.wait_ge(sel_ready.sem, sel_ready.value(l, b, j + 1))
                            else:
                                pe.wait_ge(exp_ready.sem, exp_ready.value(l, b, n_sub + j + 1))
                            for h in range(HG):
                                ein = e[:, (j % 4) * HG * P + h * nk:(j % 4) * HG * P + (h + 1) * nk]
                                mm = pe.transpose(bank[0:nk, h * P:(h + 1) * P], ein, ident[:, :])
                            mm.then_inc(abank_full.sem, 1)
                            if t == TT - 1:
                                ob = obank()
                                pe.wait_ge(abank_read.sem, abank_read.value(l, b, first_a + j + 1))
                                pb = (g % 2) * HG * N
                                for h in range(HG):
                                    if kind == "win":
                                        for tt in range(TT):
                                            mm = pe.matmul(
                                                ob[h * VW:(h + 1) * VW, tt * P:(tt + 1) * P],
                                                vs[:, (tt * H + g * HG + h) * VW:(tt * H + g * HG + h + 1) * VW],
                                                pt[:, pb + h * N + tt * P:pb + h * N + (tt + 1) * P],
                                                start=True, stop=True)
                                    else:
                                        mm = pe.matmul(ob[h * VW:(h + 1) * VW, :],
                                                       vc[:, (g * HG + h) * VW:(g * HG + h + 1) * VW],
                                                       pt[0:LC, pb + h * N:pb + (h + 1) * N], start=True, stop=True)
                                mm.then_inc(pv_done.sem, 1)
                                pv[0] += 1

                pe.wait_ge(batch_set.sem, batch_set.value(l, b, 1))
                bank = dbank()
                for i, chunk in enumerate(GATE[l]):
                    if chunk is not None:
                        mm = pe.matmul(bank[:, i * C:(i + 1) * C], condB[:, :], wcol(l, "mod", chunk * C),
                                       start=True, stop=True)
                filled(mm)
                bank = dbank()
                pe.matmul(bank[:, 0:LC], wcol(l, "kvc"), ctxb[:, :], start=True, stop=True)
                filled(pe.matmul(bank[0:LC, P:2 * P], ctxb[:, :], wcol(l, "kvc", C), start=True, stop=True))

                norm_T(0)
                if l == 1:
                    for s in (0, 1):
                        bank = dbank()
                        filled(pe.matmul(bank[:, :], wcol(l, "qkv", s * C), hT[:, :], start=True, stop=True))
                else:
                    for s in (0, 1):
                        bank = dbank()
                        filled(pe.matmul(bank[:, :], wcol(l, "qkv", s * C), hT[:, :], start=True, stop=True))
                        if l == 3:
                            bank = dbank()
                            filled(pe.matmul(bank[:, :], wcol(l, "rot", s * C), hT[:, :], start=True, stop=True))
                bank = dbank()
                for t in range(TT):
                    mm = pe.matmul(bank[:, t * C:(t + 1) * C], hT[:, t * P:(t + 1) * P], wcol(l, "qkv", 2 * C),
                                   start=True, stop=True)
                filled(mm)
                if l == 1:
                    read_d()
                    short_attention("win", 0, vs)
                else:
                    pe.wait_ge(stack_in.sem, stack_in.value(l, b, 14))
                    for h in range(H):
                        for t in range(TT):
                            bank = dbank()
                            mm = pe.matmul(bank[:, :], qstack[0:STACK_M, h * N + t * P:h * N + (t + 1) * P],
                                           kstack[0:STACK_M, h * N:(h + 1) * N], start=True, stop=l != 3)
                            if l == 3:
                                mm = pe.matmul(bank[:, :], identb[:, :], smask[:, t * N:(t + 1) * N],
                                               start=False, stop=True)
                            filled(mm)
                    read_d()
                    bank = dbank()
                    for t in range(TT):
                        mm = pe.transpose(bank[0:H, t * P:(t + 1) * P], mx[:, t * H:(t + 1) * H], ident[:, :])
                    filled(mm)
                    pe.wait_ge(mstack_in.sem, mstack_in.value(l, b, 2))
                    n_step = G * TT
                    ob = None
                    for i in range(n_step + 1):
                        if i < n_step:
                            g, kt = divmod(i, TT)
                            for half in range(2):
                                pair = abank()
                                for u in range(2):
                                    h = g * HG + 2 * half + u
                                    mm = pe.matmul(ps[pair + u][:, :],
                                                   kstack[0:STACK, h * N + kt * P:h * N + (kt + 1) * P],
                                                   qstack[0:STACK, h * N:(h + 1) * N], start=True, stop=l != 3)
                                    if l == 3:
                                        mm = pe.matmul(ps[pair + u][:, :], identb[:, :],
                                                       smask[:, (TT + kt) * N:(TT + kt + 1) * N],
                                                       start=False, stop=True)
                                mm.then_inc(abank_full.sem, 1)
                        j = i - 1
                        if j >= 0:
                            g, kt = divmod(j, TT)
                            if kt == 0:
                                ob = obank()
                            pe.wait_ge(abank_read.sem, abank_read.value(l, b, 2 * j + 2))
                            for h in range(HG):
                                hh = g * HG + h
                                mm = pe.matmul(ob[h * VW:(h + 1) * VW, :],
                                               vs[:, (kt * H + hh) * VW:(kt * H + hh + 1) * VW],
                                               pt[:, (j % 2) * HG * N + h * N:(j % 2) * HG * N + (h + 1) * N],
                                               start=kt == 0, stop=kt == TT - 1)
                            mm.then_inc(pv_done.sem, 1)
                            pv[0] += 1
                pe.wait_ge(gated.sem, gated.value(l, b, 1))
                out_proj(wproj[:, :])

                norm_T(1)
                bank = dbank()
                filled(pe.matmul(bank[:, :], wcol(l, "qc"), hT[:, :], start=True, stop=True))
                read_d()
                pe.wait_ge(kblk_ready.sem, kblk_ready.value(l, b, 1))
                short_attention(short_kind(l), 16 if l == 1 else 0, vc)
                out_proj(wcproj[:, :])

                norm_T(2)
                first_a = na[0]
                for c in range(4):
                    pair = abank()
                    pe.matmul(ps[pair][:, :], wcol(l, "m1", c * C), hT[:, :], start=True, stop=True)\
                      .then_inc(abank_full.sem, 1)
                    if l == 1:
                        bank = dbank()
                        filled(pe.matmul(bank[:, :], wcol(l, "m1", HID + c * C), hT[:, :], start=True, stop=True))
                if l == 1:
                    read_d()
                else:
                    pe.wait_ge(abank_read.sem, abank_read.value(l, b, first_a + 4))
                bank = dbank()
                for t in range(TT):
                    for c in range(4):
                        mm = pe.matmul(bank[:, t * C:(t + 1) * C], gact[:, c * N + t * P:c * N + (t + 1) * P],
                                       wm2[:, c * C:(c + 1) * C], start=c == 0, stop=c == 3)
                filled(mm)
                check_count("d", l, d[0])
                check_count("a", l, na[0])
                check_count("pv", l, pv[0])

            for l in range(LAYERS):
                with pe.Fori(0, B) as b:
                    batch(l, b)

        @block.scalar
        def _(act):
            for l in range(LAYERS):
                lo = W_AT[l]["mod"]
                hi = lo + sum(WIDTHS[l].values())
                act.dma_start(w[:, lo:hi], a["w"][:, lo:hi]).then_inc(loaded_w[l], 16)
            act.wait_ge(loaded, 16 * N_LOADS)
            act.activation(scondT[:, :], condT[:, :], ACT.Silu).then_inc(silu_done, 1)
            act.sem_inc(abank_read.sem, 1)
            act.sem_inc(obank_read.sem, 1)

            def batch(l, b):
                na, pv, o, n_sub = [0], [0], [0], [0]

                def full_pair():
                    na[0] += 1
                    act.wait_ge(abank_full.sem, abank_full.value(l, b, na[0]))
                    return 2 * ((na[0] - 1) % 2)

                def copy_out(rolled):
                    g = o[0] % G
                    bank = ps[4 + o[0] % 2]
                    o[0] += 1
                    act.wait_ge(pv_done.sem, pv_done.value(l, b, pv[0]))
                    if rolled:
                        act.activation(oe[:, g * N:g * N + SHIFT], bank[:, N - SHIFT:N], ACT.Copy)
                        act.activation(oe[:, g * N + SHIFT:(g + 1) * N], bank[:, 0:N - SHIFT], ACT.Copy)\
                           .then_inc(obank_read.sem, 1)
                    else:
                        act.activation(oe[:, g * N:(g + 1) * N], bank[:, :], ACT.Copy).then_inc(obank_read.sem, 1)

                def short_attention(kind, n_sub):
                    nk = nk_of[kind]
                    for i in range(G * TT + 1):
                        if i < G * TT:
                            act.wait_ge(dbank_read.sem, dbank_read.value(l, b, FIRST_D[kind][l] + i + 1))
                            ein = e[:, (i % 4) * HG * P:(i % 4) * HG * P + HG * nk]
                            act.activation(ein, ein, ACT.Exp, scale=SCALE).then_inc(exp_ready.sem, 1)
                        j = i - 1
                        if j >= 0:
                            g, t = divmod(j, TT)
                            pair = full_pair()
                            if t == 0 and pv[0] >= 2:
                                act.wait_ge(pv_done.sem, pv_done.value(l, b, pv[0] - 1))
                            pb = (g % 2) * HG * N
                            dst = pt[0:nk, pb:pb + HG * N].rearrange("k (h q) -> k h q", h=HG)[:, :, t * P:(t + 1) * P]
                            act.activation(dst, ps[pair][0:nk, :].rearrange("k (h q) -> k h q", h=HG), ACT.Copy)\
                               .then_inc(abank_read.sem, 1)
                            if t == TT - 1:
                                pv[0] += 1
                                copy_out(kind == "win")

                if l == 1:
                    short_attention("win", 0)
                else:
                    for i in range(G * TT + 1):
                        if i < G * TT:
                            if i >= 2:
                                act.wait_ge(pv_done.sem, pv_done.value(l, b, i - 1))
                            for half in range(2):
                                pair = full_pair()
                                o_p = (i % 2) * HG * N + half * 2 * N
                                for u in range(2):
                                    ins = act.activation(pt[:, o_p + u * N:o_p + (u + 1) * N], ps[pair + u][:, :],
                                                         ACT.Exp, scale=SCALE)
                                ins.then_inc(abank_read.sem, 1)
                        if i > 0 and i % TT == 0:
                            pv[0] = i
                            copy_out(False)
                short_attention(short_kind(l), 16 if l == 1 else 0)
                for c in range(4):
                    pair = full_pair()
                    act.activation(gact[:, c * N:(c + 1) * N], ps[pair][:, :], MLP_ACT[l],
                                   bias=col(l, "m1", c)).then_inc(abank_read.sem, 1)

            for l in range(LAYERS):
                with act.Fori(0, B) as b:
                    batch(l, b)

        @block.gpsimd
        def _(pool):
            pool.memset(neghalf[:, :], -0.5).then_inc(pool_step.sem, 1)
            pool.wait_ge(loaded, 16 * N_LOADS)
            pool.wait_ge(vstep.sem, CTX_VAR)
            pool.tensor_scalar(veps[0:LC, :], mv[0:LC, 1:2 * B:2], EPS[0], None, ALU.add).then_inc(pool_step.sem, 1)
            pool.wait_ge(pool_step.sem, 2)
            pool.tensor_tensor(rstd[0:LC, :], veps[0:LC, :], neghalf[0:LC, :], ALU.pow).then_inc(ctx_rstd, 1)
            for l in range(LAYERS):
                pool.wait_ge(loaded_w[l], 16)

            def batch(l, b):
                ns, npb, npr = [0], [0], [0]

                def step(ins):
                    ns[0] += 1
                    ins.then_inc(pool_step.sem, 1)
                    pool.wait_ge(pool_step.sem, pool_step.value(l, b, ns[0]))

                def inverse_root(i):
                    wait_apart(pool, var_ready, var_ready.value(l, b, i + 1))
                    step(pool.tensor_scalar(veps[:, :], mv[:, 1:2 * TT:2], EPS[l], None, ALU.add))
                    pool.tensor_tensor(rstd[:, :], veps[:, :], neghalf[:, :], ALU.pow).then_inc(rstd_ready.sem, 1)

                def add_bias(i):
                    wait_apart(pool, z_ready, z_ready.value(l, b, 4 * i + 4))
                    xs = x[:, bass.ds(b * N, N)].rearrange("p (t c) -> p t c", t=TT)
                    pool.tensor_tensor(xs, xs, bias3[:, i * C:(i + 1) * C].unsqueeze(1).broadcast_to([P, TT, C]),
                                       ALU.add).then_inc(xbias.sem, 1)

                inverse_root(0)
                wait_apart(pool, dbank_read, dbank_read.value(l, b, 1))
                for i, (dst, name) in enumerate(((wproj, "proj"), (wcproj, "cproj"), (wm2, "m2"))):
                    n = 4 if name == "m2" else 1
                    g3 = gate[:, i * C:(i + 1) * C]
                    src = wcol(l, name, 0, n * C)
                    last = None
                    if l == 2 or GATE[l][i] is None:
                        pool.tensor_copy(dst[:, :], src)
                    else:
                        pool.tensor_tensor(dst[:, :].rearrange("p (c n) -> p c n", c=n),
                                           src.rearrange("p (c n) -> p c n", c=n),
                                           g3.unsqueeze(1).broadcast_to([P, n, C]), ALU.mult)
                    if l == 2:
                        last = pool.tensor_tensor(bias3[:, i * C:(i + 1) * C], rowv(l, i), g3, ALU.add)
                    elif GATE[l][i] is None:
                        last = pool.tensor_copy(bias3[:, i * C:(i + 1) * C], rowv(l, i))
                    else:
                        last = pool.tensor_tensor(bias3[:, i * C:(i + 1) * C], rowv(l, i), g3, ALU.mult)
                last.then_inc(gated.sem, 1)
                pool.wait_ge(gated.sem, gated.value(l, b, 1))
                pool.wait_ge(dbank_read.sem, dbank_read.value(l, b, 2))
                pool.tensor_tensor(kblk[:, :].rearrange("p (h k) -> p h k", h=H),
                                   kcT[:, :].unsqueeze(1).broadcast_to([P, H, LC]),
                                   headmask[:, :].unsqueeze(2).broadcast_to([P, H, LC]), ALU.mult)\
                    .then_inc(kblk_ready.sem, 1)
                add_bias(0)
                if l == 1:
                    pool.wait_ge(dbank_read.sem, dbank_read.value(l, b, 5))
                    for i in range(G * TT):
                        g, t = divmod(i, TT)
                        if i >= 2:
                            pool.wait_ge(dbank_full.sem, dbank_full.value(l, b, 6 + i - 1))
                        ks = kwin[:, (i % 2) * HG * P:(i % 2 + 1) * HG * P]
                        pool.tensor_tensor(ks.rearrange("p (h k) -> p h k", h=HG),
                                           kT[:, t * P:(t + 1) * P].unsqueeze(1).broadcast_to([P, HG, P]),
                                           headmask[:, g * HG:(g + 1) * HG].unsqueeze(2).broadcast_to([P, HG, P]),
                                           ALU.mult).then_inc(kwin_ready.sem, 1)
                else:
                    for s in range(2):
                        sp3 = [split[:, (s * 3 + i) * N:(s * 3 + i + 1) * N] for i in range(3)]
                        r_s = rest[:, s * N:(s + 1) * N]
                        if l == 3:
                            pool.wait_ge(dbank_read.sem, dbank_read.value(l, b, 5 + 2 * s))
                            qf = (qT, kT)[s][:, :]
                            pool.tensor_tensor(qf, qf, rtmp[:, s * N:(s + 1) * N], ALU.add).then_inc(part_back.sem, 1)
                            npb[0] += 1
                            npr[0] += 1
                            pool.wait_ge(part_rest.sem, part_rest.value(l, b, npr[0]))
                            pool.tensor_tensor(r_s, qf, sp3[0], ALU.subtract).then_inc(part_back.sem, 1)
                            npb[0] += 1
                        npr[0] += 1
                        pool.wait_ge(part_rest.sem, part_rest.value(l, b, npr[0]))
                        pool.tensor_tensor(sp3[2], r_s, sp3[1], ALU.subtract).then_inc(qk_split.sem, 1)
                for i in (1, 2):
                    inverse_root(i)
                    add_bias(i)
                check_count("ps", l, ns[0])
                check_count("pb", l, npb[0])
                check_count("pr", l, npr[0])

            for l in range(LAYERS):
                with pool.Fori(0, B) as b:
                    batch(l, b)

        @block.vector
        def _(dve):
            n = [0]

            def pstep(ins):
                n[0] += 1
                ins.then_inc(vstep.sem, 1)
                dve.wait_ge(vstep.sem, n[0])

            dve.memset(ones16[:, :], 1.0)
            dve.memset(onesrow[:, :], 1.0)
            dve.memset(qstack[32:64, :], 0.0)
            dve.memset(qstack[64:96, :], 0.0)
            dve.memset(kstack[32:64, :], 0.0)
            dve.memset(kstack[64:96, :], 1.0)
            dve.memset(vs[:, :], 0.0)
            dve.memset(vc[:, :], 0.0)
            pstep(dve.memset(modc[:, :], 0.0))
            dve.memset(vs[:, :].rearrange("p (h n) -> p h n", n=VW)[:, :, HD], 1.0)
            dve.wait_ge(loaded, 16 * N_LOADS)
            dve.tensor_copy(identb[:, :], ident[:, :])
            dve.tensor_copy(winbias[:, :], winb32[:, :])
            dve.tensor_scalar(cmaskf[:, :], cmaskc[:, :], 0.0, None, ALU.not_equal)
            pstep(dve.tensor_scalar(cmtmp[:, :], cmrow_i[:, :], 0.0, None, ALU.not_equal))
            pstep(dve.tensor_scalar(cmrow[:, 0:B * LC], cmtmp[:, :], 1.0, -MASKED, ALU.subtract, ALU.mult))
            dve.tensor_scalar(cmrow[:, B * LC:2 * B * LC], cmrow_u[:, :], 1.0, -MASKED, ALU.subtract, ALU.mult)
            pstep(dve.tensor_scalar(smask[:, :], smask_u[:, :], 1.0, -MASKED, ALU.subtract, ALU.mult))
            for b in range(B):
                ins = dve.bn_stats(stat[0:LC, b * 6:(b + 1) * 6], ctok[:, b * C:(b + 1) * C])
            pstep(ins)
            for b in range(B):
                ins = dve.bn_aggr(mv[0:LC, 2 * b:2 * b + 2], stat[0:LC, b * 6:(b + 1) * 6])
            pstep(ins)
            assert n[0] == CTX_VAR
            dve.wait_ge(ctx_rstd, 1)
            for b in range(B):
                tok = ctok[:, b * C:(b + 1) * C]
                ins = dve.tensor_scalar(tok, tok, mv[0:LC, 2 * b:2 * b + 1], rstd[0:LC, b:b + 1],
                                        ALU.subtract, ALU.mult)
            ins.then_inc(vstep.sem, 1)
            n[0] += 1
            for b in range(B):
                dve.wait_ge(dbank_full.sem, b + 1)
                dve.tensor_copy(zctxT[:, b * LC:(b + 1) * LC], ps[6 + b % 2][:, 0:LC]).then_inc(dbank_read.sem, 1)
            dve.memset(affine[:, :], 0.0)
            for l in range(LAYERS):
                k = {0: 4, 1: 5, 3: 6}.get(l)
                if k is not None:
                    dve.wait_ge(dbank_full.sem, k + 1)
                    m = modc[:, 0:NMOD[l] * B].rearrange("p (j b) -> p j b", b=B)
                    o = C_AT[l]["mod"]
                    dve.tensor_tensor(m, ps[6 + k % 2][:, 0:NMOD[l] * B].rearrange("p (j b) -> p j b", b=B),
                                      cols[:, o:o + NMOD[l]].unsqueeze(2).broadcast_to([P, NMOD[l], B]), ALU.add)\
                       .then_inc(dbank_read.sem, 1)
                    dve.wait_ge(dbank_read.sem, k + 1)
                for i in range(3):
                    o = (l * 3 + i) * 2 * B
                    sc, sh = affine[:, o:o + B], affine[:, o + B:o + 2 * B]
                    if l == 2:
                        dve.tensor_copy(sc, col(l, "lng", i).broadcast_to([P, B]))
                        pstep(dve.tensor_copy(sh, col(l, "lnb", i).broadcast_to([P, B])))
                    elif MODS[l][i] is None:
                        pstep(dve.memset(sc, 1.0))
                    else:
                        jsh, jsc = MODS[l][i]
                        dve.tensor_copy(sh, modc[:, jsh * B:(jsh + 1) * B])
                        if l == 3:
                            pstep(dve.tensor_scalar(sc, modc[:, jsc * B:(jsc + 1) * B], 1.0, col(l, "lng", i),
                                                    ALU.add, ALU.mult))
                        else:
                            pstep(dve.tensor_scalar(sc, modc[:, jsc * B:(jsc + 1) * B], 1.0, None, ALU.add))
            dve.wait_ge(silu_done, 1)
            assert n[0] == NPRO_V, n[0]

            def batch(l, b):
                d, nv, npr, npb = [0], [0], [0], [0]

                def step(ins, separate=False):
                    nv[0] += 1
                    ins.then_inc(vstep.sem, 1)
                    if separate:
                        wait_apart(dve, vstep, vstep.value(l, b, nv[0]))
                    else:
                        dve.wait_ge(vstep.sem, vstep.value(l, b, nv[0]))

                def full():
                    d[0] += 1
                    dve.wait_ge(dbank_full.sem, dbank_full.value(l, b, d[0]))
                    return ps[6 + (d[0] - 1) % 2]

                def done(ins):
                    ins.then_inc(dbank_read.sem, 1)

                def xtile(t, nt=1):
                    return x[:, bass.ds(b * N + t * C, nt * C)]

                def layernorm(i):
                    for t in range(TT):
                        ins = dve.bn_stats(stat[:, t * 6:(t + 1) * 6], xtile(t))
                    step(ins, True)
                    for t in range(TT):
                        ins = dve.bn_aggr(mv[:, 2 * t:2 * t + 2], stat[:, t * 6:(t + 1) * 6])
                    ins.then_inc(var_ready.sem, 1)
                    dve.wait_ge(rstd_ready.sem, rstd_ready.value(l, b, i + 1))
                    for t in range(TT):
                        dve.tensor_scalar(z[:, t * P:(t + 1) * P], xtile(t), mv[:, 2 * t:2 * t + 1],
                                          rstd[:, t:t + 1], ALU.subtract, ALU.mult).then_inc(z_ready.sem, 1)

                def norm_T(i):
                    bank = full()
                    sc, sh = aff(l, i, 0, b), aff(l, i, 1, b)
                    if l == 1 and i == 0:
                        dve.tensor_scalar(hT[:, N - SHIFT:N], bank[:, 0:SHIFT], sc, sh, ALU.mult, ALU.add)
                        done(dve.tensor_scalar(hT[:, 0:N - SHIFT], bank[:, SHIFT:N], sc, sh, ALU.mult, ALU.add))
                    else:
                        done(dve.tensor_scalar(hT[:, :], bank[:, :], sc, sh, ALU.mult, ALU.add))

                def out_proj(i, vbias):
                    for t in range(TT):
                        bank = full()
                        o4 = bank[:, :].rearrange("p (h n) -> p h n", n=VW)
                        rd = rden[:, t * H:(t + 1) * H]
                        step(dve.reciprocal(rd, o4[:, :, HD]))
                        done(dve.tensor_tensor(on[:, t * P:(t + 1) * P].rearrange("p (h n) -> p h n", n=HD),
                                               o4[:, :, 0:HD], rd.unsqueeze(2).broadcast_to([P, H, HD]), ALU.mult))
                    bank = full()
                    if vbias is None:
                        done(dve.tensor_copy(oT[:, :], bank[:, :]))
                    else:
                        done(dve.tensor_scalar(oT[:, :], bank[:, :], vbias, None, ALU.add))
                    residual(i)

                def residual(i):
                    bank = full()
                    dve.wait_ge(xbias.sem, xbias.value(l, b, i + 1))
                    done(dve.tensor_tensor(xtile(0, TT), bank[:, :], xtile(0, TT), ALU.add))
                    wait_apart(dve, dbank_read, dbank_read.value(l, b, d[0]))

                def short_attention(kind, n_sub, first_a):
                    nk = nk_of[kind]
                    assert d[0] == FIRST_D[kind][l], (kind, l, d[0])
                    for i in range(G * TT + (1 if kind == "topk" else 0)):
                        if i < G * TT:
                            bank = full()
                            s4 = bank[:, 0:HG * nk].rearrange("p (h k) -> p h k", h=HG)
                            e4 = e[:, (i % 4) * HG * P:(i % 4) * HG * P + HG * nk].rearrange("p (h k) -> p h k", h=HG)
                            if kind == "topk":
                                sr = srow[:, (i % 2) * HG * LC:(i % 2 + 1) * HG * LC]
                                sp_ = spick[:, (i % 2) * HG * LC:(i % 2 + 1) * HG * LC]
                                tp = top[:, (i % 2) * HG * 8:(i % 2 + 1) * HG * 8]
                                step(dve.tensor_copy(sr, bank[:, 0:HG * LC]), True)
                                for rnd in range(TOPK // 8):
                                    src = sr if rnd == 0 else sp_
                                    best = tp if rnd == 0 else top2[:, :]
                                    for h in range(HG):
                                        ins = dve.max(best[:, h * 8:(h + 1) * 8], src[:, h * LC:(h + 1) * LC])
                                    step(ins, True)
                                    for h in range(HG):
                                        ins = dve.match_replace(sp_[:, h * LC:(h + 1) * LC], best[:, h * 8:(h + 1) * 8],
                                                                src[:, h * LC:(h + 1) * LC], TAKEN)
                                    step(ins, True)
                                m4 = tp[:, 0:HG * 8:8]
                            else:
                                m4 = mxs[:, (i % 4) * HG:(i % 4 + 1) * HG]
                                step(dve.tensor_reduce(m4, s4, AX_X, ALU.max))
                            if i >= 4:
                                dve.wait_ge(abank_full.sem, abank_full.value(l, b, first_a + i - 3))
                            done(dve.tensor_tensor(e4, s4, m4.unsqueeze(2).broadcast_to([P, HG, nk]), ALU.subtract))
                        j = i - 1
                        if kind == "topk" and j >= 0:
                            dve.wait_ge(exp_ready.sem, exp_ready.value(l, b, n_sub + j + 1))
                            ej = e[:, (j % 4) * HG * P:(j % 4) * HG * P + HG * nk]
                            dve.scalar_tensor_tensor(out=ej, in0=spick[:, (j % 2) * HG * LC:(j % 2 + 1) * HG * LC],
                                                     scalar=TAKEN, in1=ej, op0=ALU.is_le, op1=ALU.mult)\
                               .then_inc(sel_ready.sem, 1)

                src = condT if l == 3 else scondT
                dve.tensor_copy(condB[:, :], src[:, bass.ds(b, 1)].broadcast_to([P, P]))
                src = zctxT if l == 0 else ctxT
                dve.tensor_copy(ctxb[:, :], src[:, bass.ds(b * LC, LC)]).then_inc(batch_set.sem, 1)
                layernorm(0)
                bank = full()
                if l == 0:
                    dve.tensor_tensor(gate[:, 0:C], bank[:, 0:C], rowv(l, 3), ALU.add)
                    done(dve.tensor_tensor(gate[:, 2 * C:3 * C], bank[:, 2 * C:3 * C], rowv(l, 5), ALU.add))
                else:
                    done(dve.tensor_tensor(gate[:, :], bank[:, 0:3 * C], rowv(l, 3, 3), ALU.add))
                bank = full()
                if l == 3:
                    dve.tensor_copy(kcT[:, :], bank[:, 0:LC])
                else:
                    dve.tensor_scalar(kcT[:, :], bank[:, 0:LC], col(l, "kvc", 0), None, ALU.add)
                v3 = vc[:, :].rearrange("p (h n) -> p h n", n=VW)
                src = bank[0:LC, P:2 * P].rearrange("p (h n) -> p h n", n=HD)
                if l == 2:
                    mk = cmaskf[:, bass.ds(b, 1)]
                    dve.tensor_scalar(v3[:, :, HD], ones16[0:LC, :], mk, None, ALU.mult)
                    done(dve.tensor_scalar(v3[:, :, 0:HD], src, mk, None, ALU.mult))
                else:
                    dve.tensor_copy(v3[:, :, HD], ones16[0:LC, :])
                    done(dve.tensor_copy(v3[:, :, 0:HD], src))
                norm_T(0)
                first_a = 0
                if l == 1:
                    for s, dst in ((0, qT), (1, kT)):
                        bank = full()
                        done(dve.tensor_scalar(dst[:, :], bank[:, :], col(l, "qkv", s), None, ALU.add))
                else:
                    for s in range(2):
                        sp3 = [split[:, (s * 3 + i) * N:(s * 3 + i + 1) * N] for i in range(3)]
                        r_s = rest[:, s * N:(s + 1) * N]
                        if l == 3:
                            qf = (qT, kT)[s][:, :]
                            bank = full()
                            done(dve.tensor_tensor(qf, bank[:, :], rope[:, 0, :], ALU.mult))
                            bank = full()
                            done(dve.tensor_tensor(rtmp[:, s * N:(s + 1) * N], bank[:, :], rope[:, 1, :], ALU.mult))
                            npb[0] += 1
                            dve.wait_ge(part_back.sem, part_back.value(l, b, npb[0]))
                            dve.tensor_copy(sp3[0], qf).then_inc(part_rest.sem, 1)
                            npr[0] += 1
                            npb[0] += 1
                            dve.wait_ge(part_back.sem, part_back.value(l, b, npb[0]))
                        else:
                            bank = full()
                            qb = col(l, "qkv", s)
                            step(dve.tensor_scalar(sp3[0], bank[:, :], qb, None, ALU.add))
                            done(dve.scalar_tensor_tensor(out=r_s, in0=bank[:, :], scalar=qb, in1=sp3[0],
                                                          op0=ALU.add, op1=ALU.subtract))
                            dve.wait_ge(dbank_read.sem, dbank_read.value(l, b, d[0]))
                        dve.tensor_copy(sp3[1], r_s).then_inc(part_rest.sem, 1)
                        npr[0] += 1
                bank = full()
                done(dve.tensor_copy(vs[:, :].rearrange("p (t h n) -> p t h n", t=TT, n=VW)[:, :, :, 0:HD],
                                     bank[:, :].rearrange("p (t h n) -> p t h n", t=TT, n=HD)))
                if l == 1:
                    short_attention("win", 0, 0)
                    first_a = 16
                else:
                    for h in range(H):
                        for t in range(TT):
                            bank = full()
                            done(dve.tensor_reduce(mx[:, t * H + h:t * H + h + 1], bank[:, :], AX_X, ALU.max))
                    bank = full()
                    mp = [msplit[:, i * N:(i + 1) * N] for i in range(3)]
                    step(dve.tensor_scalar(mp[0], bank[0:H, :], -1.0, None, ALU.mult))
                    done(dve.scalar_tensor_tensor(out=mrest[:, :], in0=bank[0:H, :], scalar=-1.0, in1=mp[0],
                                                  op0=ALU.mult, op1=ALU.subtract))
                    dve.wait_ge(dbank_read.sem, dbank_read.value(l, b, d[0]))
                    step(dve.tensor_copy(mp[1], mrest[:, :]))
                    dve.tensor_tensor(mp[2], mrest[:, :], mp[1], ALU.subtract).then_inc(m_split.sem, 1)
                    first_a = 32
                out_proj(0, None if l == 3 else col(l, "qkv", 2))
                layernorm(1)
                norm_T(1)
                bank = full()
                if l == 3:
                    done(dve.tensor_copy(qT[:, :], bank[:, :]))
                else:
                    done(dve.tensor_scalar(qT[:, :], bank[:, :], col(l, "qc"), None, ALU.add))
                short_attention(short_kind(l), 16 if l == 1 else 0, first_a)
                first_a += 16
                out_proj(1, None if l == 3 else col(l, "kvc", 1))
                layernorm(2)
                norm_T(2)
                if l == 1:
                    for c in range(4):
                        bank = full()
                        dve.wait_ge(abank_read.sem, abank_read.value(l, b, first_a + c + 1))
                        gc = gact[:, c * N:(c + 1) * N]
                        done(dve.scalar_tensor_tensor(out=gc, in0=bank[:, :], scalar=col(l, "m1", 4 + c), in1=gc,
                                                      op0=ALU.add, op1=ALU.mult))
                residual(2)
                check_count("v", l, nv[0])
                check_count("d", l, d[0])
                check_count("pr", l, npr[0])

            for l in range(LAYERS):
                with dve.Fori(0, B) as b:
                    batch(l, b)


MLP_ACT = [ACT.Gelu_apprx_tanh, ACT.Silu, ACT.Gelu, ACT.Gelu_apprx_tanh]
N_LOADS = 15
NPRO_D = 7
CTX_VAR = 6
NPRO_V = 19
PER = {
    "d": [103, 58, 103, 105],
    "a": [52, 36, 52, 52],
    "pv": [20, 8, 20, 20],
    "ps": [3, 3, 3, 3],
    "pr": [2, 0, 2, 4],
    "pb": [0, 0, 0, 4],
    "sub": [16, 32, 16, 16],
    "v": [31, 107, 31, 29],
}


FIRST_D = {"win": {1: 6}, "topk": {1: 30}, "cross": {0: 79, 2: 79, 3: 81}}


def check_count(name, layer, n):
    if PER[name][layer] != n: print("COUNT", name, layer, n, PER[name][layer], flush=True)


NAMES = [
    dict(mod="W_mod", qkv="W_qkv", proj="W_proj", qc="W_qc", kvc="W_kvc", cproj="W_cproj", m1="W_mlp1", m2="W_mlp2"),
    dict(mod="w_ada", qkv="w_qkv", proj="w_so", qc="w_q", kvc="w_kv", cproj="w_co", m1="w_m1", m2="w_m2"),
    dict(mod="tp_w", qkv=("sa_wq", "sa_wk", "sa_wv"), proj="sa_wo", qc="ca_wq", kvc=("ca_wk", "ca_wv"),
         cproj="ca_wo", m1="w1", m2="w2"),
    dict(mod="adaLN_W", qkv="qkv_W", proj="attn_out_W", qc="cq_W", kvc=("ck_W", "cv_W"), cproj="co_W",
         m1="mlp_W1", m2="mlp_W2"),
]
COL_NAMES = [
    dict(mod="b_mod", qkv="b_qkv", qc="b_qc", kvc="b_kvc", m1="b_mlp1"),
    dict(mod="b_ada", qkv="b_qkv", qc="b_q", kvc="b_kv", m1="b_m1"),
    dict(qkv=("sa_bq", "sa_bk", "sa_bv"), qc="ca_bq", kvc=("ca_bk", "ca_bv"), m1="b1",
         lng=("ln1_g", "ln3_g", "ln2_g"), lnb=("ln1_b", "ln3_b", "ln2_b")),
    dict(mod="adaLN_b", m1="mlp_b1", lng=("norm1_w", "normc_w", "norm2_w")),
]
ROW_NAMES = [("b_proj", "b_cproj", "b_mlp2"), ("b_so", "b_co", "b_m2"), ("sa_bo", "ca_bo", "b2"), (None, None, "mlp_b2")]
GATE_ROWS = ["b_mod", "b_ada", "tp_b", "adaLN_b"]


def lay_out(inputs):
    def get(l, names):
        names = (names,) if isinstance(names, str) else names
        return [np.asarray(inputs[f"L{l}_xcond_{n}"]) for n in names]

    zero = np.zeros(C, np.float32)
    weights, cols, rows = [], [], []
    swap = np.arange(C).reshape(H, 2, HD // 2)[:, ::-1].reshape(C)
    for l in range(LAYERS):
        for name in WIDTHS[l]:
            if name == "rot":
                qkv = get(l, "qkv_W")[0]
                weights += [qkv[:, 0:C][:, swap], qkv[:, C:2 * C][:, swap]]
            elif name == "m2":
                m2 = get(l, NAMES[l][name])[0]
                weights.append(m2.reshape(4, P, C).transpose(1, 0, 2).reshape(P, 4 * C))
            else:
                weights += get(l, NAMES[l][name])
        for name in COLS[l]:
            cols += [v.reshape(-1, P).T for v in get(l, COL_NAMES[l][name])]
        rows += [zero if n is None else get(l, n)[0] for n in ROW_NAMES[l]]
        gb = get(l, GATE_ROWS[l])[0]
        rows += [zero if c is None else gb[c * C:(c + 1) * C] for c in GATE[l]]
    half = N // 2
    inv = 1.0 / 10000.0 ** (np.arange(0, HD, 2, dtype=np.float32) / HD)
    freqs = np.outer(np.arange(half, dtype=np.float32), inv)
    emb = np.concatenate([freqs, freqs], axis=-1)
    sign = np.concatenate([-np.ones(HD // 2), np.ones(HD // 2)]).astype(np.float32)
    cos = np.tile(np.cos(emb).T, (H, 2)).astype(np.float32)
    sin = np.tile((np.sin(emb) * sign).T, (H, 2)).astype(np.float32)
    win = np.arange(P) // WIN
    smask = np.asarray(inputs["mask_SxS_bk0"])
    to_tiles = lambda m: m.reshape(TT, P, N).transpose(1, 0, 2).reshape(P, TT * N)
    x = np.asarray(inputs["x"])
    ctx = np.asarray(inputs["ctx_1024"])
    return {
        "x": x.reshape(B * TT, P, C).transpose(1, 0, 2).reshape(P, B * N),
        "w": np.concatenate(weights, 1),
        "cols": np.concatenate(cols, 1),
        "rows": np.concatenate(rows),
        "ident": np.eye(P, dtype=np.float32),
        "headmask": (np.arange(P)[:, None] // HD == np.arange(H)[None]).astype(np.float32),
        "winbias": np.where(win[:, None] == win[None], 0.0, MASKED).astype(np.float32),
        "condT": np.asarray(inputs["cond_1024"]).T,
        "ctxT": ctx.transpose(2, 0, 1).reshape(P, B * LC),
        "ctok": ctx.transpose(1, 0, 2).reshape(LC, B * C),
        "cmask_i": np.asarray(inputs["mask_BxS2_ik0"]),
        "cmask_iT": np.asarray(inputs["mask_BxS2_ik0"]).T,
        "cmask_u": np.asarray(inputs["mask_BxS2_bf1"]),
        "rope": np.stack([cos, sin], 1),
        "smask": to_tiles(smask),
        "smaskT": to_tiles(np.ascontiguousarray(smask.T)),
    }


def kernel(**inputs):
    import concourse.bacc as bacc
    from concourse.bass_utils import run_bass_kernel_spmd

    nc = bacc.Bacc("TRN2", target_bir_lowering=False, num_devices=1)
    arrays, args = {}, {}
    for name, v in lay_out(inputs).items():
        v = np.ascontiguousarray(v)
        arrays[f"in_{name}"] = v
        args[name] = nc.dram_tensor(f"in_{name}", v.shape, mybir.dt.from_np(v.dtype), kind="ExternalInput").ap()
    out = nc.dram_tensor("out_x", (P, B * N), F32, kind="ExternalOutput").ap()
    build(nc, args, out)
    r = run_bass_kernel_spmd(nc, [arrays], core_ids=[0])
    y = r.results[0]["out_x"]
    return y.reshape(P, B * TT, C).transpose(1, 0, 2).reshape(B, N, C)
```

```python
from contextlib import ExitStack

import numpy as np
import concourse.bass as bass
from concourse import mybir

F32 = mybir.dt.float32
BF16 = mybir.dt.bfloat16
I32 = mybir.dt.int32
U8 = mybir.dt.uint8
ALU = mybir.AluOpType
ACT = mybir.ActivationFunctionType
AX_X = mybir.AxisListType.X

P = 128
B, N, C = 4, 512, 128
H, HD = 16, 8
LC = 77
HG = 4
G = H // HG
TT = N // P
VW = 32
SCALE = float(HD) ** -0.5
MASKED = -float(2 ** 100)
TAKEN = -3.0e38
SHIFT, WIN, TOPK = 32, 64, 16
LAYERS = 4
FULL = (0, 2, 3)

PAIRS = ((0, 0), (0, 1), (1, 0), (0, 2), (2, 0), (1, 1))
STACK_M = 73
STACK = 76

EPS = (1e-6, 1e-6, 1e-5, 1e-5)
NMOD = (6, 9, 3, 9)
HID = 512
WIDTHS = [
    dict(mod=768, qkv=384, proj=128, qc=128, kvc=256, cproj=128, m1=512, m2=512),
    dict(mod=1152, qkv=384, proj=128, qc=128, kvc=256, cproj=128, m1=1024, m2=512),
    dict(mod=384, qkv=384, proj=128, qc=128, kvc=256, cproj=128, m1=512, m2=512),
    dict(mod=1152, qkv=384, rot=256, proj=128, qc=128, kvc=256, cproj=128, m1=512, m2=512),
]
COLS = [
    dict(mod=6, qkv=3, qc=1, kvc=2, m1=4),
    dict(mod=9, qkv=3, qc=1, kvc=2, m1=8),
    dict(qkv=3, qc=1, kvc=2, m1=4, lng=3, lnb=3),
    dict(mod=9, m1=4, lng=3),
]
ROWS = 6
GATE = [(2, None, 5), (2, 5, 8), (0, 1, 2), (2, 5, 8)]
MODS = [((0, 1), None, (3, 4)), ((0, 1), (3, 4), (6, 7)), (None, None, None), ((0, 1), (3, 4), (6, 7))]


def offsets(widths):
    out, at = [], 0
    for layer in widths:
        here = {}
        for name, w in layer.items():
            here[name] = at
            at += w
        out.append(here)
    return out, at


W_AT, W_ALL = offsets(WIDTHS)
C_AT, C_ALL = offsets(COLS)


class Signal:

    def __init__(self, ctx, nc, name, per, start=0, step=1):
        self.sem = ctx.enter_context(nc.semaphore(name))
        self.name, self.per, self.start, self.step = name, per, start, step

    def value(self, layer, b, k):
        fixed = self.start + B * sum(self.per[:layer]) + k
        if isinstance(b, int):
            return self.step * (fixed + b * self.per[layer])
        return b * (self.step * self.per[layer]) + self.step * fixed


def x_steps(layer):
    attention = G * TT + 2
    rest = 3 + 3 + (G * TT + 2) + 3 + 2 + 5
    return 1 + attention, rest


def y_steps(layer):
    return (2, 3) if layer == 1 else (4, 1 + H + 1)


def interleave(nx, ny, share):
    order, done = [], 0
    for i in range(nx):
        while done < ny and done * nx * share <= i * ny:
            order.append("Y")
            done += 1
        order.append("X")
    return order + ["Y"] * (ny - done)


def body_order(x_layer, y_layer):
    xs = x_steps(x_layer) if x_layer is not None else (0, 0)
    ys = y_steps(y_layer) if y_layer is not None else (0, 0)
    first = min(1, xs[0])
    return (["X"] * first + interleave(xs[0] - first, ys[0], 0.9), interleave(xs[1], ys[1], Y_SHARE))


def run(eng, x_stream, y_stream):
    def body(x_at, y_at):
        gx = x_stream(*x_at) if x_at else None
        gy = y_stream(*y_at, x_at) if y_at else None
        for phase in body_order(x_at and x_at[0], y_at and y_at[0]):
            for which in phase:
                next(gx if which == "X" else gy)
        for g in (gx, gy):
            assert g is None or next(g, "end") == "end"

    body(None, (0, 0))
    for l in range(LAYERS):
        with eng.Fori(0, B - 1) as b:
            body((l, b), (l, b + 1))
        body((l, B - 1), (l + 1, 0) if l + 1 < LAYERS else None)


Y_SHARE = 0.8


def build(nc, a, out):
    ctx = ExitStack()
    with ctx:
        def sb(name, shape, dt=F32):
            return ctx.enter_context(nc.sbuf_tensor(name, shape, dt))

        def sem(name):
            return ctx.enter_context(nc.semaphore(name))

        x = sb("x", [P, B * N])
        w = sb("w", [P, W_ALL])
        cols = sb("cols", [P, C_ALL])
        rows = sb("rows", [P, LAYERS * ROWS * C])
        ident = sb("ident", [P, P])
        identb = sb("identb", [P, P], BF16)
        headmask = sb("headmask", [P, H])
        winbias = sb("winbias", [P, P], BF16)
        rope = sb("rope", [P, 2, N])
        ones16 = sb("ones16", [P, H])
        onesrow = sb("onesrow", [1, P], BF16)
        neghalf = sb("neghalf", [P, TT])
        condT = sb("condT", [P, B])
        scondT = sb("scondT", [P, B])
        modc = sb("modc", [P, 9 * B])
        affine = sb("affine", [P, LAYERS * 3 * 2 * B])
        ctxT = sb("ctxT", [P, B * LC])
        zctxT = sb("zctxT", [P, B * LC])
        cmaskc = sb("cmaskc", [LC, B], I32)
        cmaskf = sb("cmaskf", [LC, B])
        cmrow = sb("cmrow", [1, 2 * B * LC], BF16)
        smask = sb("smask", [P, 2 * TT * N], BF16)
        condB = sb("condB", [P, P])
        ctxb = sb("ctxb", [P, LC])
        gate = sb("gate", [P, 3 * C])
        wproj = sb("wproj", [P, C])
        wcproj = sb("wcproj", [P, C])
        wm2 = sb("wm2", [P, 4 * C])
        bias3 = sb("bias3", [P, 3 * C])
        kcT = sb("kcT", [P, LC])
        kblk = sb("kblk", [P, H * LC])
        vc = sb("vc", [LC, H * VW])
        stat = sb("stat", [P, TT * 6])
        mv = sb("mv", [P, TT * 2])
        veps = sb("veps", [P, TT])
        rstd = sb("rstd", [P, TT])
        ystat = sb("ystat", [P, TT * 6])
        ymv = sb("ymv", [P, TT * 2])
        yveps = sb("yveps", [P, TT])
        yrstd = sb("yrstd", [P, TT])
        yz = sb("yz", [P, N])
        yhT = sb("yhT", [P, N])
        qT = sb("qT", [P, N])
        qwin = sb("qwin", [P, N])
        kT = sb("kT", [P, N])
        split = sb("split", [P, 2 * 3 * N], BF16)
        vs = sb("vs", [P, TT * H * VW])
        qstack = sb("qstack", [P, H * N], BF16)
        kstack = sb("kstack", [P, H * N], BF16)
        mx = sb("mx", [P, TT * H])
        pt = sb("pt", [P, 2 * HG * N])
        e = sb("e", [P, 4 * HG * P])
        top = sb("top", [P, 2 * HG * 8])
        top2 = sb("top2", [P, HG * 8])
        mxs = sb("mxs", [P, 4 * HG])
        oe = sb("oe", [P, G * N])
        rden = sb("rden", [P, TT * H])
        on = sb("on", [P, N])
        oT = sb("oT", [P, N])
        gact = sb("gact", [P, 4 * N])

        z, hT = on, oT
        rest = gact[:, 2 * N:4 * N]
        rtmp = gact[:, 0:2 * N]
        msplit = split[0:H, 0:3 * N]
        mrest = split[0:H, 3 * N:5 * N].bitcast(F32)
        kwin = gact[:, 0:2 * HG * P]
        srow = gact[:, 2 * HG * P:2 * HG * (P + LC)]
        spick = gact[:, 0:2 * HG * LC]
        smask_u = gact[:, :].bitcast(U8)[:, 0:2 * TT * N]
        winb32 = yz[:, 0:P]
        ctok = on[0:LC, :]
        cmrow_i = oT[0:1, 0:B * LC].bitcast(I32)
        cmrow_u = yhT[0:1, :].bitcast(U8)[:, 0:B * LC]
        cmtmp = qT[0:1, 0:B * LC]

        ps = [ctx.enter_context(nc.psum_tensor(f"ps{i}", [P, 512], F32)) for i in range(8)]
        psA = [ctx.enter_context(nc.psum_tensor(f"pa{i}", [P, 1024], F32)) for i in range(0)]

        qk_dram = nc.dram_tensor("qk_parts", [2, P, 3, N], BF16, kind="Internal").ap()
        m_dram = nc.dram_tensor("m_parts", [H, 3, N], BF16, kind="Internal").ap()

        def signal(name, per, start=0, step=1):
            return Signal(ctx, nc, name, per, start, step)

        per = PER
        ybank_full = signal("ybank_full", per["yd"], start=NPRO_D)
        ybank_read = signal("ybank_read", per["yd"], start=NPRO_D)
        xbank_full = signal("xbank_full", per["xd"])
        xbank_read = signal("xbank_read", per["xd"], start=1)
        abank_full = signal("abank_full", per["a"])
        abank_read = signal("abank_read", per["a"], start=1)
        pv_done = signal("pv_done", per["pv"])
        obank_read = signal("obank_read", [8] * 4, start=1)
        batch_set = signal("batch_set", [1] * 4)
        z_ready = signal("z_ready", [8] * 4)
        var_ready = signal("var_ready", [2] * 4)
        rstd_ready = signal("rstd_ready", [2] * 4)
        yz_ready = signal("yz_ready", [4] * 4)
        yvar_ready = signal("yvar_ready", [1] * 4)
        yrstd_ready = signal("yrstd_ready", [1] * 4)
        pool_step = signal("pool_step", [2] * 4, start=2)
        ypool_step = signal("ypool_step", [1] * 4)
        gated = signal("gated", [1] * 4)
        kblk_ready = signal("kblk_ready", [1] * 4)
        xbias = signal("xbias", [3] * 4)
        part_rest = signal("part_rest", per["pr"])
        part_back = signal("part_back", per["pb"])
        qk_split = signal("qk_split", [2 if l in FULL else 0 for l in range(4)])
        stack_in = signal("stack_in", [14 if l in FULL else 0 for l in range(4)], step=16)
        m_split = signal("m_split", [1 if l in FULL else 0 for l in range(4)])
        mstack_in = signal("mstack_in", [2 if l in FULL else 0 for l in range(4)], step=16)
        kwin_ready = signal("kwin_ready", [0, 16, 0, 0])
        exp_ready = signal("exp_ready", per["sub"])
        sel_ready = signal("sel_ready", [0, 16, 0, 0])
        vstep = signal("vstep", per["v"], start=NPRO_V)
        yvstep = signal("yvstep", per["yv"])
        ctx_rstd = sem("ctx_rstd")
        loaded = sem("loaded")
        loaded_w = [sem(f"loaded_w{l}") for l in range(LAYERS)]
        silu_done = sem("silu_done")
        stored = sem("stored")

        def wcol(l, name, at=0, n=C):
            o = W_AT[l][name] + at
            return w[:, o:o + n]

        def col(l, name, j=0):
            o = C_AT[l][name] + j
            return cols[:, o:o + 1]

        def rowv(l, j, n=1):
            o = (l * ROWS + j) * C
            return rows[:, o:o + n * C]

        def aff(l, i, which, b):
            o = ((l * 3 + i) * 2 + which) * B
            return affine[:, bass.ds(b + o, 1)]

        def heads(ap, n):
            return ap.rearrange("p (h n) -> p h n", n=n)

        nk_of = {"win": P, "cross": LC, "topk": LC}

        def short_kind(l):
            return "topk" if l == 1 else "cross"

        def wait_apart(eng, sig, value):
            if not isinstance(value, int):
                value = eng.to_reg(value)
            eng.wait_ge(loaded, 16 * N_LOADS)
            eng.wait_ge(sig.sem, value)

        block = ctx.enter_context(nc.Block())

        @block.sync
        def _(sp):
            for dst, src in ((x[:, :], a["x"]), (cols[:, :], a["cols"]),
                             (rows[:, :], a["rows"].partition_broadcast(P)), (ident[:, :], a["ident"]),
                             (headmask[:, :], a["headmask"]), (winb32[:, :], a["winbias"]),
                             (condT[:, :], a["condT"]), (ctxT[:, :], a["ctxT"]), (ctok[:, :], a["ctok"]),
                             (cmaskc[:, :], a["cmask_iT"]),
                             (cmrow_i[:, :], a["cmask_i"].rearrange("(o b) k -> o (b k)", o=1)),
                             (cmrow_u[:, :], a["cmask_u"].rearrange("(o b) k -> o (b k)", o=1)),
                             (rope[:, :, :], a["rope"]), (smask_u[:, 0:TT * N], a["smask"]),
                             (smask_u[:, TT * N:2 * TT * N], a["smaskT"])):
                sp.dma_start(dst, src).then_inc(loaded, 16)
            qk_view = qk_dram.rearrange("s (h d) i t -> s i d h t", d=HD)

            def stacks(l, b, x_at):
                if l not in FULL:
                    return
                k = 0
                for s, stack in ((0, qstack), (1, kstack)):
                    sp.wait_ge(qk_split.sem, qk_split.value(l, b, s + 1))
                    sp.dma_start(qk_dram[s], split[:, s * 3 * N:(s + 1) * 3 * N].rearrange(
                        "p (i t) -> p i t", i=3)).then_inc(stack_in.sem, 16)
                    k += 1
                    sp.wait_ge(stack_in.sem, stack_in.value(l, b, k))
                    if s == 0 and x_at:
                        sp.wait_ge(pv_done.sem, pv_done.value(*x_at, ATT_PV[x_at[0]]))
                    for r, pair in enumerate(PAIRS):
                        sp.dma_start(stack[r * HD:(r + 1) * HD, :].rearrange("d (h t) -> d h t", h=H),
                                     qk_view[s, pair[s]]).then_inc(stack_in.sem, 16)
                        k += 1
                sp.wait_ge(m_split.sem, m_split.value(l, b, 1))
                sp.dma_start(m_dram, msplit.rearrange("h (i t) -> h i t", i=3)).then_inc(mstack_in.sem, 16)
                sp.wait_ge(mstack_in.sem, mstack_in.value(l, b, 1))
                sp.dma_start(qstack[STACK_M:STACK, :].rearrange("i (h t) -> i h t", h=H),
                             m_dram.rearrange("h i t -> i h t")).then_inc(mstack_in.sem, 16)
                wait_apart(sp, mstack_in, mstack_in.value(l, b, 2))

            stacks(0, 0, None)
            for l in range(LAYERS):
                if l in FULL:
                    with sp.Fori(0, B - 1) as b:
                        stacks(l, b + 1, (l, b))
                if l + 1 < LAYERS:
                    stacks(l + 1, 0, (l, B - 1))
            for b in range(B):
                sp.wait_ge(xbank_read.sem, xbank_read.value(3, b, per["xd"][3]))
                sp.dma_start(out[:, b * N:(b + 1) * N], x[:, b * N:(b + 1) * N]).then_inc(stored, 16)
            sp.wait_ge(stored, 16 * B)

        @block.tensor
        def _(pe):
            n_pro = [0]

            def pro_bank():
                if n_pro[0] >= 2:
                    pe.wait_ge(ybank_read.sem, n_pro[0] - 1)
                n_pro[0] += 1
                return ps[6 + (n_pro[0] - 1) % 2]

            pe.wait_ge(loaded, 16 * N_LOADS)
            for b in range(B):
                bank = pro_bank()
                pe.wait_ge(vstep.sem, CTX_VAR + 1)
                pe.transpose(bank[:, 0:LC], ctok[:, b * C:(b + 1) * C], ident[0:LC, 0:LC]).then_inc(ybank_full.sem, 1)
            pe.wait_ge(silu_done, 1)
            for l in (0, 1, 3):
                pe.wait_ge(loaded_w[l], 16)
                bank = pro_bank()
                rhs = condT if l == 3 else scondT
                for j in range(NMOD[l]):
                    mm = pe.matmul(bank[:, j * B:(j + 1) * B], wcol(l, "mod", j * C), rhs[:, :], start=True, stop=True)
                mm.then_inc(ybank_full.sem, 1)
            pe.wait_ge(loaded_w[2], 16)

            def y_stream(l, b, x_at):
                d = [0]

                def ybank():
                    pe.wait_ge(ybank_read.sem, ybank_read.value(l, b, max(d[0] - 1, 0)))
                    d[0] += 1
                    return ps[6 + (d[0] - 1) % 2]

                def filled(mm):
                    mm.then_inc(ybank_full.sem, 1)

                def read_y():
                    pe.wait_ge(ybank_read.sem, ybank_read.value(l, b, d[0]))

                def project(name, s_):
                    bank = ybank()
                    filled(pe.matmul(bank[:, :], wcol(l, name, s_ * C), yhT[:, :], start=True, stop=True))

                yield
                bank = ybank()
                for t in range(TT):
                    pe.wait_ge(yz_ready.sem, yz_ready.value(l, b, t + 1))
                    mm = pe.transpose(bank[:, t * P:(t + 1) * P], yz[:, t * P:(t + 1) * P], ident[:, :])
                filled(mm)
                yield
                read_y()
                for s_ in (0, 1):
                    project("qkv", s_)
                    if l == 3:
                        project("rot", s_)
                    yield
                bank = ybank()
                for t in range(TT):
                    mm = pe.matmul(bank[:, t * C:(t + 1) * C], yhT[:, t * P:(t + 1) * P], wcol(l, "qkv", 2 * C),
                                   start=True, stop=True)
                filled(mm)
                yield
                if l != 1:
                    pe.wait_ge(stack_in.sem, stack_in.value(l, b, 14))
                    for h in range(H):
                        for t in range(TT):
                            bank = ybank()
                            mm = pe.matmul(bank[:, :], qstack[0:STACK_M, h * N + t * P:h * N + (t + 1) * P],
                                           kstack[0:STACK_M, h * N:(h + 1) * N], start=True, stop=l != 3)
                            if l == 3:
                                mm = pe.matmul(bank[:, :], identb[:, :], smask[:, t * N:(t + 1) * N],
                                               start=False, stop=True)
                            filled(mm)
                        yield
                    read_y()
                    bank = ybank()
                    for t in range(TT):
                        mm = pe.transpose(bank[0:H, t * P:(t + 1) * P], mx[:, t * H:(t + 1) * H], ident[:, :])
                    filled(mm)
                    yield
                check_count("yd", l, d[0])

            def x_stream(l, b):
                d, na, pv, o = [0], [0], [0], [0]

                def xbank():
                    pe.wait_ge(xbank_read.sem, xbank_read.value(l, b, max(d[0] - 1, 0)))
                    d[0] += 1
                    return ps[2 + (d[0] - 1) % 2]

                def abank():
                    pe.wait_ge(abank_read.sem, abank_read.value(l, b, max(na[0] - 1, 0)))
                    na[0] += 1
                    return (na[0] - 1) % 2

                def obank():
                    pe.wait_ge(obank_read.sem, obank_read.value(l, b, max(o[0] - 1, 0)))
                    o[0] += 1
                    return ps[4 + (o[0] - 1) % 2]

                def filled(mm):
                    mm.then_inc(xbank_full.sem, 1)

                def read_x():
                    pe.wait_ge(xbank_read.sem, xbank_read.value(l, b, d[0]))

                def norm_T(i):
                    yield
                    bank = xbank()
                    for t in range(TT):
                        pe.wait_ge(z_ready.sem, z_ready.value(l, b, 4 * (i - 1) + t + 1))
                        mm = pe.transpose(bank[:, t * P:(t + 1) * P], z[:, t * P:(t + 1) * P], ident[:, :])
                    filled(mm)
                    yield
                    read_x()

                def out_proj(weight):
                    pe.wait_ge(obank_read.sem, obank_read.value(l, b, o[0]))
                    first_d = d[0]
                    for t in range(TT):
                        bank = xbank()
                        for g in range(G):
                            mm = pe.transpose(bank[:, g * P:(g + 1) * P], oe[:, g * N + t * P:g * N + (t + 1) * P],
                                              ident[:, :])
                        filled(mm)
                    yield
                    bank = xbank()
                    for t in range(TT):
                        pe.wait_ge(xbank_read.sem, xbank_read.value(l, b, first_d + t + 1))
                        mm = pe.transpose(bank[:, t * P:(t + 1) * P], on[:, t * P:(t + 1) * P], ident[:, :])
                    filled(mm)
                    yield
                    read_x()
                    bank = xbank()
                    for t in range(TT):
                        mm = pe.matmul(bank[:, t * C:(t + 1) * C], oT[:, t * P:(t + 1) * P], weight,
                                       start=True, stop=True)
                    filled(mm)
                    yield

                def short_attention(kind, n_sub):
                    nk = nk_of[kind]
                    queries = qwin if kind == "win" else qT
                    lag = 2
                    first_a = na[0]
                    for i in range(G * TT + lag):
                        if i < G * TT:
                            g, t = divmod(i, TT)
                            q = queries[:, t * P:(t + 1) * P]
                            bank = xbank()
                            if kind == "win":
                                pe.wait_ge(kwin_ready.sem, kwin_ready.value(l, b, i + 1))
                                ks = kwin[:, (i % 2) * HG * P:(i % 2 + 1) * HG * P]
                                pe.matmul(bank[:, :], q, ks, start=True, stop=False)
                                mm = pe.matmul(bank[:, :].rearrange("p (h k) -> p h k", h=HG), identb[:, :],
                                               winbias[:, :].unsqueeze(1).broadcast_to([P, HG, P]),
                                               start=False, stop=True)
                            else:
                                masked = l in (2, 3)
                                mm = pe.matmul(bank[:, 0:HG * LC], q, kblk[:, g * HG * LC:(g + 1) * HG * LC],
                                               start=True, stop=not masked)
                                if masked:
                                    mrow = cmrow[:, bass.ds(b * LC + (l - 2) * B * LC, LC)]
                                    mm = pe.matmul(bank[:, 0:HG * LC].rearrange("p (h k) -> p h k", h=HG),
                                                   onesrow[:, :], mrow.unsqueeze(1).broadcast_to([1, HG, LC]),
                                                   start=False, stop=True)
                            filled(mm)
                        j = i - lag
                        if j >= 0:
                            g, t = divmod(j, TT)
                            bank = ps[abank()]
                            if kind == "topk":
                                pe.wait_ge(sel_ready.sem, sel_ready.value(l, b, j + 1))
                            else:
                                pe.wait_ge(exp_ready.sem, exp_ready.value(l, b, n_sub + j + 1))
                            for h in range(HG):
                                ein = e[:, (j % 4) * HG * P + h * nk:(j % 4) * HG * P + (h + 1) * nk]
                                mm = pe.transpose(bank[0:nk, h * P:(h + 1) * P], ein, ident[:, :])
                            mm.then_inc(abank_full.sem, 1)
                            if t == TT - 1:
                                ob = obank()
                                pe.wait_ge(abank_read.sem, abank_read.value(l, b, first_a + j + 1))
                                pb = (g % 2) * HG * N
                                if kind == "win":
                                    for tt in range(TT):
                                        for h in range(HG):
                                            mm = pe.matmul(
                                                ob[h * VW:(h + 1) * VW, tt * P:(tt + 1) * P],
                                                vs[:, (tt * H + g * HG + h) * VW:(tt * H + g * HG + h + 1) * VW],
                                                pt[:, pb + h * N + tt * P:pb + h * N + (tt + 1) * P],
                                                start=True, stop=True)
                                else:
                                    for h in range(HG):
                                        mm = pe.matmul(ob[h * VW:(h + 1) * VW, :],
                                                       vc[:, (g * HG + h) * VW:(g * HG + h + 1) * VW],
                                                       pt[0:LC, pb + h * N:pb + (h + 1) * N], start=True, stop=True)
                                mm.then_inc(pv_done.sem, 1)
                                pv[0] += 1
                        yield

                pe.wait_ge(batch_set.sem, batch_set.value(l, b, 1))
                bank = xbank()
                for i, chunk in enumerate(GATE[l]):
                    if chunk is not None:
                        mm = pe.matmul(bank[:, i * C:(i + 1) * C], condB[:, :], wcol(l, "mod", chunk * C),
                                       start=True, stop=True)
                filled(mm)
                bank = xbank()
                pe.matmul(bank[:, 0:LC], wcol(l, "kvc"), ctxb[:, :], start=True, stop=True)
                filled(pe.matmul(bank[0:LC, P:2 * P], ctxb[:, :], wcol(l, "kvc", C), start=True, stop=True))
                if l != 1:
                    pe.wait_ge(mstack_in.sem, mstack_in.value(l, b, 2))
                yield

                if l == 1:
                    yield from short_attention("win", 0)
                else:
                    n_step = G * TT
                    ob = None
                    for i in range(n_step + 2):
                        if i < n_step:
                            g, kt = divmod(i, TT)
                            for half in range(2):
                                pair = 2 * abank()
                                if i == 0 and half == 1:
                                    read_x()
                                for u in range(2):
                                    h = g * HG + 2 * half + u
                                    mm = pe.matmul(ps[pair + u][:, :],
                                                   kstack[0:STACK, h * N + kt * P:h * N + (kt + 1) * P],
                                                   qstack[0:STACK, h * N:(h + 1) * N], start=True, stop=l != 3)
                                    if l == 3:
                                        mm = pe.matmul(ps[pair + u][:, :], identb[:, :],
                                                       smask[:, (TT + kt) * N:(TT + kt + 1) * N],
                                                       start=False, stop=True)
                                mm.then_inc(abank_full.sem, 1)
                        j = i - 1
                        if 0 <= j < n_step:
                            g, kt = divmod(j, TT)
                            if kt == 0:
                                ob = obank()
                            pe.wait_ge(abank_read.sem, abank_read.value(l, b, 2 * j + 2))
                            for h in range(HG):
                                hh = g * HG + h
                                mm = pe.matmul(ob[h * VW:(h + 1) * VW, :],
                                               vs[:, (kt * H + hh) * VW:(kt * H + hh + 1) * VW],
                                               pt[:, (j % 2) * HG * N + h * N:(j % 2) * HG * N + (h + 1) * N],
                                               start=kt == 0, stop=kt == TT - 1)
                            mm.then_inc(pv_done.sem, 1)
                            pv[0] += 1
                        yield
                pe.wait_ge(gated.sem, gated.value(l, b, 1))
                yield from out_proj(wproj[:, :])

                yield from norm_T(1)
                bank = xbank()
                filled(pe.matmul(bank[:, :], wcol(l, "qc"), hT[:, :], start=True, stop=True))
                yield
                read_x()
                pe.wait_ge(kblk_ready.sem, kblk_ready.value(l, b, 1))
                yield from short_attention(short_kind(l), 16 if l == 1 else 0)
                yield from out_proj(wcproj[:, :])

                yield from norm_T(2)
                first_a = na[0]
                for c in range(4):
                    bank = ps[abank()]
                    pe.matmul(bank[:, :], wcol(l, "m1", c * C), hT[:, :], start=True, stop=True)\
                      .then_inc(abank_full.sem, 1)
                    if l == 1:
                        bank = xbank()
                        filled(pe.matmul(bank[:, :], wcol(l, "m1", HID + c * C), hT[:, :], start=True, stop=True))
                    yield
                if l == 1:
                    read_x()
                else:
                    pe.wait_ge(abank_read.sem, abank_read.value(l, b, first_a + 4))
                bank = xbank()
                for t in range(TT):
                    for c in range(4):
                        mm = pe.matmul(bank[:, t * C:(t + 1) * C], gact[:, c * N + t * P:c * N + (t + 1) * P],
                                       wm2[:, c * C:(c + 1) * C], start=c == 0, stop=c == 3)
                filled(mm)
                yield
                check_count("xd", l, d[0])
                check_count("a", l, na[0])
                check_count("pv", l, pv[0])

            run(pe, x_stream, y_stream)

        @block.scalar
        def _(act):
            for l in range(LAYERS):
                lo = W_AT[l]["mod"]
                hi = lo + sum(WIDTHS[l].values())
                act.dma_start(w[:, lo:hi], a["w"][:, lo:hi]).then_inc(loaded_w[l], 16)
            act.wait_ge(loaded, 16 * N_LOADS)
            act.activation(scondT[:, :], condT[:, :], ACT.Silu).then_inc(silu_done, 1)
            act.sem_inc(abank_read.sem, 1)
            act.sem_inc(obank_read.sem, 1)
            act.sem_inc(xbank_read.sem, 1)

            def x_stream(l, b):
                na, pv, o = [0], [0], [0]

                def full():
                    na[0] += 1
                    act.wait_ge(abank_full.sem, abank_full.value(l, b, na[0]))
                    return (na[0] - 1) % 2

                def copy_out(rolled):
                    g = o[0] % G
                    bank = ps[4 + o[0] % 2]
                    o[0] += 1
                    act.wait_ge(pv_done.sem, pv_done.value(l, b, pv[0]))
                    if rolled:
                        act.activation(oe[:, g * N:g * N + SHIFT], bank[:, N - SHIFT:N], ACT.Copy)
                        act.activation(oe[:, g * N + SHIFT:(g + 1) * N], bank[:, 0:N - SHIFT], ACT.Copy)\
                           .then_inc(obank_read.sem, 1)
                    else:
                        act.activation(oe[:, g * N:(g + 1) * N], bank[:, :], ACT.Copy).then_inc(obank_read.sem, 1)

                def short_attention(kind, n_sub):
                    nk = nk_of[kind]
                    for i in range(G * TT + 2):
                        if i < G * TT:
                            act.wait_ge(xbank_read.sem, xbank_read.value(l, b, FIRST_D[kind][l] + i + 1))
                            ein = e[:, (i % 4) * HG * P:(i % 4) * HG * P + HG * nk]
                            act.activation(ein, ein, ACT.Exp, scale=SCALE).then_inc(exp_ready.sem, 1)
                        j = i - 1
                        if 0 <= j < G * TT:
                            g, t = divmod(j, TT)
                            bank = ps[full()]
                            if t == 0 and pv[0] >= 2:
                                act.wait_ge(pv_done.sem, pv_done.value(l, b, pv[0] - 1))
                            pb = (g % 2) * HG * N
                            dst = pt[0:nk, pb:pb + HG * N].rearrange("k (h q) -> k h q", h=HG)[:, :, t * P:(t + 1) * P]
                            act.activation(dst, bank[0:nk, :].rearrange("k (h q) -> k h q", h=HG), ACT.Copy)\
                               .then_inc(abank_read.sem, 1)
                            if t == TT - 1:
                                pv[0] += 1
                                copy_out(kind == "win")
                        yield

                yield
                if l == 1:
                    yield from short_attention("win", 0)
                else:
                    for i in range(G * TT + 2):
                        if i < G * TT:
                            if i >= 2:
                                act.wait_ge(pv_done.sem, pv_done.value(l, b, i - 1))
                            for half in range(2):
                                pair = 2 * full()
                                o_p = (i % 2) * HG * N + half * 2 * N
                                for u in range(2):
                                    ins = act.activation(pt[:, o_p + u * N:o_p + (u + 1) * N], ps[pair + u][:, :],
                                                         ACT.Exp, scale=SCALE)
                                ins.then_inc(abank_read.sem, 1)
                        if 0 < i <= G * TT and i % TT == 0:
                            pv[0] = i
                            copy_out(False)
                        yield
                for _ in range(6):
                    yield
                yield from short_attention(short_kind(l), 16 if l == 1 else 0)
                for _ in range(5):
                    yield
                for c in range(4):
                    bank = ps[full()]
                    act.activation(gact[:, c * N:(c + 1) * N], bank[:, :], MLP_ACT[l],
                                   bias=col(l, "m1", c)).then_inc(abank_read.sem, 1)
                    yield
                yield

            def y_stream(l, b, x_at):
                for _ in range(sum(y_steps(l))):
                    yield

            run(act, x_stream, y_stream)

        @block.gpsimd
        def _(pool):
            pool.memset(neghalf[:, :], -0.5).then_inc(pool_step.sem, 1)
            pool.wait_ge(loaded, 16 * N_LOADS)
            pool.wait_ge(vstep.sem, CTX_VAR)
            pool.tensor_scalar(veps[0:LC, :], mv[0:LC, 1:2 * B:2], EPS[0], None, ALU.add).then_inc(pool_step.sem, 1)
            pool.wait_ge(pool_step.sem, 2)
            pool.tensor_tensor(rstd[0:LC, :], veps[0:LC, :], neghalf[0:LC, :], ALU.pow).then_inc(ctx_rstd, 1)
            for l in range(LAYERS):
                pool.wait_ge(loaded_w[l], 16)

            def y_stream(l, b, x_at):
                npb, npr = [0], [0]
                wait_apart(pool, yvar_ready, yvar_ready.value(l, b, 1))
                pool.tensor_scalar(yveps[:, :], ymv[:, 1:2 * TT:2], EPS[l], None, ALU.add).then_inc(ypool_step.sem, 1)
                pool.wait_ge(ypool_step.sem, ypool_step.value(l, b, 1))
                pool.tensor_tensor(yrstd[:, :], yveps[:, :], neghalf[:, :], ALU.pow).then_inc(yrstd_ready.sem, 1)
                yield
                yield
                for s_ in range(2):
                    if l != 1:
                        sp3 = [split[:, (s_ * 3 + i) * N:(s_ * 3 + i + 1) * N] for i in range(3)]
                        r_s = rest[:, s_ * N:(s_ + 1) * N]
                        if l == 3:
                            pool.wait_ge(ybank_read.sem, ybank_read.value(l, b, 3 + 2 * s_))
                            qf = (qT, kT)[s_][:, :]
                            pool.tensor_tensor(qf, qf, rtmp[:, s_ * N:(s_ + 1) * N], ALU.add).then_inc(part_back.sem, 1)
                            npb[0] += 1
                            npr[0] += 1
                            pool.wait_ge(part_rest.sem, part_rest.value(l, b, npr[0]))
                            pool.tensor_tensor(r_s, qf, sp3[0], ALU.subtract).then_inc(part_back.sem, 1)
                            npb[0] += 1
                        npr[0] += 1
                        pool.wait_ge(part_rest.sem, part_rest.value(l, b, npr[0]))
                        pool.tensor_tensor(sp3[2], r_s, sp3[1], ALU.subtract).then_inc(qk_split.sem, 1)
                    yield
                for _ in range(y_steps(l)[1] - (2 if l == 1 else 0)):
                    yield
                check_count("pb", l, npb[0])
                check_count("pr", l, npr[0])

            def x_stream(l, b):
                def inverse_root(i):
                    wait_apart(pool, var_ready, var_ready.value(l, b, i))
                    pool.tensor_scalar(veps[:, :], mv[:, 1:2 * TT:2], EPS[l], None, ALU.add).then_inc(pool_step.sem, 1)
                    pool.wait_ge(pool_step.sem, pool_step.value(l, b, i))
                    pool.tensor_tensor(rstd[:, :], veps[:, :], neghalf[:, :], ALU.pow).then_inc(rstd_ready.sem, 1)

                def add_bias(i):
                    if i == 0:
                        wait_apart(pool, yz_ready, yz_ready.value(l, b, 4))
                    else:
                        wait_apart(pool, z_ready, z_ready.value(l, b, 4 * i))
                    xs = x[:, bass.ds(b * N, N)].rearrange("p (t c) -> p t c", t=TT)
                    pool.tensor_tensor(xs, xs, bias3[:, i * C:(i + 1) * C].unsqueeze(1).broadcast_to([P, TT, C]),
                                       ALU.add).then_inc(xbias.sem, 1)

                wait_apart(pool, xbank_read, xbank_read.value(l, b, 1))
                for i, (dst, name) in enumerate(((wproj, "proj"), (wcproj, "cproj"), (wm2, "m2"))):
                    n = 4 if name == "m2" else 1
                    g3 = gate[:, i * C:(i + 1) * C]
                    src = wcol(l, name, 0, n * C)
                    if l == 2 or GATE[l][i] is None:
                        pool.tensor_copy(dst[:, :], src)
                    else:
                        pool.tensor_tensor(dst[:, :].rearrange("p (c n) -> p c n", c=n),
                                           src.rearrange("p (c n) -> p c n", c=n),
                                           g3.unsqueeze(1).broadcast_to([P, n, C]), ALU.mult)
                    if l == 2:
                        last = pool.tensor_tensor(bias3[:, i * C:(i + 1) * C], rowv(l, i), g3, ALU.add)
                    elif GATE[l][i] is None:
                        last = pool.tensor_copy(bias3[:, i * C:(i + 1) * C], rowv(l, i))
                    else:
                        last = pool.tensor_tensor(bias3[:, i * C:(i + 1) * C], rowv(l, i), g3, ALU.mult)
                last.then_inc(gated.sem, 1)
                pool.wait_ge(gated.sem, gated.value(l, b, 1))
                pool.wait_ge(xbank_read.sem, xbank_read.value(l, b, 2))
                pool.tensor_tensor(kblk[:, :].rearrange("p (h k) -> p h k", h=H),
                                   kcT[:, :].unsqueeze(1).broadcast_to([P, H, LC]),
                                   headmask[:, :].unsqueeze(2).broadcast_to([P, H, LC]), ALU.mult)\
                    .then_inc(kblk_ready.sem, 1)
                add_bias(0)
                yield
                for i in range(G * TT + 2):
                    if l == 1 and i < G * TT:
                        g, t = divmod(i, TT)
                        if i >= 2:
                            pool.wait_ge(xbank_full.sem, xbank_full.value(l, b, 2 + i - 1))
                        ks = kwin[:, (i % 2) * HG * P:(i % 2 + 1) * HG * P]
                        pool.tensor_tensor(ks.rearrange("p (h k) -> p h k", h=HG),
                                           kT[:, t * P:(t + 1) * P].unsqueeze(1).broadcast_to([P, HG, P]),
                                           headmask[:, g * HG:(g + 1) * HG].unsqueeze(2).broadcast_to([P, HG, P]),
                                           ALU.mult).then_inc(kwin_ready.sem, 1)
                    yield
                for _ in range(3):
                    yield
                inverse_root(1)
                add_bias(1)
                yield
                for _ in range(2 + G * TT + 2 + 3):
                    yield
                inverse_root(2)
                add_bias(2)
                yield
                for _ in range(1 + 5):
                    yield

            run(pool, x_stream, y_stream)

        @block.vector
        def _(dve):
            n = [0]

            def pstep(ins):
                n[0] += 1
                ins.then_inc(vstep.sem, 1)
                dve.wait_ge(vstep.sem, n[0])

            dve.memset(ones16[:, :], 1.0)
            dve.memset(onesrow[:, :], 1.0)
            dve.memset(qstack[32:64, :], 0.0)
            dve.memset(qstack[64:96, :], 0.0)
            dve.memset(kstack[32:64, :], 0.0)
            dve.memset(kstack[64:96, :], 1.0)
            dve.memset(vs[:, :], 0.0)
            dve.memset(vc[:, :], 0.0)
            pstep(dve.memset(modc[:, :], 0.0))
            dve.memset(vs[:, :].rearrange("p (h n) -> p h n", n=VW)[:, :, HD], 1.0)
            dve.wait_ge(loaded, 16 * N_LOADS)
            dve.tensor_copy(identb[:, :], ident[:, :])
            dve.tensor_copy(winbias[:, :], winb32[:, :])
            dve.tensor_scalar(cmaskf[:, :], cmaskc[:, :], 0.0, None, ALU.not_equal)
            pstep(dve.tensor_scalar(cmtmp[:, :], cmrow_i[:, :], 0.0, None, ALU.not_equal))
            pstep(dve.tensor_scalar(cmrow[:, 0:B * LC], cmtmp[:, :], 1.0, -MASKED, ALU.subtract, ALU.mult))
            dve.tensor_scalar(cmrow[:, B * LC:2 * B * LC], cmrow_u[:, :], 1.0, -MASKED, ALU.subtract, ALU.mult)
            pstep(dve.tensor_scalar(smask[:, :], smask_u[:, :], 1.0, -MASKED, ALU.subtract, ALU.mult))
            for b in range(B):
                ins = dve.bn_stats(stat[0:LC, b * 6:(b + 1) * 6], ctok[:, b * C:(b + 1) * C])
            pstep(ins)
            for b in range(B):
                ins = dve.bn_aggr(mv[0:LC, 2 * b:2 * b + 2], stat[0:LC, b * 6:(b + 1) * 6])
            pstep(ins)
            assert n[0] == CTX_VAR
            dve.wait_ge(ctx_rstd, 1)
            for b in range(B):
                tok = ctok[:, b * C:(b + 1) * C]
                ins = dve.tensor_scalar(tok, tok, mv[0:LC, 2 * b:2 * b + 1], rstd[0:LC, b:b + 1],
                                        ALU.subtract, ALU.mult)
            ins.then_inc(vstep.sem, 1)
            n[0] += 1
            for b in range(B):
                dve.wait_ge(ybank_full.sem, b + 1)
                dve.tensor_copy(zctxT[:, b * LC:(b + 1) * LC], ps[6 + b % 2][:, 0:LC]).then_inc(ybank_read.sem, 1)
            dve.memset(affine[:, :], 0.0)
            for l in range(LAYERS):
                k = {0: 4, 1: 5, 3: 6}.get(l)
                if k is not None:
                    dve.wait_ge(ybank_full.sem, k + 1)
                    m = modc[:, 0:NMOD[l] * B].rearrange("p (j b) -> p j b", b=B)
                    o = C_AT[l]["mod"]
                    dve.tensor_tensor(m, ps[6 + k % 2][:, 0:NMOD[l] * B].rearrange("p (j b) -> p j b", b=B),
                                      cols[:, o:o + NMOD[l]].unsqueeze(2).broadcast_to([P, NMOD[l], B]), ALU.add)\
                       .then_inc(ybank_read.sem, 1)
                    dve.wait_ge(ybank_read.sem, k + 1)
                for i in range(3):
                    o = (l * 3 + i) * 2 * B
                    sc, sh = affine[:, o:o + B], affine[:, o + B:o + 2 * B]
                    if l == 2:
                        dve.tensor_copy(sc, col(l, "lng", i).broadcast_to([P, B]))
                        pstep(dve.tensor_copy(sh, col(l, "lnb", i).broadcast_to([P, B])))
                    elif MODS[l][i] is None:
                        pstep(dve.memset(sc, 1.0))
                    else:
                        jsh, jsc = MODS[l][i]
                        dve.tensor_copy(sh, modc[:, jsh * B:(jsh + 1) * B])
                        if l == 3:
                            pstep(dve.tensor_scalar(sc, modc[:, jsc * B:(jsc + 1) * B], 1.0, col(l, "lng", i),
                                                    ALU.add, ALU.mult))
                        else:
                            pstep(dve.tensor_scalar(sc, modc[:, jsc * B:(jsc + 1) * B], 1.0, None, ALU.add))
            dve.wait_ge(silu_done, 1)
            assert n[0] == NPRO_V, n[0]

            def xtile(b, t, nt=1):
                return x[:, bass.ds(b * N + t * C, nt * C)]

            def affine_T(l, b, i, bank, dst):
                sc, sh = aff(l, i, 0, b), aff(l, i, 1, b)
                if l == 1 and i == 0:
                    dve.tensor_scalar(dst[:, N - SHIFT:N], bank[:, 0:SHIFT], sc, sh, ALU.mult, ALU.add)
                    return dve.tensor_scalar(dst[:, 0:N - SHIFT], bank[:, SHIFT:N], sc, sh, ALU.mult, ALU.add)
                return dve.tensor_scalar(dst[:, :], bank[:, :], sc, sh, ALU.mult, ALU.add)

            def y_stream(l, b, x_at):
                d, nv, npr, npb = [0], [0], [0], [0]

                def step(ins, separate=False):
                    nv[0] += 1
                    ins.then_inc(yvstep.sem, 1)
                    if separate:
                        wait_apart(dve, yvstep, yvstep.value(l, b, nv[0]))
                    else:
                        dve.wait_ge(yvstep.sem, yvstep.value(l, b, nv[0]))

                def full():
                    d[0] += 1
                    dve.wait_ge(ybank_full.sem, ybank_full.value(l, b, d[0]))
                    return ps[6 + (d[0] - 1) % 2]

                def done(ins):
                    ins.then_inc(ybank_read.sem, 1)

                if l > 0:
                    wait_apart(dve, xbank_read, xbank_read.value(l - 1, b, per["xd"][l - 1]))
                for t in range(TT):
                    ins = dve.bn_stats(ystat[:, t * 6:(t + 1) * 6], xtile(b, t))
                step(ins, True)
                for t in range(TT):
                    ins = dve.bn_aggr(ymv[:, 2 * t:2 * t + 2], ystat[:, t * 6:(t + 1) * 6])
                ins.then_inc(yvar_ready.sem, 1)
                yield
                dve.wait_ge(yrstd_ready.sem, yrstd_ready.value(l, b, 1))
                for t in range(TT):
                    dve.tensor_scalar(yz[:, t * P:(t + 1) * P], xtile(b, t), ymv[:, 2 * t:2 * t + 1],
                                      yrstd[:, t:t + 1], ALU.subtract, ALU.mult).then_inc(yz_ready.sem, 1)
                bank = full()
                done(affine_T(l, b, 0, bank, yhT))
                yield
                for s_ in range(2):
                    if l == 1:
                        bank = full()
                        if x_at and x_at[0] == 1:
                            dve.wait_ge(pv_done.sem, pv_done.value(*x_at, ATT_PV[1]))
                        done(dve.tensor_scalar((qwin, kT)[s_][:, :], bank[:, :], col(l, "qkv", s_), None, ALU.add))
                        yield
                        continue
                    sp3 = [split[:, (s_ * 3 + i) * N:(s_ * 3 + i + 1) * N] for i in range(3)]
                    r_s = rest[:, s_ * N:(s_ + 1) * N]
                    if l == 3:
                        qf = (qT, kT)[s_][:, :]
                        bank = full()
                        done(dve.tensor_tensor(qf, bank[:, :], rope[:, 0, :], ALU.mult))
                        bank = full()
                        done(dve.tensor_tensor(rtmp[:, s_ * N:(s_ + 1) * N], bank[:, :], rope[:, 1, :], ALU.mult))
                        npb[0] += 1
                        dve.wait_ge(part_back.sem, part_back.value(l, b, npb[0]))
                        dve.tensor_copy(sp3[0], qf).then_inc(part_rest.sem, 1)
                        npr[0] += 1
                        npb[0] += 1
                        dve.wait_ge(part_back.sem, part_back.value(l, b, npb[0]))
                    else:
                        bank = full()
                        qb = col(l, "qkv", s_)
                        step(dve.tensor_scalar(sp3[0], bank[:, :], qb, None, ALU.add))
                        done(dve.scalar_tensor_tensor(out=r_s, in0=bank[:, :], scalar=qb, in1=sp3[0],
                                                      op0=ALU.add, op1=ALU.subtract))
                        dve.wait_ge(ybank_read.sem, ybank_read.value(l, b, d[0]))
                    dve.tensor_copy(sp3[1], r_s).then_inc(part_rest.sem, 1)
                    npr[0] += 1
                    yield
                bank = full()
                if x_at:
                    dve.wait_ge(pv_done.sem, pv_done.value(*x_at, ATT_PV[x_at[0]]))
                if l != 1:
                    dve.wait_ge(qk_split.sem, qk_split.value(l, b, 2))
                done(dve.tensor_copy(vs[:, :].rearrange("p (t h n) -> p t h n", t=TT, n=VW)[:, :, :, 0:HD],
                                     bank[:, :].rearrange("p (t h n) -> p t h n", t=TT, n=HD)))
                yield
                if l != 1:
                    for h in range(H):
                        for t in range(TT):
                            bank = full()
                            done(dve.tensor_reduce(mx[:, t * H + h:t * H + h + 1], bank[:, :], AX_X, ALU.max))
                        yield
                    bank = full()
                    mp = [msplit[:, i * N:(i + 1) * N] for i in range(3)]
                    step(dve.tensor_scalar(mp[0], bank[0:H, :], -1.0, None, ALU.mult))
                    done(dve.scalar_tensor_tensor(out=mrest, in0=bank[0:H, :], scalar=-1.0, in1=mp[0],
                                                  op0=ALU.mult, op1=ALU.subtract))
                    dve.wait_ge(ybank_read.sem, ybank_read.value(l, b, d[0]))
                    step(dve.tensor_copy(mp[1], mrest))
                    dve.tensor_tensor(mp[2], mrest, mp[1], ALU.subtract).then_inc(m_split.sem, 1)
                    yield
                check_count("yd", l, d[0])
                check_count("yv", l, nv[0])

            def x_stream(l, b):
                d, nv = [0], [0]

                def step(ins, separate=False):
                    nv[0] += 1
                    ins.then_inc(vstep.sem, 1)
                    if separate:
                        wait_apart(dve, vstep, vstep.value(l, b, nv[0]))
                    else:
                        dve.wait_ge(vstep.sem, vstep.value(l, b, nv[0]))

                def full():
                    d[0] += 1
                    dve.wait_ge(xbank_full.sem, xbank_full.value(l, b, d[0]))
                    return ps[2 + (d[0] - 1) % 2]

                def done(ins):
                    ins.then_inc(xbank_read.sem, 1)

                def norm_T(i):
                    for t in range(TT):
                        ins = dve.bn_stats(stat[:, t * 6:(t + 1) * 6], xtile(b, t))
                    step(ins, True)
                    for t in range(TT):
                        ins = dve.bn_aggr(mv[:, 2 * t:2 * t + 2], stat[:, t * 6:(t + 1) * 6])
                    ins.then_inc(var_ready.sem, 1)
                    yield
                    dve.wait_ge(rstd_ready.sem, rstd_ready.value(l, b, i))
                    for t in range(TT):
                        dve.tensor_scalar(z[:, t * P:(t + 1) * P], xtile(b, t), mv[:, 2 * t:2 * t + 1],
                                          rstd[:, t:t + 1], ALU.subtract, ALU.mult).then_inc(z_ready.sem, 1)
                    bank = full()
                    done(affine_T(l, b, i, bank, hT))
                    yield

                def out_proj(i, vbias):
                    for t in range(TT):
                        bank = full()
                        o4 = bank[:, :].rearrange("p (h n) -> p h n", n=VW)
                        rd = rden[:, t * H:(t + 1) * H]
                        step(dve.reciprocal(rd, o4[:, :, HD]))
                        done(dve.tensor_tensor(on[:, t * P:(t + 1) * P].rearrange("p (h n) -> p h n", n=HD),
                                               o4[:, :, 0:HD], rd.unsqueeze(2).broadcast_to([P, H, HD]), ALU.mult))
                    yield
                    bank = full()
                    if vbias is None:
                        done(dve.tensor_copy(oT[:, :], bank[:, :]))
                    else:
                        done(dve.tensor_scalar(oT[:, :], bank[:, :], vbias, None, ALU.add))
                    yield
                    residual(i)
                    yield

                def residual(i):
                    bank = full()
                    dve.wait_ge(xbias.sem, xbias.value(l, b, i + 1))
                    done(dve.tensor_tensor(xtile(b, 0, TT), bank[:, :], xtile(b, 0, TT), ALU.add))
                    wait_apart(dve, xbank_read, xbank_read.value(l, b, d[0]))

                def short_attention(kind, n_sub, first_a):
                    nk = nk_of[kind]
                    assert d[0] == FIRST_D[kind][l], (kind, l, d[0])
                    for i in range(G * TT + 2):
                        if i < G * TT:
                            bank = full()
                            s4 = bank[:, 0:HG * nk].rearrange("p (h k) -> p h k", h=HG)
                            e4 = e[:, (i % 4) * HG * P:(i % 4) * HG * P + HG * nk].rearrange("p (h k) -> p h k", h=HG)
                            if kind == "topk":
                                sr = srow[:, (i % 2) * HG * LC:(i % 2 + 1) * HG * LC]
                                sp_ = spick[:, (i % 2) * HG * LC:(i % 2 + 1) * HG * LC]
                                tp = top[:, (i % 2) * HG * 8:(i % 2 + 1) * HG * 8]
                                step(dve.tensor_copy(sr, bank[:, 0:HG * LC]), True)
                                for rnd in range(TOPK // 8):
                                    src = sr if rnd == 0 else sp_
                                    best = tp if rnd == 0 else top2[:, :]
                                    for h in range(HG):
                                        ins = dve.max(best[:, h * 8:(h + 1) * 8], src[:, h * LC:(h + 1) * LC])
                                    step(ins, True)
                                    for h in range(HG):
                                        ins = dve.match_replace(sp_[:, h * LC:(h + 1) * LC], best[:, h * 8:(h + 1) * 8],
                                                                src[:, h * LC:(h + 1) * LC], TAKEN)
                                    step(ins, True)
                                m4 = tp[:, 0:HG * 8:8]
                            else:
                                m4 = mxs[:, (i % 4) * HG:(i % 4 + 1) * HG]
                                step(dve.tensor_reduce(m4, s4, AX_X, ALU.max))
                            if i >= 4:
                                dve.wait_ge(abank_full.sem, abank_full.value(l, b, first_a + i - 3))
                            done(dve.tensor_tensor(e4, s4, m4.unsqueeze(2).broadcast_to([P, HG, nk]), ALU.subtract))
                        j = i - 1
                        if kind == "topk" and 0 <= j < G * TT:
                            dve.wait_ge(exp_ready.sem, exp_ready.value(l, b, n_sub + j + 1))
                            ej = e[:, (j % 4) * HG * P:(j % 4) * HG * P + HG * nk]
                            dve.scalar_tensor_tensor(out=ej, in0=spick[:, (j % 2) * HG * LC:(j % 2 + 1) * HG * LC],
                                                     scalar=TAKEN, in1=ej, op0=ALU.is_le, op1=ALU.mult)\
                               .then_inc(sel_ready.sem, 1)
                        yield

                src = condT if l == 3 else scondT
                dve.tensor_copy(condB[:, :], src[:, bass.ds(b, 1)].broadcast_to([P, P]))
                src = zctxT if l == 0 else ctxT
                dve.tensor_copy(ctxb[:, :], src[:, bass.ds(b * LC, LC)]).then_inc(batch_set.sem, 1)
                bank = full()
                if l == 0:
                    dve.tensor_tensor(gate[:, 0:C], bank[:, 0:C], rowv(l, 3), ALU.add)
                    done(dve.tensor_tensor(gate[:, 2 * C:3 * C], bank[:, 2 * C:3 * C], rowv(l, 5), ALU.add))
                else:
                    done(dve.tensor_tensor(gate[:, :], bank[:, 0:3 * C], rowv(l, 3, 3), ALU.add))
                bank = full()
                if l == 3:
                    dve.tensor_copy(kcT[:, :], bank[:, 0:LC])
                else:
                    dve.tensor_scalar(kcT[:, :], bank[:, 0:LC], col(l, "kvc", 0), None, ALU.add)
                v3 = vc[:, :].rearrange("p (h n) -> p h n", n=VW)
                src = bank[0:LC, P:2 * P].rearrange("p (h n) -> p h n", n=HD)
                if l == 2:
                    mk = cmaskf[:, bass.ds(b, 1)]
                    dve.tensor_scalar(v3[:, :, HD], ones16[0:LC, :], mk, None, ALU.mult)
                    done(dve.tensor_scalar(v3[:, :, 0:HD], src, mk, None, ALU.mult))
                else:
                    dve.tensor_copy(v3[:, :, HD], ones16[0:LC, :])
                    done(dve.tensor_copy(v3[:, :, 0:HD], src))
                yield
                if l == 1:
                    yield from short_attention("win", 0, 0)
                    first_a = 16
                else:
                    for _ in range(G * TT + 2):
                        yield
                    first_a = 32
                yield from out_proj(0, None if l == 3 else col(l, "qkv", 2))
                yield from norm_T(1)
                bank = full()
                if l == 3:
                    done(dve.tensor_copy(qT[:, :], bank[:, :]))
                else:
                    done(dve.tensor_scalar(qT[:, :], bank[:, :], col(l, "qc"), None, ALU.add))
                yield
                yield from short_attention(short_kind(l), 16 if l == 1 else 0, first_a)
                first_a += 16
                yield from out_proj(1, None if l == 3 else col(l, "kvc", 1))
                yield from norm_T(2)
                for c in range(4):
                    if l == 1:
                        bank = full()
                        dve.wait_ge(abank_read.sem, abank_read.value(l, b, first_a + c + 1))
                        gc = gact[:, c * N:(c + 1) * N]
                        done(dve.scalar_tensor_tensor(out=gc, in0=bank[:, :], scalar=col(l, "m1", 4 + c), in1=gc,
                                                      op0=ALU.add, op1=ALU.mult))
                    yield
                residual(2)
                yield
                check_count("v", l, nv[0])
                check_count("xd", l, d[0])

            run(dve, x_stream, y_stream)


MLP_ACT = [ACT.Gelu_apprx_tanh, ACT.Silu, ACT.Gelu, ACT.Gelu_apprx_tanh]
N_LOADS = 15
NPRO_D = 7
CTX_VAR = 6
NPRO_V = 19
PER = {
    "yd": [69, 4, 69, 71],
    "xd": [34, 54, 34, 34],
    "a": [52, 36, 52, 52],
    "pv": [20, 8, 20, 20],
    "pr": [2, 0, 2, 4],
    "pb": [0, 0, 0, 4],
    "sub": [16, 32, 16, 16],
    "v": [26, 106, 26, 26],
    "yv": [5, 1, 5, 3],
}
ATT_PV = [16, 4, 16, 16]
FIRST_D = {"win": {1: 2}, "topk": {1: 26}, "cross": {0: 10, 2: 10, 3: 10}}


def check_count(name, layer, n):
    if PER[name][layer] != n: print("COUNT", name, layer, n, PER[name][layer], flush=True)


NAMES = [
    dict(mod="W_mod", qkv="W_qkv", proj="W_proj", qc="W_qc", kvc="W_kvc", cproj="W_cproj", m1="W_mlp1", m2="W_mlp2"),
    dict(mod="w_ada", qkv="w_qkv", proj="w_so", qc="w_q", kvc="w_kv", cproj="w_co", m1="w_m1", m2="w_m2"),
    dict(mod="tp_w", qkv=("sa_wq", "sa_wk", "sa_wv"), proj="sa_wo", qc="ca_wq", kvc=("ca_wk", "ca_wv"),
         cproj="ca_wo", m1="w1", m2="w2"),
    dict(mod="adaLN_W", qkv="qkv_W", proj="attn_out_W", qc="cq_W", kvc=("ck_W", "cv_W"), cproj="co_W",
         m1="mlp_W1", m2="mlp_W2"),
]
COL_NAMES = [
    dict(mod="b_mod", qkv="b_qkv", qc="b_qc", kvc="b_kvc", m1="b_mlp1"),
    dict(mod="b_ada", qkv="b_qkv", qc="b_q", kvc="b_kv", m1="b_m1"),
    dict(qkv=("sa_bq", "sa_bk", "sa_bv"), qc="ca_bq", kvc=("ca_bk", "ca_bv"), m1="b1",
         lng=("ln1_g", "ln3_g", "ln2_g"), lnb=("ln1_b", "ln3_b", "ln2_b")),
    dict(mod="adaLN_b", m1="mlp_b1", lng=("norm1_w", "normc_w", "norm2_w")),
]
ROW_NAMES = [("b_proj", "b_cproj", "b_mlp2"), ("b_so", "b_co", "b_m2"), ("sa_bo", "ca_bo", "b2"), (None, None, "mlp_b2")]
GATE_ROWS = ["b_mod", "b_ada", "tp_b", "adaLN_b"]


def lay_out(inputs):
    def get(l, names):
        names = (names,) if isinstance(names, str) else names
        return [np.asarray(inputs[f"L{l}_xcond_{n}"]) for n in names]

    zero = np.zeros(C, np.float32)
    weights, cols, rows = [], [], []
    swap = np.arange(C).reshape(H, 2, HD // 2)[:, ::-1].reshape(C)
    for l in range(LAYERS):
        for name in WIDTHS[l]:
            if name == "rot":
                qkv = get(l, "qkv_W")[0]
                weights += [qkv[:, 0:C][:, swap], qkv[:, C:2 * C][:, swap]]
            elif name == "m2":
                m2 = get(l, NAMES[l][name])[0]
                weights.append(m2.reshape(4, P, C).transpose(1, 0, 2).reshape(P, 4 * C))
            else:
                weights += get(l, NAMES[l][name])
        for name in COLS[l]:
            cols += [v.reshape(-1, P).T for v in get(l, COL_NAMES[l][name])]
        rows += [zero if n is None else get(l, n)[0] for n in ROW_NAMES[l]]
        gb = get(l, GATE_ROWS[l])[0]
        rows += [zero if c is None else gb[c * C:(c + 1) * C] for c in GATE[l]]
    half = N // 2
    inv = 1.0 / 10000.0 ** (np.arange(0, HD, 2, dtype=np.float32) / HD)
    freqs = np.outer(np.arange(half, dtype=np.float32), inv)
    emb = np.concatenate([freqs, freqs], axis=-1)
    sign = np.concatenate([-np.ones(HD // 2), np.ones(HD // 2)]).astype(np.float32)
    cos = np.tile(np.cos(emb).T, (H, 2)).astype(np.float32)
    sin = np.tile((np.sin(emb) * sign).T, (H, 2)).astype(np.float32)
    win = np.arange(P) // WIN
    smask = np.asarray(inputs["mask_SxS_bk0"])
    to_tiles = lambda m: m.reshape(TT, P, N).transpose(1, 0, 2).reshape(P, TT * N)
    x = np.asarray(inputs["x"])
    ctx = np.asarray(inputs["ctx_1024"])
    return {
        "x": x.reshape(B * TT, P, C).transpose(1, 0, 2).reshape(P, B * N),
        "w": np.concatenate(weights, 1),
        "cols": np.concatenate(cols, 1),
        "rows": np.concatenate(rows),
        "ident": np.eye(P, dtype=np.float32),
        "headmask": (np.arange(P)[:, None] // HD == np.arange(H)[None]).astype(np.float32),
        "winbias": np.where(win[:, None] == win[None], 0.0, MASKED).astype(np.float32),
        "condT": np.asarray(inputs["cond_1024"]).T,
        "ctxT": ctx.transpose(2, 0, 1).reshape(P, B * LC),
        "ctok": ctx.transpose(1, 0, 2).reshape(LC, B * C),
        "cmask_i": np.asarray(inputs["mask_BxS2_ik0"]),
        "cmask_iT": np.asarray(inputs["mask_BxS2_ik0"]).T,
        "cmask_u": np.asarray(inputs["mask_BxS2_bf1"]),
        "rope": np.stack([cos, sin], 1),
        "smask": to_tiles(smask),
        "smaskT": to_tiles(np.ascontiguousarray(smask.T)),
    }


def kernel(**inputs):
    import concourse.bacc as bacc
    from concourse.bass_utils import run_bass_kernel_spmd

    nc = bacc.Bacc("TRN2", target_bir_lowering=False, num_devices=1)
    arrays, args = {}, {}
    for name, v in lay_out(inputs).items():
        v = np.ascontiguousarray(v)
        arrays[f"in_{name}"] = v
        args[name] = nc.dram_tensor(f"in_{name}", v.shape, mybir.dt.from_np(v.dtype), kind="ExternalInput").ap()
    out = nc.dram_tensor("out_x", (P, B * N), F32, kind="ExternalOutput").ap()
    build(nc, args, out)
    r = run_bass_kernel_spmd(nc, [arrays], core_ids=[0])
    y = r.results[0]["out_x"]
    return y.reshape(P, B * TT, C).transpose(1, 0, 2).reshape(B, N, C)
```

```python
from contextlib import ExitStack

import numpy as np
import concourse.bass as bass
from concourse import mybir

F32 = mybir.dt.float32
BF16 = mybir.dt.bfloat16
I32 = mybir.dt.int32
U8 = mybir.dt.uint8
ALU = mybir.AluOpType
ACT = mybir.ActivationFunctionType
AX_X = mybir.AxisListType.X

P = 128
B, N, C = 4, 512, 128
H, HD = 16, 8
LC = 77
HG = 4
G = H // HG
TT = N // P
VW = 32
SCALE = float(HD) ** -0.5
MASKED = -float(2 ** 100)
TAKEN = -3.0e38
SHIFT, WIN, TOPK = 32, 64, 16
LAYERS = 4
FULL = (0, 2, 3)

RUNS = ((0, 1, 2), (1, 2, 1), (3, 3, 0))
STACK_M = 73
STACK = 76

EPS = (1e-6, 1e-6, 1e-5, 1e-5)
NMOD = (6, 9, 3, 9)
HID = 512
WIDTHS = [
    dict(mod=768, qkv=384, proj=128, qc=128, kvc=256, cproj=128, m1=512, m2=512),
    dict(mod=1152, qkv=384, proj=128, qc=128, kvc=256, cproj=128, m1=1024, m2=512),
    dict(mod=384, qkv=384, proj=128, qc=128, kvc=256, cproj=128, m1=512, m2=512),
    dict(mod=1152, qkv=384, rot=256, proj=128, qc=128, kvc=256, cproj=128, m1=512, m2=512),
]
COLS = [
    dict(mod=6, qkv=3, qc=1, kvc=2, m1=4),
    dict(mod=9, qkv=3, qc=1, kvc=2, m1=8),
    dict(qkv=3, qc=1, kvc=2, m1=4, lng=3, lnb=3),
    dict(mod=9, m1=4, lng=3),
]
ROWS = 6
GATE = [(2, None, 5), (2, 5, 8), (0, 1, 2), (2, 5, 8)]
MODS = [((0, 1), None, (3, 4)), ((0, 1), (3, 4), (6, 7)), (None, None, None), ((0, 1), (3, 4), (6, 7))]


def offsets(widths):
    out, at = [], 0
    for layer in widths:
        here = {}
        for name, w in layer.items():
            here[name] = at
            at += w
        out.append(here)
    return out, at


W_AT, W_ALL = offsets(WIDTHS)
C_AT, C_ALL = offsets(COLS)


class Signal:

    def __init__(self, ctx, nc, name, per, start=0, step=1):
        self.sem = ctx.enter_context(nc.semaphore(name))
        self.name, self.per, self.start, self.step = name, per, start, step

    def value(self, layer, b, k):
        fixed = self.start + B * sum(self.per[:layer]) + k
        if isinstance(b, int):
            return self.step * (fixed + b * self.per[layer])
        return b * (self.step * self.per[layer]) + self.step * fixed


def x_steps(layer):
    attention = G * TT + TAIL + 1 if layer == 1 else 4 * (G * TT + 1)
    rest = 1 + 3 + 3 + (G * TT + TAIL + 1) + 3 + 2 + 5
    return 1 + attention, rest


def y_steps(layer):
    return (0, 3) if layer == 1 else (2 + EARLY, 1 + H * TT - EARLY + 1)


def body_order(x_layer, y_layer):
    xs = x_steps(x_layer) if x_layer is not None else (0, 0)
    ys = y_steps(y_layer) if y_layer is not None else (0, 0)
    if y_layer == 1:
        early, late = [], [2, 7, 12]
    else:
        every, first = (2, 5) if x_layer == 1 else (1, FIRST_A)
        early = [1, 3] + [first + i // every for i in range(EARLY)]
        late = LATE
    phases = []
    for nx, places, n in ((xs[0], early, ys[0]), (xs[1], late, ys[1])):
        places, order = list(places[:n]), []
        for i in range(nx):
            while places and places[0] <= i:
                order.append("Y")
                places.pop(0)
            order.append("X")
        phases.append(order + ["Y"] * len(places))
    for back in HEAD:
        at = len(phases[1]) - back
        phases[1].insert(max(at, 0) if xs[1] else len(phases[1]), "H")
    return phases


def run(eng, x_stream, y_head, y_stream, second_prologue):
    def body(x_at, y_at, next_at):
        streams = {"X": x_at and x_stream(*x_at), "Y": y_at and y_stream(*y_at, x_at),
                   "H": next_at and y_head(*next_at)}
        for phase in body_order(x_at and x_at[0], y_at and y_at[0]):
            for which in phase:
                if streams[which]:
                    next(streams[which])
        assert all(g is None or next(g, "end") == "end" for g in streams.values())

    def at(l, b):
        l, b = l + b // B, b % B
        return (l, b) if l < LAYERS else None

    body(None, None, (0, 0))
    body(None, (0, 0), (0, 1))
    second_prologue()
    for l in range(LAYERS):
        with eng.Fori(0, B - 2) as b:
            body((l, b), (l, b + 1), (l, b + 2))
        for b in (B - 2, B - 1):
            body((l, b), at(l, b + 1), at(l, b + 2))


EARLY = 36
FIRST_A = 30
LATE = [1] + [5, 5, 6] + list(range(8, 8 + H * TT - EARLY - 3)) + [33]
HEAD = (5, 1)
LOADS = 4
LAG = 3
ACT_LAG = 2
TAIL = LAG + 1


def build(nc, a, out):
    ctx = ExitStack()
    with ctx:
        def sb(name, shape, dt=F32):
            return ctx.enter_context(nc.sbuf_tensor(name, shape, dt))

        def sem(name):
            return ctx.enter_context(nc.semaphore(name))

        x = sb("x", [P, B * N])
        w = sb("w", [P, W_ALL])
        cols = sb("cols", [P, C_ALL])
        rows = sb("rows", [P, LAYERS * ROWS * C])
        ident = sb("ident", [P, P])
        identb = sb("identb", [P, P], BF16)
        headmask = sb("headmask", [P, H])
        winbias = sb("winbias", [P, P], BF16)
        rope = sb("rope", [P, 2, N])
        ones16 = sb("ones16", [P, H])
        onesrow = sb("onesrow", [1, P], BF16)
        neghalf = sb("neghalf", [P, TT])
        condT = sb("condT", [P, B])
        scondT = sb("scondT", [P, B])
        modc = sb("modc", [P, 9 * B])
        affine = sb("affine", [P, LAYERS * 3 * 2 * B])
        ctxT = sb("ctxT", [P, B * LC])
        zctxT = sb("zctxT", [P, B * LC])
        cmaskc = sb("cmaskc", [LC, B], I32)
        cmaskf = sb("cmaskf", [LC, B])
        cmrow = sb("cmrow", [1, 2 * B * LC], BF16)
        smask = sb("smask", [P, 2 * TT * N], BF16)
        condB = sb("condB", [P, P])
        ctxb = sb("ctxb", [P, LC])
        gate = sb("gate", [P, 3 * C])
        wproj = sb("wproj", [P, C])
        wcproj = sb("wcproj", [P, C])
        wm2 = sb("wm2", [P, 4 * C])
        bias3 = sb("bias3", [P, 3 * C])
        kcT = sb("kcT", [P, LC])
        kblk = sb("kblk", [P, H * LC])
        vc = sb("vc", [LC, H * VW])
        stat = sb("stat", [P, TT * 6])
        mv = sb("mv", [P, TT * 2])
        veps = sb("veps", [P, TT])
        rstd = sb("rstd", [P, TT])
        ystat = sb("ystat", [P, TT * 6])
        ymv = sb("ymv", [P, TT * 2])
        yveps = sb("yveps", [P, TT])
        yrstd = sb("yrstd", [P, TT])
        yz = sb("yz", [P, N])
        yhT = sb("yhT", [P, N])
        qT = sb("qT", [P, N])
        qwin = sb("qwin", [P, N])
        kT = sb("kT", [P, N])
        split = sb("split", [P, 2 * 3 * N], BF16)
        vs = sb("vs", [P, TT * H * VW])
        qstack = sb("qstack", [P, H * N], BF16)
        kstack = sb("kstack", [P, H * N], BF16)
        mx = sb("mx", [P, TT * H])
        pt = sb("pt", [P, 2 * HG * N])
        e = sb("e", [P, 4 * HG * P])
        top = sb("top", [P, 2 * HG * 8])
        top2 = sb("top2", [P, HG * 8])
        mxs = sb("mxs", [P, 4 * HG])
        oe = sb("oe", [P, G * N])
        rden = sb("rden", [P, TT * H])
        on = sb("on", [P, N])
        oT = sb("oT", [P, N])
        gact = sb("gact", [P, 4 * N])

        z, hT = on, oT
        rest = gact[:, 2 * N:4 * N]
        rtmp = gact[:, 0:2 * N]
        msplit = split[0:H, 0:3 * N]
        mrest = split[0:H, 3 * N:5 * N].bitcast(F32)
        kwin = gact[:, 0:2 * HG * P]
        srow = gact[:, 0:3 * HG * LC]
        spick = gact[:, 3 * HG * LC:6 * HG * LC]
        smask_u = pt[:, :].bitcast(U8)[:, 0:2 * TT * N]
        winb32 = e[:, 0:P]
        ctok = on[0:LC, :]
        cmrow_i = oT[0:1, 0:B * LC].bitcast(I32)
        cmrow_u = e[0:1, P:P + N].bitcast(U8)[:, 0:B * LC]
        cmtmp = qT[0:1, 0:B * LC]

        pairs = [ctx.enter_context(nc.psum_tensor(f"ps{i}", [P, 2 * N], F32)) for i in range(4)]
        ps = [pairs[i // 2][:, (i % 2) * N:(i % 2 + 1) * N] for i in range(8)]

        qk_dram = nc.dram_tensor("qk_parts", [2, 3, HD, H * N], BF16, kind="Internal").ap()
        m_dram = nc.dram_tensor("m_parts", [H, 3, N], BF16, kind="Internal").ap()

        def signal(name, per, start=0, step=1):
            return Signal(ctx, nc, name, per, start, step)

        per = PER
        ybank_full = signal("ybank_full", per["yd"], start=NPRO_D)
        ybank_read = signal("ybank_read", per["yd"], start=NPRO_D)
        xbank_full = signal("xbank_full", per["xd"])
        xbank_read = signal("xbank_read", per["xd"], start=1)
        abank_full = signal("abank_full", per["a"])
        abank_read = signal("abank_read", per["a"], start=1)
        pv_done = signal("pv_done", per["pv"])
        obank_read = signal("obank_read", [8] * 4, start=1)
        batch_set = signal("batch_set", [1] * 4)
        z_ready = signal("z_ready", [8] * 4)
        var_ready = signal("var_ready", [2] * 4)
        rstd_ready = signal("rstd_ready", [2] * 4)
        yz_ready = signal("yz_ready", [4] * 4)
        yvar_ready = signal("yvar_ready", [1] * 4)
        yrstd_ready = signal("yrstd_ready", [1] * 4)
        pool_step = signal("pool_step", [2] * 4, start=2)
        ypool_step = signal("ypool_step", [1] * 4)
        gated = signal("gated", [3] * 4)
        kblk_ready = signal("kblk_ready", [1] * 4)
        xbias = signal("xbias", [3] * 4)
        part_rest = signal("part_rest", per["pr"])
        part_back = signal("part_back", per["pb"])
        qk_split = signal("qk_split", [2 if l in FULL else 0 for l in range(4)])
        parts_out = signal("parts_out", [6 if l in FULL else 0 for l in range(4)], step=16)
        stack_in = [signal(f"stack_in{i}", [6 if l in FULL else 0 for l in range(4)], step=16)
                    for i in range(LOADS)]
        m_split = signal("m_split", [1 if l in FULL else 0 for l in range(4)])
        mstack_in = signal("mstack_in", [2 if l in FULL else 0 for l in range(4)], step=16)
        kwin_ready = signal("kwin_ready", [0, 16, 0, 0])
        exp_ready = signal("exp_ready", per["sub"])
        top_ready = signal("top_ready", [0, 16, 0, 0])
        picked = signal("picked", [0, 16, 0, 0])
        centred = signal("centred", [0, 16, 0, 0])
        sel_ready = signal("sel_ready", [0, 16, 0, 0])
        vstep = signal("vstep", per["v"], start=NPRO_V)
        yvstep = signal("yvstep", per["yv"])
        ctx_rstd = sem("ctx_rstd")
        mod_full = sem("mod_full")
        mod_read = sem("mod_read")
        loaded_first = sem("loaded_first")
        loaded = sem("loaded")
        loaded_w = [sem(f"loaded_w{l}") for l in range(LAYERS)]
        silu_done = sem("silu_done")
        pads_set = sem("pads_set")
        stored = sem("stored")

        def wcol(l, name, at=0, n=C):
            o = W_AT[l][name] + at
            return w[:, o:o + n]

        def col(l, name, j=0):
            o = C_AT[l][name] + j
            return cols[:, o:o + 1]

        def rowv(l, j, n=1):
            o = (l * ROWS + j) * C
            return rows[:, o:o + n * C]

        def aff(l, i, which, b):
            o = ((l * 3 + i) * 2 + which) * B
            return affine[:, bass.ds(b + o, 1)]

        def heads(ap, n):
            return ap.rearrange("p (h n) -> p h n", n=n)

        nk_of = {"win": P, "cross": LC, "topk": LC}

        def short_kind(l):
            return "topk" if l == 1 else "cross"

        def wait_apart(eng, sig, value):
            if not isinstance(value, int):
                value = eng.to_reg(value)
            eng.wait_ge(loaded_first, 16 * N_FIRST)
            eng.wait_ge(sig.sem, value)

        block = ctx.enter_context(nc.Block())

        @block.sync
        def _(sp):
            for dst, src in ((x[:, 0:N], a["x"][:, 0:N]), (condT[:, :], a["condT"]), (ident[:, :], a["ident"]),
                             (cols[:, :], a["cols"])):
                sp.dma_start(dst, src).then_inc(loaded_first, 16)
            for dst, src in ((ctok[:, :], a["ctok"]), (x[:, N:B * N], a["x"][:, N:B * N]),
                             (headmask[:, :], a["headmask"]), (winb32[:, :], a["winbias"]),
                             (ctxT[:, :], a["ctxT"]),
                             (cmaskc[:, :], a["cmask_iT"]),
                             (cmrow_i[:, :], a["cmask_i"].rearrange("(o b) k -> o (b k)", o=1)),
                             (cmrow_u[:, :], a["cmask_u"].rearrange("(o b) k -> o (b k)", o=1)),
                             (rope[:, :, :], a["rope"]), (smask_u[:, 0:TT * N], a["smask"]),
                             (smask_u[:, TT * N:2 * TT * N], a["smaskT"]),
                             (rows[:, :], a["rows"].partition_broadcast(P))):
                sp.dma_start(dst, src).then_inc(loaded, 16)

            def stacks(l, b, x_at):
                if l not in FULL:
                    return
                for s in range(2):
                    sp.wait_ge(qk_split.sem, qk_split.value(l, b, s + 1))
                    for i in range(3):
                        o = (s * 3 + i) * N
                        sp.dma_start(qk_dram[s, i].rearrange("d (h t) -> h d t", h=H),
                                     split[:, o:o + N]).then_inc(parts_out.sem, 16)
                sp.wait_ge(parts_out.sem, parts_out.value(l, b, 6))
                for part in range(LOADS):
                    if x_at:
                        n = ATT_PV[x_at[0]] * (part + 1) // LOADS if x_at[0] in FULL else 0
                        sp.wait_ge(pv_done.sem, pv_done.value(*x_at, n))
                    c0, c1 = part * H // LOADS * N, (part + 1) * H // LOADS * N
                    for r0, n, kpart in RUNS:
                        sp.dma_start(qstack[r0 * HD:(r0 + n) * HD, c0:c1],
                                     qk_dram[0, 0:n, :, c0:c1].rearrange("i d c -> (i d) c"))\
                          .then_inc(stack_in[part].sem, 16)
                        sp.dma_start(kstack[r0 * HD:(r0 + n) * HD, c0:c1],
                                     qk_dram[1, kpart:kpart + 1, :, c0:c1].broadcast_to([n, HD, c1 - c0]))\
                          .then_inc(stack_in[part].sem, 16)
                sp.wait_ge(m_split.sem, m_split.value(l, b, 1))
                sp.dma_start(m_dram, msplit.rearrange("h (i t) -> h i t", i=3)).then_inc(mstack_in.sem, 16)
                sp.wait_ge(mstack_in.sem, mstack_in.value(l, b, 1))
                sp.dma_start(qstack[STACK_M:STACK, :].rearrange("i (h t) -> i h t", h=H),
                             m_dram.rearrange("h i t -> i h t")).then_inc(mstack_in.sem, 16)
                wait_apart(sp, mstack_in, mstack_in.value(l, b, 2))

            stacks(0, 0, None)
            for l in range(LAYERS):
                if l in FULL:
                    with sp.Fori(0, B - 1) as b:
                        stacks(l, b + 1, (l, b))
                if l + 1 < LAYERS:
                    stacks(l + 1, 0, (l, B - 1))
            for b in range(B):
                sp.wait_ge(xbank_read.sem, xbank_read.value(3, b, per["xd"][3]))
                sp.dma_start(out[:, b * N:(b + 1) * N], x[:, b * N:(b + 1) * N]).then_inc(stored, 16)
            sp.wait_ge(stored, 16 * B)

        @block.tensor
        def _(pe):
            def modulation(l, bank):
                rhs = condT if l == 3 else scondT
                for j in range(NMOD[l]):
                    mm = pe.matmul(bank[:, j * B:(j + 1) * B], wcol(l, "mod", j * C), rhs[:, :], start=True, stop=True)
                return mm

            pe.wait_ge(loaded_first, 16 * N_FIRST)
            pe.wait_ge(silu_done, 1)
            modulation(0, ps[6]).then_inc(ybank_full.sem, 1)

            def second_prologue():
                for i, l in enumerate((1, 3)):
                    pe.wait_ge(loaded_w[l], 16)
                    modulation(l, ps[i]).then_inc(mod_full, 1)
                pe.wait_ge(loaded, 16 * N_LOADS)
                for l in (0, 2):
                    pe.wait_ge(loaded_w[l], 16)
                pe.wait_ge(vstep.sem, CTX_NORM)
                for b in range(B):
                    pe.wait_ge(mod_read, b + 1)
                    pe.transpose(ps[b % 2][:, 0:LC], ctok[:, b * C:(b + 1) * C], ident[0:LC, 0:LC])\
                      .then_inc(mod_full, 1)
                pe.wait_ge(mod_read, 2 + B)

            def y_head(l, b):
                yield
                pe.wait_ge(ybank_read.sem, ybank_read.value(l, b, 0))
                for t in range(TT):
                    pe.wait_ge(yz_ready.sem, yz_ready.value(l, b, t + 1))
                    mm = pe.transpose(ps[6][:, t * P:(t + 1) * P], yz[:, t * P:(t + 1) * P], ident[:, :])
                mm.then_inc(ybank_full.sem, 1)
                yield

            def y_stream(l, b, x_at):
                d = [1]

                def ybank():
                    pe.wait_ge(ybank_read.sem, ybank_read.value(l, b, max(d[0] - 1, 0)))
                    d[0] += 1
                    return ps[6 + (d[0] - 1) % 2]

                def filled(mm):
                    mm.then_inc(ybank_full.sem, 1)

                def read_y():
                    pe.wait_ge(ybank_read.sem, ybank_read.value(l, b, d[0]))

                def project(name, s_):
                    bank = ybank()
                    filled(pe.matmul(bank[:, :], wcol(l, name, s_ * C), yhT[:, :], start=True, stop=True))

                read_y()
                for s_ in (0, 1):
                    project("qkv", s_)
                    if l == 3:
                        project("rot", s_)
                    yield
                def values():
                    bank = ybank()
                    for t in range(TT):
                        mm = pe.matmul(bank[:, t * C:(t + 1) * C], yhT[:, t * P:(t + 1) * P], wcol(l, "qkv", 2 * C),
                                       start=True, stop=True)
                    filled(mm)

                if l == 1:
                    values()
                    yield
                else:
                    for i in range(H * TT):
                        h, t = divmod(i, TT)
                        if i == EARLY:
                            values()
                            yield
                        if i % (H * TT // LOADS) == 0:
                            part = stack_in[i // (H * TT // LOADS)]
                            pe.wait_ge(part.sem, part.value(l, b, 6))
                        bank = ybank()
                        mm = pe.matmul(bank[:, :], qstack[0:STACK_M, h * N + t * P:h * N + (t + 1) * P],
                                       kstack[0:STACK_M, h * N:(h + 1) * N], start=True, stop=True)
                        filled(mm)
                        yield
                    read_y()
                    bank = ybank()
                    for t in range(TT):
                        mm = pe.transpose(bank[0:H, t * P:(t + 1) * P], mx[:, t * H:(t + 1) * H], ident[:, :])
                    filled(mm)
                    yield
                check_count("yd", l, d[0])

            def x_stream(l, b):
                d, na, pv, o = [0], [0], [0], [0]

                def xbank():
                    pe.wait_ge(xbank_read.sem, xbank_read.value(l, b, max(d[0] - 1, 0)))
                    d[0] += 1
                    return ps[2 + (d[0] - 1) % 2]

                def abank():
                    pe.wait_ge(abank_read.sem, abank_read.value(l, b, max(na[0] - 1, 0)))
                    na[0] += 1
                    return (na[0] - 1) % 2

                def obank():
                    pe.wait_ge(obank_read.sem, obank_read.value(l, b, max(o[0] - 1, 0)))
                    o[0] += 1
                    return ps[4 + (o[0] - 1) % 2]

                def filled(mm):
                    mm.then_inc(xbank_full.sem, 1)

                def read_x():
                    pe.wait_ge(xbank_read.sem, xbank_read.value(l, b, d[0]))

                def norm_T(i):
                    yield
                    bank = xbank()
                    for t in range(TT):
                        pe.wait_ge(z_ready.sem, z_ready.value(l, b, 4 * (i - 1) + t + 1))
                        mm = pe.transpose(bank[:, t * P:(t + 1) * P], z[:, t * P:(t + 1) * P], ident[:, :])
                    filled(mm)
                    yield
                    read_x()

                def out_proj(weight):
                    pe.wait_ge(obank_read.sem, obank_read.value(l, b, o[0]))
                    first_d = d[0]
                    for t in range(TT):
                        bank = xbank()
                        for g in range(G):
                            mm = pe.transpose(bank[:, g * P:(g + 1) * P], oe[:, g * N + t * P:g * N + (t + 1) * P],
                                              ident[:, :])
                        filled(mm)
                    yield
                    bank = xbank()
                    for t in range(TT):
                        pe.wait_ge(xbank_read.sem, xbank_read.value(l, b, first_d + t + 1))
                        mm = pe.transpose(bank[:, t * P:(t + 1) * P], on[:, t * P:(t + 1) * P], ident[:, :])
                    filled(mm)
                    yield
                    read_x()
                    bank = xbank()
                    for t in range(TT):
                        mm = pe.matmul(bank[:, t * C:(t + 1) * C], oT[:, t * P:(t + 1) * P], weight,
                                       start=True, stop=True)
                    filled(mm)
                    yield

                def short_attention(kind, n_sub):
                    nk = nk_of[kind]
                    queries = qwin if kind == "win" else qT
                    first_a = na[0]
                    for i in range(G * TT + TAIL + 1):
                        if i < G * TT:
                            g, t = divmod(i, TT)
                            q = queries[:, t * P:(t + 1) * P]
                            bank = xbank()
                            if kind == "win":
                                pe.wait_ge(kwin_ready.sem, kwin_ready.value(l, b, i + 1))
                                ks = kwin[:, (i % 2) * HG * P:(i % 2 + 1) * HG * P]
                                pe.matmul(bank[:, :], q, ks, start=True, stop=False)
                                mm = pe.matmul(bank[:, :].rearrange("p (h k) -> p h k", h=HG), identb[:, :],
                                               winbias[:, :].unsqueeze(1).broadcast_to([P, HG, P]),
                                               start=False, stop=True)
                            else:
                                masked = l in (2, 3)
                                mm = pe.matmul(bank[:, 0:HG * LC], q, kblk[:, g * HG * LC:(g + 1) * HG * LC],
                                               start=True, stop=not masked)
                                if masked:
                                    mrow = cmrow[:, bass.ds(b * LC + (l - 2) * B * LC, LC)]
                                    mm = pe.matmul(bank[:, 0:HG * LC].rearrange("p (h k) -> p h k", h=HG),
                                                   onesrow[:, :], mrow.unsqueeze(1).broadcast_to([1, HG, LC]),
                                                   start=False, stop=True)
                            filled(mm)
                        j = i - LAG
                        if 0 <= j < G * TT:
                            g, t = divmod(j, TT)
                            bank = ps[abank()]
                            if kind == "topk":
                                pe.wait_ge(sel_ready.sem, sel_ready.value(l, b, j + 1))
                            else:
                                pe.wait_ge(exp_ready.sem, exp_ready.value(l, b, n_sub + j + 1))
                            for h in range(HG):
                                ein = e[:, (j % 4) * HG * P + h * nk:(j % 4) * HG * P + (h + 1) * nk]
                                mm = pe.transpose(bank[0:nk, h * P:(h + 1) * P], ein, ident[:, :])
                            mm.then_inc(abank_full.sem, 1)
                        j = i - TAIL
                        if j >= 0 and j % TT == TT - 1:
                            g = j // TT
                            ob = obank()
                            pe.wait_ge(abank_read.sem, abank_read.value(l, b, first_a + j + 1))
                            pb = (g % 2) * HG * N
                            if kind == "win":
                                for tt in range(TT):
                                    for h in range(HG):
                                        mm = pe.matmul(
                                            ob[h * VW:(h + 1) * VW, tt * P:(tt + 1) * P],
                                            vs[:, (tt * H + g * HG + h) * VW:(tt * H + g * HG + h + 1) * VW],
                                            pt[:, pb + h * N + tt * P:pb + h * N + (tt + 1) * P],
                                            start=True, stop=True)
                            else:
                                for h in range(HG):
                                    mm = pe.matmul(ob[h * VW:(h + 1) * VW, :],
                                                   vc[:, (g * HG + h) * VW:(g * HG + h + 1) * VW],
                                                   pt[0:LC, pb + h * N:pb + (h + 1) * N], start=True, stop=True)
                            mm.then_inc(pv_done.sem, 1)
                            pv[0] += 1
                        yield

                if l != 1:
                    pe.wait_ge(mstack_in.sem, mstack_in.value(l, b, 2))
                yield

                if l == 1:
                    yield from short_attention("win", 0)
                else:
                    n_step = G * TT
                    ob = None
                    for i in range(n_step + 1):
                        j = i - 1
                        for half in range(2):
                            if i < n_step:
                                g, kt = divmod(i, TT)
                                pair = 2 * abank()
                                if i == 0 and half == 1:
                                    read_x()
                                for u in range(2):
                                    h = g * HG + 2 * half + u
                                    mm = pe.matmul(ps[pair + u][:, :],
                                                   kstack[0:STACK, h * N + kt * P:h * N + (kt + 1) * P],
                                                   qstack[0:STACK, h * N:(h + 1) * N], start=True, stop=l != 3)
                                    if l == 3:
                                        mm = pe.matmul(ps[pair + u][:, :], identb[:, :],
                                                       smask[:, (TT + kt) * N:(TT + kt + 1) * N],
                                                       start=False, stop=True)
                                mm.then_inc(abank_full.sem, 1)
                            yield
                            if j >= 0 and half == 1:
                                g, kt = divmod(j, TT)
                                if kt == 0:
                                    ob = obank()
                                pe.wait_ge(abank_read.sem, abank_read.value(l, b, 2 * j + 2))
                                for h in range(HG):
                                    hh = g * HG + h
                                    mm = pe.matmul(ob[h * VW:(h + 1) * VW, :],
                                                   vs[:, (kt * H + hh) * VW:(kt * H + hh + 1) * VW],
                                                   pt[:, (j % 2) * HG * N + h * N:(j % 2) * HG * N + (h + 1) * N],
                                                   start=kt == 0, stop=kt == TT - 1)
                                mm.then_inc(pv_done.sem, 1)
                                pv[0] += 1
                            yield
                pe.wait_ge(batch_set.sem, batch_set.value(l, b, 1))
                bank = xbank()
                for i, chunk in enumerate(GATE[l]):
                    if chunk is not None:
                        mm = pe.matmul(bank[:, i * C:(i + 1) * C], condB[:, :], wcol(l, "mod", chunk * C),
                                       start=True, stop=True)
                filled(mm)
                bank = xbank()
                pe.matmul(bank[:, 0:LC], wcol(l, "kvc"), ctxb[:, :], start=True, stop=True)
                filled(pe.matmul(bank[0:LC, P:2 * P], ctxb[:, :], wcol(l, "kvc", C), start=True, stop=True))
                yield
                pe.wait_ge(gated.sem, gated.value(l, b, 1))
                yield from out_proj(wproj[:, :])

                yield from norm_T(1)
                bank = xbank()
                filled(pe.matmul(bank[:, :], wcol(l, "qc"), hT[:, :], start=True, stop=True))
                yield
                read_x()
                pe.wait_ge(kblk_ready.sem, kblk_ready.value(l, b, 1))
                yield from short_attention(short_kind(l), 16 if l == 1 else 0)
                pe.wait_ge(gated.sem, gated.value(l, b, 2))
                yield from out_proj(wcproj[:, :])

                yield from norm_T(2)
                first_a = na[0]
                for c in range(4):
                    bank = ps[abank()]
                    pe.matmul(bank[:, :], wcol(l, "m1", c * C), hT[:, :], start=True, stop=True)\
                      .then_inc(abank_full.sem, 1)
                    if l == 1:
                        bank = xbank()
                        filled(pe.matmul(bank[:, :], wcol(l, "m1", HID + c * C), hT[:, :], start=True, stop=True))
                    yield
                if l == 1:
                    read_x()
                else:
                    pe.wait_ge(abank_read.sem, abank_read.value(l, b, first_a + 4))
                pe.wait_ge(gated.sem, gated.value(l, b, 3))
                bank = xbank()
                for t in range(TT):
                    for c in range(4):
                        mm = pe.matmul(bank[:, t * C:(t + 1) * C], gact[:, c * N + t * P:c * N + (t + 1) * P],
                                       wm2[:, c * C:(c + 1) * C], start=c == 0, stop=c == 3)
                filled(mm)
                yield
                check_count("xd", l, d[0])
                check_count("a", l, na[0])
                check_count("pv", l, pv[0])

            run(pe, x_stream, y_head, y_stream, second_prologue)

        @block.scalar
        def _(act):
            first = W_AT[0]["proj"]
            act.dma_start(w[:, 0:first], a["w"][:, 0:first]).then_inc(loaded_first, 16)
            for l in range(LAYERS):
                lo = W_AT[l]["mod"]
                hi = lo + sum(WIDTHS[l].values())
                lo = max(lo, first)
                act.dma_start(w[:, lo:hi], a["w"][:, lo:hi]).then_inc(loaded_w[l], 16)
            act.wait_ge(loaded_first, 16 * N_FIRST)
            act.activation(scondT[:, :], condT[:, :], ACT.Silu).then_inc(silu_done, 1)

            def second_prologue():
                act.wait_ge(loaded, 16 * N_LOADS)
                act.wait_ge(vstep.sem, NPRO_V)

            act.sem_inc(abank_read.sem, 1)
            act.sem_inc(obank_read.sem, 1)
            act.sem_inc(xbank_read.sem, 1)

            def x_stream(l, b):
                na, pv, o = [0], [0], [0]

                def full():
                    na[0] += 1
                    act.wait_ge(abank_full.sem, abank_full.value(l, b, na[0]))
                    return (na[0] - 1) % 2

                def copy_out(rolled):
                    g = o[0] % G
                    bank = ps[4 + o[0] % 2]
                    o[0] += 1
                    act.wait_ge(pv_done.sem, pv_done.value(l, b, pv[0]))
                    if rolled:
                        act.activation(oe[:, g * N:g * N + SHIFT], bank[:, N - SHIFT:N], ACT.Copy)
                        act.activation(oe[:, g * N + SHIFT:(g + 1) * N], bank[:, 0:N - SHIFT], ACT.Copy)\
                           .then_inc(obank_read.sem, 1)
                    else:
                        act.activation(oe[:, g * N:(g + 1) * N], bank[:, :], ACT.Copy).then_inc(obank_read.sem, 1)

                def short_attention(kind, n_sub):
                    nk = nk_of[kind]
                    first_pv = pv[0]
                    for i in range(G * TT + TAIL + 1):
                        if kind == "topk":
                            if i < G * TT:
                                act.wait_ge(xbank_full.sem, xbank_full.value(l, b, FIRST_D[kind][l] + i + 1))
                                if i >= 3:
                                    act.wait_ge(picked.sem, picked.value(l, b, i - 2))
                                    act.wait_ge(centred.sem, centred.value(l, b, i - 2))
                                act.activation(srow[:, (i % 3) * HG * LC:(i % 3 + 1) * HG * LC],
                                               ps[2 + (FIRST_D[kind][l] + i) % 2][:, 0:HG * LC], ACT.Copy)\
                                   .then_inc(xbank_read.sem, 1)
                            j = i - 1
                            if 0 <= j < G * TT:
                                act.wait_ge(centred.sem, centred.value(l, b, j + 1))
                                ein = e[:, (j % 4) * HG * P:(j % 4) * HG * P + HG * nk]
                                act.activation(ein, ein, ACT.Exp, scale=SCALE).then_inc(exp_ready.sem, 1)
                        elif i < G * TT:
                            act.wait_ge(xbank_read.sem, xbank_read.value(l, b, FIRST_D[kind][l] + i + 1))
                            ein = e[:, (i % 4) * HG * P:(i % 4) * HG * P + HG * nk]
                            act.activation(ein, ein, ACT.Exp, scale=SCALE).then_inc(exp_ready.sem, 1)
                        j = i - (LAG if kind == "topk" else ACT_LAG)
                        if 0 <= j < G * TT:
                            g, t = divmod(j, TT)
                            bank = ps[full()]
                            if t == 0 and g >= 2:
                                act.wait_ge(pv_done.sem, pv_done.value(l, b, first_pv + g - 1))
                            pb = (g % 2) * HG * N
                            dst = pt[0:nk, pb:pb + HG * N].rearrange("k (h q) -> k h q", h=HG)[:, :, t * P:(t + 1) * P]
                            act.activation(dst, bank[0:nk, :].rearrange("k (h q) -> k h q", h=HG), ACT.Copy)\
                               .then_inc(abank_read.sem, 1)
                        j = i - TAIL
                        if j >= 0 and j % TT == TT - 1:
                            pv[0] += 1
                            copy_out(kind == "win")
                        yield

                yield
                if l == 1:
                    yield from short_attention("win", 0)
                else:
                    for i in range(G * TT + 1):
                        if 2 <= i < G * TT:
                            act.wait_ge(pv_done.sem, pv_done.value(l, b, i - 1))
                        for half in range(2):
                            if i < G * TT:
                                pair = full()
                                o_p = (i % 2) * HG * N + half * 2 * N
                                act.activation(pt[:, o_p:o_p + 2 * N], pairs[pair][:, :], ACT.Exp, scale=SCALE)\
                                   .then_inc(abank_read.sem, 1)
                            yield
                            if half == 1 and i > 0 and i % TT == 0:
                                pv[0] = i
                                copy_out(False)
                            yield
                for _ in range(7):
                    yield
                yield from short_attention(short_kind(l), 16 if l == 1 else 0)
                for _ in range(5):
                    yield
                for c in range(4):
                    bank = ps[full()]
                    act.activation(gact[:, c * N:(c + 1) * N], bank[:, :], MLP_ACT[l],
                                   bias=col(l, "m1", c)).then_inc(abank_read.sem, 1)
                    yield
                yield

            def y_head(l, b):
                yield
                yield

            def y_stream(l, b, x_at):
                for _ in range(sum(y_steps(l))):
                    yield

            run(act, x_stream, y_head, y_stream, second_prologue)

        @block.gpsimd
        def _(pool):
            pool.memset(neghalf[:, :], -0.5).then_inc(pool_step.sem, 1)
            pool.wait_ge(pool_step.sem, 1)
            pool.memset(kstack[32:64, :], 0.0).then_inc(pads_set, 1)
            pool.memset(kstack[64:96, :], 1.0).then_inc(pads_set, 1)
            pool.wait_ge(pads_set, 2)

            def second_prologue():
                pool.wait_ge(loaded, 16 * N_LOADS)
                pool.wait_ge(vstep.sem, CTX_VAR)
                pool.tensor_scalar(veps[0:LC, :], mv[0:LC, 1:2 * B:2], EPS[0], None, ALU.add).then_inc(pool_step.sem, 1)
                pool.wait_ge(pool_step.sem, 2)
                pool.tensor_tensor(rstd[0:LC, :], veps[0:LC, :], neghalf[0:LC, :], ALU.pow).then_inc(ctx_rstd, 1)
                for l in range(LAYERS):
                    pool.wait_ge(loaded_w[l], 16)

            def y_head(l, b):
                wait_apart(pool, yvar_ready, yvar_ready.value(l, b, 1))
                pool.tensor_scalar(yveps[:, :], ymv[:, 1:2 * TT:2], EPS[l], None, ALU.add).then_inc(ypool_step.sem, 1)
                pool.wait_ge(ypool_step.sem, ypool_step.value(l, b, 1))
                pool.tensor_tensor(yrstd[:, :], yveps[:, :], neghalf[:, :], ALU.pow).then_inc(yrstd_ready.sem, 1)
                yield
                yield

            def y_stream(l, b, x_at):
                npb, npr = [0], [0]
                for s_ in range(2):
                    if l != 1:
                        sp3 = [split[:, (s_ * 3 + i) * N:(s_ * 3 + i + 1) * N] for i in range(3)]
                        r_s = rest[:, s_ * N:(s_ + 1) * N]
                        if l == 3:
                            pool.wait_ge(ybank_read.sem, ybank_read.value(l, b, 3 + 2 * s_))
                            qf = (qT, kT)[s_][:, :]
                            pool.tensor_tensor(qf, qf, rtmp[:, s_ * N:(s_ + 1) * N], ALU.add).then_inc(part_back.sem, 1)
                            npb[0] += 1
                            npr[0] += 1
                            pool.wait_ge(part_rest.sem, part_rest.value(l, b, npr[0]))
                            pool.tensor_tensor(r_s, qf, sp3[0], ALU.subtract).then_inc(part_back.sem, 1)
                            npb[0] += 1
                        npr[0] += 1
                        pool.wait_ge(part_rest.sem, part_rest.value(l, b, npr[0]))
                        pool.tensor_tensor(sp3[2], r_s, sp3[1], ALU.subtract).then_inc(qk_split.sem, 1)
                    yield
                for _ in range(sum(y_steps(l)) - 2):
                    yield
                check_count("pb", l, npb[0])
                check_count("pr", l, npr[0])

            def x_stream(l, b):
                def inverse_root(i):
                    wait_apart(pool, var_ready, var_ready.value(l, b, i))
                    pool.tensor_scalar(veps[:, :], mv[:, 1:2 * TT:2], EPS[l], None, ALU.add).then_inc(pool_step.sem, 1)
                    pool.wait_ge(pool_step.sem, pool_step.value(l, b, i))
                    pool.tensor_tensor(rstd[:, :], veps[:, :], neghalf[:, :], ALU.pow).then_inc(rstd_ready.sem, 1)

                def add_bias(i):
                    pool.wait_ge(gated.sem, gated.value(l, b, i + 1))
                    if i == 0:
                        wait_apart(pool, yz_ready, yz_ready.value(l, b, 4))
                    else:
                        wait_apart(pool, z_ready, z_ready.value(l, b, 4 * i))
                    xs = x[:, bass.ds(b * N, N)].rearrange("p (t c) -> p t c", t=TT)
                    pool.tensor_tensor(xs, xs, bias3[:, i * C:(i + 1) * C].unsqueeze(1).broadcast_to([P, TT, C]),
                                       ALU.add).then_inc(xbias.sem, 1)

                yield
                if l == 1:
                    wait_apart(pool, ybank_read, ybank_read.value(l, b, 3))
                    wait_apart(pool, xbank_read, xbank_read.value(l, b, 0))
                    for i in range(G * TT + TAIL + 1):
                        if i < G * TT:
                            g, t = divmod(i, TT)
                            if i >= 2:
                                pool.wait_ge(xbank_full.sem, xbank_full.value(l, b, FIRST_D["win"][1] + i - 1))
                            ks = kwin[:, (i % 2) * HG * P:(i % 2 + 1) * HG * P]
                            pool.tensor_tensor(ks.rearrange("p (h k) -> p h k", h=HG),
                                               kT[:, t * P:(t + 1) * P].unsqueeze(1).broadcast_to([P, HG, P]),
                                               headmask[:, g * HG:(g + 1) * HG].unsqueeze(2).broadcast_to([P, HG, P]),
                                               ALU.mult).then_inc(kwin_ready.sem, 1)
                        yield
                else:
                    for _ in range(4 * (G * TT + 1)):
                        yield
                first_d = 16 if l == 1 else 0
                wait_apart(pool, xbank_read, xbank_read.value(l, b, first_d + 1))
                for i, (dst, name) in enumerate(((wproj, "proj"), (wcproj, "cproj"), (wm2, "m2"))):
                    n = 4 if name == "m2" else 1
                    g3 = gate[:, i * C:(i + 1) * C]
                    src = wcol(l, name, 0, n * C)
                    if l == 2 or GATE[l][i] is None:
                        pool.tensor_copy(dst[:, :], src)
                    else:
                        pool.tensor_tensor(dst[:, :].rearrange("p (c n) -> p c n", c=n),
                                           src.rearrange("p (c n) -> p c n", c=n),
                                           g3.unsqueeze(1).broadcast_to([P, n, C]), ALU.mult)
                    if l == 2:
                        last = pool.tensor_tensor(bias3[:, i * C:(i + 1) * C], rowv(l, i), g3, ALU.add)
                    elif GATE[l][i] is None:
                        last = pool.tensor_copy(bias3[:, i * C:(i + 1) * C], rowv(l, i))
                    else:
                        last = pool.tensor_tensor(bias3[:, i * C:(i + 1) * C], rowv(l, i), g3, ALU.mult)
                    last.then_inc(gated.sem, 1)
                    if i == 0:
                        add_bias(0)
                        pool.wait_ge(xbank_read.sem, xbank_read.value(l, b, first_d + 2))
                        pool.tensor_tensor(kblk[:, :].rearrange("p (h k) -> p h k", h=H),
                                           kcT[:, :].unsqueeze(1).broadcast_to([P, H, LC]),
                                           headmask[:, :].unsqueeze(2).broadcast_to([P, H, LC]), ALU.mult)\
                            .then_inc(kblk_ready.sem, 1)
                yield
                for _ in range(3):
                    yield
                inverse_root(1)
                add_bias(1)
                yield
                yield
                yield
                for i in range(G * TT + TAIL + 1):
                    if l == 1 and i < G * TT:
                        wait_apart(pool, top_ready, top_ready.value(l, b, i + 1))
                        if i >= 4:
                            wait_apart(pool, abank_full, abank_full.value(l, b, 16 + i - 3))
                        e4 = e[:, (i % 4) * HG * P:(i % 4) * HG * P + HG * LC].rearrange("p (h k) -> p h k", h=HG)
                        m4 = top[:, (i % 2) * HG * 8:(i % 2 + 1) * HG * 8:8]
                        pool.tensor_tensor(e4, srow[:, (i % 3) * HG * LC:(i % 3 + 1) * HG * LC]
                                           .rearrange("p (h k) -> p h k", h=HG),
                                           m4.unsqueeze(2).broadcast_to([P, HG, LC]), ALU.subtract)\
                            .then_inc(centred.sem, 1)
                    yield
                for _ in range(3):
                    yield
                inverse_root(2)
                add_bias(2)
                yield
                for _ in range(1 + 5):
                    yield

            run(pool, x_stream, y_head, y_stream, second_prologue)

        @block.vector
        def _(dve):
            n = [0]

            def pstep(ins):
                n[0] += 1
                ins.then_inc(vstep.sem, 1)
                dve.wait_ge(vstep.sem, n[0])

            dve.memset(ones16[:, :], 1.0)
            dve.memset(onesrow[:, :], 1.0)
            dve.memset(qstack[32:64, :], 0.0)
            dve.memset(qstack[64:96, :], 0.0)
            dve.memset(vs[:, :], 0.0)
            dve.memset(vc[:, :], 0.0)
            pstep(dve.memset(modc[:, :], 0.0))
            dve.memset(vs[:, :].rearrange("p (h n) -> p h n", n=VW)[:, :, HD], 1.0)
            dve.memset(affine[:, :], 0.0)

            def norms(l, bank=None, full=None, read=None):
                if bank is not None:
                    dve.wait_ge(*full)
                    m = modc[:, 0:NMOD[l] * B].rearrange("p (j b) -> p j b", b=B)
                    o = C_AT[l]["mod"]
                    dve.tensor_tensor(m, bank[:, 0:NMOD[l] * B].rearrange("p (j b) -> p j b", b=B),
                                      cols[:, o:o + NMOD[l]].unsqueeze(2).broadcast_to([P, NMOD[l], B]), ALU.add)\
                       .then_inc(read[0], 1)
                    dve.wait_ge(*read)
                for i in range(3):
                    o = (l * 3 + i) * 2 * B
                    sc, sh = affine[:, o:o + B], affine[:, o + B:o + 2 * B]
                    if l == 2:
                        dve.tensor_copy(sc, col(l, "lng", i).broadcast_to([P, B]))
                        pstep(dve.tensor_copy(sh, col(l, "lnb", i).broadcast_to([P, B])))
                    elif MODS[l][i] is None:
                        pstep(dve.memset(sc, 1.0))
                    else:
                        jsh, jsc = MODS[l][i]
                        dve.tensor_copy(sh, modc[:, jsh * B:(jsh + 1) * B])
                        if l == 3:
                            pstep(dve.tensor_scalar(sc, modc[:, jsc * B:(jsc + 1) * B], 1.0, col(l, "lng", i),
                                                    ALU.add, ALU.mult))
                        else:
                            pstep(dve.tensor_scalar(sc, modc[:, jsc * B:(jsc + 1) * B], 1.0, None, ALU.add))

            dve.wait_ge(loaded_first, 16 * N_FIRST)
            norms(0, ps[6], (ybank_full.sem, 1), (ybank_read.sem, 1))

            def second_prologue():
                dve.wait_ge(loaded, 16 * N_LOADS)
                for b in range(B):
                    ins = dve.bn_stats(stat[0:LC, b * 6:(b + 1) * 6], ctok[:, b * C:(b + 1) * C])
                pstep(ins)
                for b in range(B):
                    ins = dve.bn_aggr(mv[0:LC, 2 * b:2 * b + 2], stat[0:LC, b * 6:(b + 1) * 6])
                pstep(ins)
                assert n[0] == CTX_VAR, n[0]
                dve.wait_ge(ctx_rstd, 1)
                for b in range(B):
                    tok = ctok[:, b * C:(b + 1) * C]
                    ins = dve.tensor_scalar(tok, tok, mv[0:LC, 2 * b:2 * b + 1], rstd[0:LC, b:b + 1],
                                            ALU.subtract, ALU.mult)
                pstep(ins)
                assert n[0] == CTX_NORM, n[0]
                norms(1, ps[0], (mod_full, 1), (mod_read, 1))
                norms(2)
                norms(3, ps[1], (mod_full, 2), (mod_read, 2))
                for b in range(B):
                    dve.wait_ge(mod_full, 2 + b + 1)
                    dve.tensor_copy(zctxT[:, b * LC:(b + 1) * LC], ps[b % 2][:, 0:LC]).then_inc(mod_read, 1)
                dve.tensor_copy(identb[:, :], ident[:, :])
                dve.tensor_copy(winbias[:, :], winb32[:, :])
                dve.tensor_scalar(cmaskf[:, :], cmaskc[:, :], 0.0, None, ALU.not_equal)
                pstep(dve.tensor_scalar(cmtmp[:, :], cmrow_i[:, :], 0.0, None, ALU.not_equal))
                dve.tensor_scalar(cmrow[:, 0:B * LC], cmtmp[:, :], 1.0, -MASKED, ALU.subtract, ALU.mult)
                dve.tensor_scalar(cmrow[:, B * LC:2 * B * LC], cmrow_u[:, :], 1.0, -MASKED, ALU.subtract, ALU.mult)
                pstep(dve.tensor_scalar(smask[:, :], smask_u[:, :], 1.0, -MASKED, ALU.subtract, ALU.mult))
                dve.wait_ge(silu_done, 1)
                assert n[0] == NPRO_V, n[0]

            def xtile(b, t, nt=1):
                return x[:, bass.ds(b * N + t * C, nt * C)]

            def affine_T(l, b, i, bank, dst):
                sc, sh = aff(l, i, 0, b), aff(l, i, 1, b)
                if l == 1 and i == 0:
                    dve.tensor_scalar(dst[:, N - SHIFT:N], bank[:, 0:SHIFT], sc, sh, ALU.mult, ALU.add)
                    return dve.tensor_scalar(dst[:, 0:N - SHIFT], bank[:, SHIFT:N], sc, sh, ALU.mult, ALU.add)
                return dve.tensor_scalar(dst[:, :], bank[:, :], sc, sh, ALU.mult, ALU.add)

            def y_head(l, b):
                if l > 0:
                    wait_apart(dve, xbank_read, xbank_read.value(l - 1, b, per["xd"][l - 1]))
                for t in range(TT):
                    ins = dve.bn_stats(ystat[:, t * 6:(t + 1) * 6], xtile(b, t))
                ins.then_inc(yvstep.sem, 1)
                wait_apart(dve, yvstep, yvstep.value(l, b, 1))
                for t in range(TT):
                    ins = dve.bn_aggr(ymv[:, 2 * t:2 * t + 2], ystat[:, t * 6:(t + 1) * 6])
                ins.then_inc(yvar_ready.sem, 1)
                yield
                dve.wait_ge(yrstd_ready.sem, yrstd_ready.value(l, b, 1))
                for t in range(TT):
                    dve.tensor_scalar(yz[:, t * P:(t + 1) * P], xtile(b, t), ymv[:, 2 * t:2 * t + 1],
                                      yrstd[:, t:t + 1], ALU.subtract, ALU.mult).then_inc(yz_ready.sem, 1)
                dve.wait_ge(ybank_full.sem, ybank_full.value(l, b, 1))
                affine_T(l, b, 0, ps[6], yhT).then_inc(ybank_read.sem, 1)
                yield

            def y_stream(l, b, x_at):
                d, nv, npr, npb = [1], [1], [0], [0]

                def step(ins, separate=False):
                    nv[0] += 1
                    ins.then_inc(yvstep.sem, 1)
                    if separate:
                        wait_apart(dve, yvstep, yvstep.value(l, b, nv[0]))
                    else:
                        dve.wait_ge(yvstep.sem, yvstep.value(l, b, nv[0]))

                def full():
                    d[0] += 1
                    dve.wait_ge(ybank_full.sem, ybank_full.value(l, b, d[0]))
                    return ps[6 + (d[0] - 1) % 2]

                def done(ins):
                    ins.then_inc(ybank_read.sem, 1)

                for s_ in range(2):
                    if l == 1:
                        bank = full()
                        if x_at and x_at[0] == 1:
                            dve.wait_ge(pv_done.sem, pv_done.value(*x_at, ATT_PV[1]))
                        done(dve.tensor_scalar((qwin, kT)[s_][:, :], bank[:, :], col(l, "qkv", s_), None, ALU.add))
                        yield
                        continue
                    sp3 = [split[:, (s_ * 3 + i) * N:(s_ * 3 + i + 1) * N] for i in range(3)]
                    r_s = rest[:, s_ * N:(s_ + 1) * N]
                    if l == 3:
                        qf = (qT, kT)[s_][:, :]
                        bank = full()
                        done(dve.tensor_tensor(qf, bank[:, :], rope[:, 0, :], ALU.mult))
                        bank = full()
                        done(dve.tensor_tensor(rtmp[:, s_ * N:(s_ + 1) * N], bank[:, :], rope[:, 1, :], ALU.mult))
                        npb[0] += 1
                        dve.wait_ge(part_back.sem, part_back.value(l, b, npb[0]))
                        dve.tensor_copy(sp3[0], qf).then_inc(part_rest.sem, 1)
                        npr[0] += 1
                        npb[0] += 1
                        dve.wait_ge(part_back.sem, part_back.value(l, b, npb[0]))
                    else:
                        bank = full()
                        qb = col(l, "qkv", s_)
                        step(dve.tensor_scalar(sp3[0], bank[:, :], qb, None, ALU.add))
                        done(dve.scalar_tensor_tensor(out=r_s, in0=bank[:, :], scalar=qb, in1=sp3[0],
                                                      op0=ALU.add, op1=ALU.subtract))
                        dve.wait_ge(ybank_read.sem, ybank_read.value(l, b, d[0]))
                    dve.tensor_copy(sp3[1], r_s).then_inc(part_rest.sem, 1)
                    npr[0] += 1
                    yield
                def values():
                    bank = full()
                    if x_at:
                        dve.wait_ge(pv_done.sem, pv_done.value(*x_at, ATT_PV[x_at[0]]))
                    done(dve.tensor_copy(vs[:, :].rearrange("p (t h n) -> p t h n", t=TT, n=VW)[:, :, :, 0:HD],
                                         bank[:, :].rearrange("p (t h n) -> p t h n", t=TT, n=HD)))

                if l == 1:
                    values()
                    yield
                else:
                    dve.wait_ge(qk_split.sem, qk_split.value(l, b, 2))
                    for i in range(H * TT):
                        h, t = divmod(i, TT)
                        if i == EARLY:
                            values()
                            yield
                        d[0] += 1
                        bank = ps[6 + (d[0] - 1) % 2]
                        m1 = mx[:, t * H + h:t * H + h + 1]
                        if l == 3:
                            wait_apart(dve, ybank_full, ybank_full.value(l, b, d[0]))
                            done(dve.tensor_tensor_reduce(bank[:, :], bank[:, :], smask[:, t * N:(t + 1) * N],
                                                          1.0, TAKEN, ALU.add, ALU.max, m1))
                        else:
                            dve.wait_ge(ybank_full.sem, ybank_full.value(l, b, d[0]))
                            done(dve.tensor_reduce(m1, bank[:, :], AX_X, ALU.max))
                        yield
                    bank = full()
                    mp = [msplit[:, i * N:(i + 1) * N] for i in range(3)]
                    step(dve.tensor_scalar(mp[0], bank[0:H, :], -1.0, None, ALU.mult))
                    done(dve.scalar_tensor_tensor(out=mrest, in0=bank[0:H, :], scalar=-1.0, in1=mp[0],
                                                  op0=ALU.mult, op1=ALU.subtract))
                    dve.wait_ge(ybank_read.sem, ybank_read.value(l, b, d[0]))
                    step(dve.tensor_copy(mp[1], mrest))
                    dve.tensor_tensor(mp[2], mrest, mp[1], ALU.subtract).then_inc(m_split.sem, 1)
                    yield
                check_count("yd", l, d[0])
                check_count("yv", l, nv[0])

            def x_stream(l, b):
                d, nv = [0], [0]

                def step(ins, separate=False):
                    nv[0] += 1
                    ins.then_inc(vstep.sem, 1)
                    if separate:
                        wait_apart(dve, vstep, vstep.value(l, b, nv[0]))
                    else:
                        dve.wait_ge(vstep.sem, vstep.value(l, b, nv[0]))

                def full():
                    d[0] += 1
                    dve.wait_ge(xbank_full.sem, xbank_full.value(l, b, d[0]))
                    return ps[2 + (d[0] - 1) % 2]

                def done(ins):
                    ins.then_inc(xbank_read.sem, 1)

                def norm_T(i):
                    for t in range(TT):
                        ins = dve.bn_stats(stat[:, t * 6:(t + 1) * 6], xtile(b, t))
                    step(ins, True)
                    for t in range(TT):
                        ins = dve.bn_aggr(mv[:, 2 * t:2 * t + 2], stat[:, t * 6:(t + 1) * 6])
                    ins.then_inc(var_ready.sem, 1)
                    yield
                    dve.wait_ge(rstd_ready.sem, rstd_ready.value(l, b, i))
                    for t in range(TT):
                        dve.tensor_scalar(z[:, t * P:(t + 1) * P], xtile(b, t), mv[:, 2 * t:2 * t + 1],
                                          rstd[:, t:t + 1], ALU.subtract, ALU.mult).then_inc(z_ready.sem, 1)
                    bank = full()
                    done(affine_T(l, b, i, bank, hT))
                    yield

                def out_proj(i, vbias):
                    for t in range(TT):
                        bank = full()
                        o4 = bank[:, :].rearrange("p (h n) -> p h n", n=VW)
                        rd = rden[:, t * H:(t + 1) * H]
                        step(dve.reciprocal(rd, o4[:, :, HD]))
                        done(dve.tensor_tensor(on[:, t * P:(t + 1) * P].rearrange("p (h n) -> p h n", n=HD),
                                               o4[:, :, 0:HD], rd.unsqueeze(2).broadcast_to([P, H, HD]), ALU.mult))
                    yield
                    bank = full()
                    if vbias is None:
                        done(dve.tensor_copy(oT[:, :], bank[:, :]))
                    else:
                        done(dve.tensor_scalar(oT[:, :], bank[:, :], vbias, None, ALU.add))
                    yield
                    residual(i)
                    yield

                def residual(i):
                    bank = full()
                    dve.wait_ge(xbias.sem, xbias.value(l, b, i + 1))
                    done(dve.tensor_tensor(xtile(b, 0, TT), bank[:, :], xtile(b, 0, TT), ALU.add))
                    wait_apart(dve, xbank_read, xbank_read.value(l, b, d[0]))

                def short_attention(kind, n_sub, first_a):
                    nk = nk_of[kind]
                    assert d[0] == FIRST_D[kind][l], (kind, l, d[0])
                    if kind == "topk":
                        yield from top_k(n_sub)
                        return
                    for i in range(G * TT + TAIL + 1):
                        if i < G * TT:
                            bank = full()
                            s4 = bank[:, 0:HG * nk].rearrange("p (h k) -> p h k", h=HG)
                            e4 = e[:, (i % 4) * HG * P:(i % 4) * HG * P + HG * nk].rearrange("p (h k) -> p h k", h=HG)
                            m4 = mxs[:, (i % 4) * HG:(i % 4 + 1) * HG]
                            step(dve.tensor_reduce(m4, s4, AX_X, ALU.max))
                            if i >= 4:
                                dve.wait_ge(abank_full.sem, abank_full.value(l, b, first_a + i - 3))
                            done(dve.tensor_tensor(e4, s4, m4.unsqueeze(2).broadcast_to([P, HG, nk]), ALU.subtract))
                        yield

                def top_k(n_sub):
                    def mine(ins):
                        nv[0] += 1
                        ins.then_inc(vstep.sem, 1)
                        return nv[0]

                    marked = None
                    for i in range(G * TT + TAIL + 1):
                        sr = srow[:, (i % 3) * HG * LC:(i % 3 + 1) * HG * LC]
                        sp_ = spick[:, (i % 3) * HG * LC:(i % 3 + 1) * HG * LC]
                        tp = top[:, (i % 2) * HG * 8:(i % 2 + 1) * HG * 8]
                        last = spick[:, ((i - 1) % 3) * HG * LC:((i - 1) % 3 + 1) * HG * LC]
                        if i < G * TT:
                            d[0] += 1
                            wait_apart(dve, xbank_read, xbank_read.value(l, b, d[0]))
                            if i >= 2:
                                wait_apart(dve, centred, centred.value(l, b, i - 1))
                            for h in range(HG):
                                ins = dve.max(tp[:, h * 8:(h + 1) * 8], sr[:, h * LC:(h + 1) * LC])
                            ins.then_inc(top_ready.sem, 1)
                        if 0 <= i - 1 < G * TT:
                            wait_apart(dve, vstep, vstep.value(l, b, marked))
                            if i >= 2:
                                wait_apart(dve, picked, picked.value(l, b, i - 1))
                            for h in range(HG):
                                ins = dve.max(top2[:, h * 8:(h + 1) * 8], last[:, h * LC:(h + 1) * LC])
                            second = mine(ins)
                        if i < G * TT:
                            wait_apart(dve, top_ready, top_ready.value(l, b, i + 1))
                            if i >= 3:
                                wait_apart(dve, sel_ready, sel_ready.value(l, b, i - 2))
                            for h in range(HG):
                                ins = dve.match_replace(sp_[:, h * LC:(h + 1) * LC], tp[:, h * 8:(h + 1) * 8],
                                                        sr[:, h * LC:(h + 1) * LC], TAKEN)
                            marked = mine(ins)
                        j = i - 2
                        if 0 <= j < G * TT:
                            if i > G * TT:
                                wait_apart(dve, picked, picked.value(l, b, j + 1))
                            dve.wait_ge(exp_ready.sem, exp_ready.value(l, b, n_sub + j + 1))
                            ej = e[:, (j % 4) * HG * P:(j % 4) * HG * P + HG * LC]
                            dve.scalar_tensor_tensor(out=ej, in0=spick[:, (j % 3) * HG * LC:(j % 3 + 1) * HG * LC],
                                                     scalar=TAKEN, in1=ej, op0=ALU.is_le, op1=ALU.mult)\
                               .then_inc(sel_ready.sem, 1)
                        if 0 <= i - 1 < G * TT:
                            wait_apart(dve, vstep, vstep.value(l, b, second))
                            for h in range(HG):
                                ins = dve.match_replace(last[:, h * LC:(h + 1) * LC], top2[:, h * 8:(h + 1) * 8],
                                                        last[:, h * LC:(h + 1) * LC], TAKEN)
                            ins.then_inc(picked.sem, 1)
                        yield

                yield
                if l == 1:
                    yield from short_attention("win", 0, 0)
                    first_a = 16
                else:
                    for _ in range(4 * (G * TT + 1)):
                        yield
                    first_a = 32
                src = condT if l == 3 else scondT
                dve.tensor_copy(condB[:, :], src[:, bass.ds(b, 1)].broadcast_to([P, P]))
                src = zctxT if l == 0 else ctxT
                dve.tensor_copy(ctxb[:, :], src[:, bass.ds(b * LC, LC)]).then_inc(batch_set.sem, 1)
                bank = full()
                if l == 0:
                    dve.tensor_tensor(gate[:, 0:C], bank[:, 0:C], rowv(l, 3), ALU.add)
                    done(dve.tensor_tensor(gate[:, 2 * C:3 * C], bank[:, 2 * C:3 * C], rowv(l, 5), ALU.add))
                else:
                    done(dve.tensor_tensor(gate[:, :], bank[:, 0:3 * C], rowv(l, 3, 3), ALU.add))
                bank = full()
                if l == 3:
                    dve.tensor_copy(kcT[:, :], bank[:, 0:LC])
                else:
                    dve.tensor_scalar(kcT[:, :], bank[:, 0:LC], col(l, "kvc", 0), None, ALU.add)
                v3 = vc[:, :].rearrange("p (h n) -> p h n", n=VW)
                src = bank[0:LC, P:2 * P].rearrange("p (h n) -> p h n", n=HD)
                if l == 2:
                    mk = cmaskf[:, bass.ds(b, 1)]
                    dve.tensor_scalar(v3[:, :, HD], ones16[0:LC, :], mk, None, ALU.mult)
                    done(dve.tensor_scalar(v3[:, :, 0:HD], src, mk, None, ALU.mult))
                else:
                    dve.tensor_copy(v3[:, :, HD], ones16[0:LC, :])
                    done(dve.tensor_copy(v3[:, :, 0:HD], src))
                yield
                yield from out_proj(0, None if l == 3 else col(l, "qkv", 2))
                yield from norm_T(1)
                bank = full()
                if l == 3:
                    done(dve.tensor_copy(qT[:, :], bank[:, :]))
                else:
                    done(dve.tensor_scalar(qT[:, :], bank[:, :], col(l, "qc"), None, ALU.add))
                yield
                yield from short_attention(short_kind(l), 16 if l == 1 else 0, first_a)
                first_a += 16
                yield from out_proj(1, None if l == 3 else col(l, "kvc", 1))
                yield from norm_T(2)
                for c in range(4):
                    if l == 1:
                        bank = full()
                        dve.wait_ge(abank_read.sem, abank_read.value(l, b, first_a + c + 1))
                        gc = gact[:, c * N:(c + 1) * N]
                        done(dve.scalar_tensor_tensor(out=gc, in0=bank[:, :], scalar=col(l, "m1", 4 + c), in1=gc,
                                                      op0=ALU.add, op1=ALU.mult))
                    yield
                residual(2)
                yield
                check_count("v", l, nv[0])
                check_count("xd", l, d[0])

            run(dve, x_stream, y_head, y_stream, second_prologue)


MLP_ACT = [ACT.Gelu_apprx_tanh, ACT.Silu, ACT.Gelu, ACT.Gelu_apprx_tanh]
N_FIRST = 5
N_LOADS = 12
NPRO_D = 1
CTX_VAR = 6
CTX_NORM = 7
NPRO_V = 18
PER = {
    "yd": [69, 4, 69, 71],
    "xd": [34, 54, 34, 34],
    "a": [52, 36, 52, 52],
    "pv": [20, 8, 20, 20],
    "pr": [2, 0, 2, 4],
    "pb": [0, 0, 0, 4],
    "sub": [16, 32, 16, 16],
    "v": [26, 58, 26, 26],
    "yv": [5, 1, 5, 3],
}
ATT_PV = [16, 4, 16, 16]
FIRST_D = {"win": {1: 0}, "topk": {1: 26}, "cross": {0: 10, 2: 10, 3: 10}}


def check_count(name, layer, n):
    assert PER[name][layer] == n, (name, layer, n)


NAMES = [
    dict(mod="W_mod", qkv="W_qkv", proj="W_proj", qc="W_qc", kvc="W_kvc", cproj="W_cproj", m1="W_mlp1", m2="W_mlp2"),
    dict(mod="w_ada", qkv="w_qkv", proj="w_so", qc="w_q", kvc="w_kv", cproj="w_co", m1="w_m1", m2="w_m2"),
    dict(mod="tp_w", qkv=("sa_wq", "sa_wk", "sa_wv"), proj="sa_wo", qc="ca_wq", kvc=("ca_wk", "ca_wv"),
         cproj="ca_wo", m1="w1", m2="w2"),
    dict(mod="adaLN_W", qkv="qkv_W", proj="attn_out_W", qc="cq_W", kvc=("ck_W", "cv_W"), cproj="co_W",
         m1="mlp_W1", m2="mlp_W2"),
]
COL_NAMES = [
    dict(mod="b_mod", qkv="b_qkv", qc="b_qc", kvc="b_kvc", m1="b_mlp1"),
    dict(mod="b_ada", qkv="b_qkv", qc="b_q", kvc="b_kv", m1="b_m1"),
    dict(qkv=("sa_bq", "sa_bk", "sa_bv"), qc="ca_bq", kvc=("ca_bk", "ca_bv"), m1="b1",
         lng=("ln1_g", "ln3_g", "ln2_g"), lnb=("ln1_b", "ln3_b", "ln2_b")),
    dict(mod="adaLN_b", m1="mlp_b1", lng=("norm1_w", "normc_w", "norm2_w")),
]
ROW_NAMES = [("b_proj", "b_cproj", "b_mlp2"), ("b_so", "b_co", "b_m2"), ("sa_bo", "ca_bo", "b2"), (None, None, "mlp_b2")]
GATE_ROWS = ["b_mod", "b_ada", "tp_b", "adaLN_b"]


def lay_out(inputs):
    def get(l, names):
        names = (names,) if isinstance(names, str) else names
        return [np.asarray(inputs[f"L{l}_xcond_{n}"]) for n in names]

    zero = np.zeros(C, np.float32)
    weights, cols, rows = [], [], []
    swap = np.arange(C).reshape(H, 2, HD // 2)[:, ::-1].reshape(C)
    for l in range(LAYERS):
        for name in WIDTHS[l]:
            if name == "rot":
                qkv = get(l, "qkv_W")[0]
                weights += [qkv[:, 0:C][:, swap], qkv[:, C:2 * C][:, swap]]
            elif name == "m2":
                m2 = get(l, NAMES[l][name])[0]
                weights.append(m2.reshape(4, P, C).transpose(1, 0, 2).reshape(P, 4 * C))
            else:
                weights += get(l, NAMES[l][name])
        for name in COLS[l]:
            cols += [v.reshape(-1, P).T for v in get(l, COL_NAMES[l][name])]
        rows += [zero if n is None else get(l, n)[0] for n in ROW_NAMES[l]]
        gb = get(l, GATE_ROWS[l])[0]
        rows += [zero if c is None else gb[c * C:(c + 1) * C] for c in GATE[l]]
    half = N // 2
    inv = 1.0 / 10000.0 ** (np.arange(0, HD, 2, dtype=np.float32) / HD)
    freqs = np.outer(np.arange(half, dtype=np.float32), inv)
    emb = np.concatenate([freqs, freqs], axis=-1)
    sign = np.concatenate([-np.ones(HD // 2), np.ones(HD // 2)]).astype(np.float32)
    cos = np.tile(np.cos(emb).T, (H, 2)).astype(np.float32)
    sin = np.tile((np.sin(emb) * sign).T, (H, 2)).astype(np.float32)
    win = np.arange(P) // WIN
    smask = np.asarray(inputs["mask_SxS_bk0"])
    to_tiles = lambda m: m.reshape(TT, P, N).transpose(1, 0, 2).reshape(P, TT * N)
    x = np.asarray(inputs["x"])
    ctx = np.asarray(inputs["ctx_1024"])
    return {
        "x": x.reshape(B * TT, P, C).transpose(1, 0, 2).reshape(P, B * N),
        "w": np.concatenate(weights, 1),
        "cols": np.concatenate(cols, 1),
        "rows": np.concatenate(rows),
        "ident": np.eye(P, dtype=np.float32),
        "headmask": (np.arange(P)[:, None] // HD == np.arange(H)[None]).astype(np.float32),
        "winbias": np.where(win[:, None] == win[None], 0.0, MASKED).astype(np.float32),
        "condT": np.asarray(inputs["cond_1024"]).T,
        "ctxT": ctx.transpose(2, 0, 1).reshape(P, B * LC),
        "ctok": ctx.transpose(1, 0, 2).reshape(LC, B * C),
        "cmask_i": np.asarray(inputs["mask_BxS2_ik0"]),
        "cmask_iT": np.asarray(inputs["mask_BxS2_ik0"]).T,
        "cmask_u": np.asarray(inputs["mask_BxS2_bf1"]),
        "rope": np.stack([cos, sin], 1),
        "smask": to_tiles(smask),
        "smaskT": to_tiles(np.ascontiguousarray(smask.T)),
    }


def kernel(**inputs):
    import concourse.bacc as bacc
    from concourse.bass_utils import run_bass_kernel_spmd

    nc = bacc.Bacc("TRN2", target_bir_lowering=False, num_devices=1)
    arrays, args = {}, {}
    for name, v in lay_out(inputs).items():
        v = np.ascontiguousarray(v)
        arrays[f"in_{name}"] = v
        args[name] = nc.dram_tensor(f"in_{name}", v.shape, mybir.dt.from_np(v.dtype), kind="ExternalInput").ap()
    out = nc.dram_tensor("out_x", (P, B * N), F32, kind="ExternalOutput").ap()
    build(nc, args, out)
    r = run_bass_kernel_spmd(nc, [arrays], core_ids=[0])
    y = r.results[0]["out_x"]
    return y.reshape(P, B * TT, C).transpose(1, 0, 2).reshape(B, N, C)
```
